# Optimizing a Trainium2 kernel written in Bass

```python
import numpy as np
import jax
import jax.numpy as jnp

def _softmax(x, axis=-1):
    return jax.nn.softmax(x, axis=axis)

def _gelu(x):
    return jax.nn.gelu(x, approximate=True)

def _silu(x):
    return jax.nn.silu(x)

def _sigmoid(x):
    return jax.nn.sigmoid(x)

def _layernorm(x, axis=-1, eps=1e-05):
    m = jnp.mean(x, axis=axis, keepdims=True)
    v = jnp.var(x, axis=axis, keepdims=True)
    return (x - m) / jnp.sqrt(v + eps)

def _scatter_add(tgt, idx, src, axis=0):
    return tgt.at[idx].add(src)

def _segment_sum(src, seg, n):
    return jax.ops.segment_sum(src, seg, n)
kernel_name = 'mk_decoder_postln_d1_seqx_r8_d3d1ed'

def setup_inputs(seed: int=0):
    np.random.seed(seed)
    _w = jnp.asarray

    def _rec_inputs():
        import jax
        import jax.numpy as jnp
        _rk = jax.random.key(seed)
        x = 7.22e-05 + 1 * jax.random.normal(jax.random.fold_in(_rk, 1), (64, 64, 256), jnp.float32)
        _lenS = 64 - jax.random.randint(jax.random.fold_in(_rk, 7), (64,), 0, max(1, 64 // 4) + 1, jnp.int32)
        _lenS2 = 64 - jax.random.randint(jax.random.fold_in(_rk, 8), (64,), 0, max(1, 64 // 4) + 1, jnp.int32)
        _ctx_2048P = jax.random.normal(jax.random.fold_in(_rk, 11), (64, 16, 256), jnp.float32)
        _ctx_2048c = jax.random.dirichlet(jax.random.fold_in(_rk, 511), 0.3 * jnp.ones((16,), jnp.float32), (64, 64))
        _ctx_2048t = jnp.einsum('bsk,bkd->bsd', _ctx_2048c, _ctx_2048P)
        _ctx_2048t = _ctx_2048t * jax.lax.rsqrt(jnp.mean(jnp.square(_ctx_2048t)) + 1e-12) * 0.953939
        ctx_2048 = 4.13588e-05 + 0.999923 * (_ctx_2048t + 0.3 * jax.random.normal(jax.random.fold_in(_rk, 611), (64, 64, 256), jnp.float32))
        return (x, ctx_2048)
    x, ctx_2048 = _rec_inputs()

    def _L0_attn_setup():
        import jax, jax.numpy as jnp
        import numpy as np
        B, S, D, H = (2, 256, 256, 16)
        HD = D // H
        NEG = jnp.float32(-1000000000.0)
        key = jax.random.key(seed)
        ks = jax.random.split(key, 6)
        slopes = np.array([2 ** (-8.0 * (i + 1) / H) for i in range(H)], dtype=np.float32)
        return {'hidden_states': jax.random.normal(ks[0], (B, S, D), jnp.float32), 'qkv_w': jax.random.normal(ks[1], (3 * D, D), jnp.float32) * (1.0 / np.sqrt(D)), 'qkv_b': jax.random.normal(ks[2], (3 * D,), jnp.float32) * 0.01, 'out_w': jax.random.normal(ks[3], (D, D), jnp.float32) * (1.0 / np.sqrt(D)), 'out_b': jax.random.normal(ks[4], (D,), jnp.float32) * 0.01, 'alibi_slopes': jnp.asarray(slopes)}
    _L0_attn_all = _L0_attn_setup()
    _L0_attn_in = {k: v for k, v in _L0_attn_all.items() if k in ('qkv_w', 'qkv_b', 'out_w', 'out_b', 'alibi_slopes')}
    del _L0_attn_all

    def _L0_xattn_setup():
        import jax, jax.numpy as jnp
        import numpy as np
        B, S, DIM, HD = (4, 128, 256, 128)
        H = DIM // HD
        GN_EPS = 0.001

        def _decay_masks(n_heads, seq_len):
            gam = 1.0 - 2.0 ** (-5.0 - jnp.arange(n_heads, dtype=jnp.float32))
            idx = jnp.arange(seq_len, dtype=jnp.float32)
            expo = idx[None, :] - idx[:, None]
            D = jnp.where(expo[None, :, :] <= 0, gam[:, None, None] ** expo[None, :, :], 0.0)
            return D / jnp.sqrt(D.sum(axis=-1))[:, None, :]
        key = jax.random.key(seed)
        ks = jax.random.split(key, 8)
        x = jax.random.normal(ks[0], (B, S, DIM), dtype=jnp.float32)
        k = jax.random.normal(ks[1], (B, S, DIM), dtype=jnp.float32)
        v = jax.random.normal(ks[2], (B, S, DIM), dtype=jnp.float32)
        Wh = jax.random.normal(ks[3], (H, HD, HD), dtype=jnp.float32) / np.sqrt(HD)
        wg_w = jax.random.normal(ks[4], (DIM, DIM), dtype=jnp.float32) / np.sqrt(DIM)
        wo_w = jax.random.normal(ks[5], (DIM, DIM), dtype=jnp.float32) / np.sqrt(DIM)
        gn_gamma = jnp.ones((DIM,), dtype=jnp.float32)
        gn_beta = jnp.zeros((DIM,), dtype=jnp.float32)
        return {'x': x, 'k': k, 'v': v, 'Wh': Wh, 'wg_w': wg_w, 'wo_w': wo_w, 'gn_gamma': gn_gamma, 'gn_beta': gn_beta}
    _L0_xattn_all = _L0_xattn_setup()
    _L0_xattn_in = {k: v for k, v in _L0_xattn_all.items() if k in ('Wh', 'wg_w', 'wo_w', 'gn_gamma', 'gn_beta')}
    del _L0_xattn_all

    def _L0_ffn_setup():
        import jax, jax.numpy as jnp
        import numpy as np
        B, S, H = (2, 64, 256)
        E, I, K = (64, 176, 6)
        NS = 2
        SH_I = I * NS
        key = jax.random.key(seed)
        ks = jax.random.split(key, 6)
        s = 0.02
        return {'hidden_states': jax.random.normal(ks[0], (B, S, H), jnp.float32), 'gate_w': jax.random.normal(ks[1], (E, H), jnp.float32) * s, 'experts_w1': jax.random.normal(ks[2], (E, I, H), jnp.float32) * s, 'experts_w2': jax.random.normal(ks[3], (E, H, I), jnp.float32) * s, 'shared_gate_up': jax.random.normal(ks[4], (2 * SH_I, H), jnp.float32) * s, 'shared_down': jax.random.normal(ks[5], (H, SH_I), jnp.float32) * s}
    _L0_ffn_all = _L0_ffn_setup()
    _L0_ffn_in = {k: v for k, v in _L0_ffn_all.items() if k in ('gate_w', 'experts_w1', 'experts_w2', 'shared_gate_up', 'shared_down')}
    del _L0_ffn_all
    return {'x': x, 'ctx_2048': ctx_2048, 'L0_attn_qkv_w': _L0_attn_in['qkv_w'], 'L0_attn_qkv_b': _L0_attn_in['qkv_b'], 'L0_attn_out_w': _L0_attn_in['out_w'], 'L0_attn_out_b': _L0_attn_in['out_b'], 'L0_attn_alibi_slopes': _L0_attn_in['alibi_slopes'], 'L0_xattn_Wh': _L0_xattn_in['Wh'], 'L0_xattn_wg_w': _L0_xattn_in['wg_w'], 'L0_xattn_wo_w': _L0_xattn_in['wo_w'], 'L0_xattn_gn_gamma': _L0_xattn_in['gn_gamma'], 'L0_xattn_gn_beta': _L0_xattn_in['gn_beta'], 'L0_ffn_gate_w': _L0_ffn_in['gate_w'], 'L0_ffn_experts_w1': _L0_ffn_in['experts_w1'], 'L0_ffn_experts_w2': _L0_ffn_in['experts_w2'], 'L0_ffn_shared_gate_up': _L0_ffn_in['shared_gate_up'], 'L0_ffn_shared_down': _L0_ffn_in['shared_down']}

def reference(x, ctx_2048, L0_attn_qkv_w, L0_attn_qkv_b, L0_attn_out_w, L0_attn_out_b, L0_attn_alibi_slopes, L0_xattn_Wh, L0_xattn_wg_w, L0_xattn_wo_w, L0_xattn_gn_gamma, L0_xattn_gn_beta, L0_ffn_gate_w, L0_ffn_experts_w1, L0_ffn_experts_w2, L0_ffn_shared_gate_up, L0_ffn_shared_down):
    import jax
    import jax.numpy as jnp

    def _L0_attn_ref(hidden_states, qkv_w, qkv_b, out_w, out_b, alibi_slopes):
        import jax, jax.numpy as jnp
        import numpy as np
        B, S, D, H = (2, 256, 256, 16)
        HD = D // H
        NEG = jnp.float32(-1000000000.0)
        b, s, d = hidden_states.shape
        qkv = hidden_states @ qkv_w.T + qkv_b
        q, k, v = jnp.split(qkv, 3, axis=-1)
        q = q.reshape(b, s, H, HD)
        k = k.reshape(b, s, H, HD)
        v = v.reshape(b, s, H, HD)
        scale = 1.0 / np.sqrt(HD)
        scores = jnp.einsum('bqhd,bkhd->bhqk', q, k) * scale
        pos = jnp.arange(s)
        rel = (pos[None, :] - pos[:, None]).astype(jnp.float32)
        bias = alibi_slopes[:, None, None] * rel
        causal = pos[None, :] <= pos[:, None]
        scores = jnp.where(causal[None, None], scores + bias[None], NEG)
        attn = jax.nn.softmax(scores, axis=-1)
        out = jnp.einsum('bhqk,bkhd->bqhd', attn, v).reshape(b, s, d)
        out = out @ out_w.T + out_b
        return out

    def _L0_xattn_ref(x, k, v, Wh, wg_w, wo_w, gn_gamma, gn_beta):
        import jax, jax.numpy as jnp
        import numpy as np
        B, S, DIM, HD = (4, 128, 256, 128)
        H = DIM // HD
        GN_EPS = 0.001

        def _decay_masks(n_heads, seq_len):
            gam = 1.0 - 2.0 ** (-5.0 - jnp.arange(n_heads, dtype=jnp.float32))
            idx = jnp.arange(seq_len, dtype=jnp.float32)
            expo = idx[None, :] - idx[:, None]
            D = jnp.where(expo[None, :, :] <= 0, gam[:, None, None] ** expo[None, :, :], 0.0)
            return D / jnp.sqrt(D.sum(axis=-1))[:, None, :]
        b, s, dim = x.shape
        h, hd, _ = Wh.shape
        xh = x.reshape(b, s, h, hd)
        kh = k.reshape(b, s, h, hd)
        vh = v.reshape(b, s, h, hd)
        Q = jnp.einsum('bshd,hde->bshe', xh, Wh)
        K = jnp.einsum('bshd,hde->bshe', kh, Wh)
        V = jnp.einsum('bshd,hde->bshe', vh, Wh)
        scores = jnp.einsum('bshe,bthe->bhst', Q, K) / jnp.sqrt(jnp.float32(hd))
        Dn = _decay_masks(h, s)
        masked = scores * Dn[None, :, :, :]
        A = jnp.maximum(jnp.abs(masked.sum(axis=0)), 1.0)
        O = jnp.einsum('hst,bthe->bshe', A, V).reshape(b, s, dim)
        mu = O.mean(axis=-1, keepdims=True)
        var = O.var(axis=-1, keepdims=True)
        Y = (O - mu) / jnp.sqrt(var + GN_EPS) * gn_gamma + gn_beta
        W = jax.nn.relu(x @ wg_w)
        return W * Y @ wo_w

    def _L0_ffn_ref(hidden_states, gate_w, experts_w1, experts_w2, shared_gate_up, shared_down):
        import jax, jax.numpy as jnp
        import numpy as np
        B, S, H = (2, 64, 256)
        E, I, K = (64, 176, 6)
        NS = 2
        SH_I = I * NS
        orig_shape = hidden_states.shape
        x = hidden_states.reshape(-1, orig_shape[-1])
        router_logits = x @ gate_w.T
        probs = jax.nn.softmax(router_logits, axis=-1)
        topk_w, topk_idx = jax.lax.top_k(probs, K)
        topk_w = topk_w / jnp.sum(topk_w, axis=-1, keepdims=True)
        combine = jnp.sum(jax.nn.one_hot(topk_idx, E, dtype=x.dtype) * topk_w[..., None], axis=1)
        h = jax.nn.silu(jnp.einsum('th,eih->tei', x, experts_w1))
        y = jnp.einsum('tei,ehi->teh', h, experts_w2)
        routed_out = jnp.einsum('teh,te->th', y, combine)
        gu = x @ shared_gate_up.T
        g, u = jnp.split(gu, 2, axis=-1)
        shared_out = jax.nn.silu(g) * u @ shared_down.T
        return (routed_out + shared_out).reshape(orig_shape)
    x = _layernorm(x + _L0_attn_ref(x, L0_attn_qkv_w, L0_attn_qkv_b, L0_attn_out_w, L0_attn_out_b, L0_attn_alibi_slopes), axis=-1)
    x = _layernorm(x + _L0_xattn_ref(x, ctx_2048, ctx_2048, L0_xattn_Wh, L0_xattn_wg_w, L0_xattn_wo_w, L0_xattn_gn_gamma, L0_xattn_gn_beta), axis=-1)
    x = _layernorm(x + _L0_ffn_ref(x, L0_ffn_gate_w, L0_ffn_experts_w1, L0_ffn_experts_w2, L0_ffn_shared_gate_up, L0_ffn_shared_down), axis=-1)
    return x

_drawn_inputs = setup_inputs


def setup_inputs(seed=0):
    import zlib

    import numpy as np

    out = dict(_drawn_inputs(seed))
    spreads = {'L0_xattn_gn_gamma': (1.0, 0.2), 'L0_xattn_gn_beta': (0.0, 0.1)}
    factors = {'L0_attn_qkv_b': 4.73,
     'L0_attn_out_b': 6.032,
     'L0_ffn_gate_w': 3.251,
     'L0_ffn_experts_w1': 3.101,
     'L0_ffn_experts_w2': 3.077,
     'L0_ffn_shared_gate_up': 2.843,
     'L0_ffn_shared_down': 2.843}
    for name, (base, spread) in spreads.items():
        noise = np.random.default_rng([zlib.crc32(name.encode()), seed]).standard_normal(out[name].shape)
        drawn = base * np.exp(spread * noise) if base else spread * noise
        out[name] = jnp.asarray(drawn.astype(out[name].dtype))
    for name, factor in factors.items():
        out[name] = (out[name] * factor).astype(out[name].dtype)
    return out
```

```python
from contextlib import ExitStack

import numpy as np

import concourse.bass as bass
from concourse import mybir

F32 = mybir.dt.float32
BF16 = mybir.dt.bfloat16
I32 = mybir.dt.int32
U32 = mybir.dt.uint32
ACT = mybir.ActivationFunctionType
ALU = mybir.AluOpType
AX = mybir.AxisListType.X

P = 128
B, S, D = 64, 64, 256
T = B * S
NT = T // P
H, HD = 16, 16
RH = 2
E, I, K = 64, 176, 6
IC = I // 2
SH = 2 * I
SC = SH // IC
UNIT = 256
G = 2
RC = T // G + UNIT
ROW = D + 2 * K
NOWHERE = 1 << 20
ORDER = [8 * m + 2 * (2 * g2 + g1) + par for g1 in range(2) for g2 in range(2) for m in range(2) for par in range(2)]
LN_EPS, GN_EPS = 1e-5, 1e-3

PER_TILE = {"pt_ready": 2, "pt_evac": 2}
CREDIT = 6


def decoder_layer(nc, a, out):
    x1d = nc.dram_tensor("x1_rows", (T, D), F32, kind="Internal").ap()
    x1td = nc.dram_tensor("x1_transposed", (NT, P, D), F32, kind="Internal").ap()
    x2d = nc.dram_tensor("x2_rows", (T, D), F32, kind="Internal").ap()
    shd = nc.dram_tensor("x2_plus_shared", (T, D), F32, kind="Internal").ap()
    listd = [nc.dram_tensor(f"expert_lists{g}", (E * RC, ROW), F32, kind="Internal").ap() for g in range(G)]
    yd = nc.dram_tensor("expert_results", (T * K, D), F32, kind="Internal").ap()

    with ExitStack() as ctx:
        def sb(name, shape, dt=F32):
            return ctx.enter_context(nc.sbuf_tensor(name, shape, dt))

        sems = {}

        def sem(name):
            if name not in sems:
                sems[name] = ctx.enter_context(nc.semaphore(name))
            return sems[name]

        def ev(name, t):
            n = PER_TILE.get(name, 1)
            return sem(name), (t + 1 + CREDIT) * n

        def clipped(name, t):
            return ev(name, min(t, NT - 1) if isinstance(t, int) else t)

        def half(name, t, h):
            return sem(name), (t + CREDIT) * 2 + h + 1

        def credit(eng, *names):
            for name in names:
                eng.sem_inc(sem(name), CREDIT * PER_TILE.get(name, 1))

        def tiles(eng, lags, end=NT):
            deep = max(l for l, _ in lags)
            deep += deep % 2
            for s in range(deep):
                for l, f in lags:
                    if s - l >= 0:
                        f((s - l) // 2, (s - l) % 2)
            with eng.Fori(0, (end - deep) // 2) as i:
                for r in range(2):
                    for l, f in lags:
                        f(i + (deep + r - l) // 2, (r - l) % 2)
            for s in range(end, end + deep):
                for l, f in lags:
                    if 0 <= s - l < end:
                        f((s - l) // 2, (s - l) % 2)

        consts = {}

        def const(name, src, shape, dt=F32):
            consts[name] = (sb("c_" + name, shape, dt), src)
            return consts[name][0]

        kc = "(c p) n -> p c n"
        ident = const("ident", a["ident"], [P, P])
        wqkv = const("wqkv", a["wqkv_t"].rearrange(kc, p=P), [P, 2, 3 * D])
        bqk = const("bqk", a["b_qk"], [P, 4])
        bv = const("bv", a["b_v"], [P, 2])
        kpar = const("kpar", a["k_parity"], [P, 2])
        vpar = const("vpar", a["v_parity"], [P, D])
        rel = const("rel", a["rel"], [P, S])
        causal = const("causal", a["causal"], [P, S])
        slopes = const("slopes", a["slopes"], [P, H])
        wout = const("wout", a["wout_t"].rearrange(kc, p=P), [P, 2, D])
        bout = const("bout", a["b_out"], [P, D])
        wht = const("wht", a["wh_t"].rearrange("h e d -> e h d"), [P, RH, P])
        wh = const("wh", a["wh"].rearrange("h d e -> d h e"), [P, RH, P])
        decay = const("decay", a["decay_t"], [P, RH, S])
        wg = const("wg", a["wg"].rearrange(kc, p=P), [P, 2, D])
        wo = const("wo", a["wo"].rearrange(kc, p=P), [P, 2, D])
        gamma = const("gamma", a["gamma"], [P, 2])
        beta = const("beta", a["beta"], [P, 2])
        wgate = const("wgate", a["gate_t"].rearrange(kc, p=P), [P, 2, E])
        tri_f = const("tri_f", a["tri"], [P, P])
        iota_e = const("iota_e", a["iota_e"], [P, E])
        places = const("places", a["places"], [P, NT, K])
        sgu = const("sgu", a["sgu_t"].rearrange(kc, p=P), [P, 2, 2 * SH])
        sdn = const("sdn", a["sdn_t"].rearrange("(c p) n -> p c n", p=IC), [IC, SC, D])
        tri = sb("tri", [P, P], BF16)
        ones = sb("ones", [P, P], BF16)
        bqs = sb("bqs", [P, 2])
        bias = sb("bias", [P, H, S])
        m2 = sb("m2", [P, RH, P])
        eps = sb("eps", [P, 2])
        mhalf = sb("mhalf", [P, 1])
        zeros = sb("zeros", [P, UNIT // P, ROW])
        junk = sb("junk", [1, 16])

        xt = [sb(f"xt{u}", [P, 2, 2, 2, S]) for u in range(2)]
        xn = [sb(f"xn{u}", [P, D]) for u in range(2)]
        xnb = [sb(f"xnb{u}", [P, D]) for u in range(2)]
        qt = [sb(f"qt{u}", [P, 2, P]) for u in range(2)]
        kt = [sb(f"kt{u}", [P, 2, 2, P]) for u in range(2)]
        vbd = [sb(f"vbd{u}", [P, 2, D]) for u in range(2)]
        prob = [sb(f"prob{u}", [P, H, S]) for u in range(2)]
        mx = [sb(f"mx{u}", [P, H]) for u in range(2)]
        rsum = [sb(f"rsum{u}", [P, H]) for u in range(2)]
        rinv = [sb(f"rinv{u}", [P, H]) for u in range(2)]
        pt = [sb(f"pt{u}", [P, H // 2, P]) for u in range(2)]
        on = [sb(f"on{u}", [P, D]) for u in range(2)]
        ot = [sb(f"ot{u}", [P, 2, P]) for u in range(2)]
        ln = {}
        for name in ("ln1", "gn", "ln2", "ln3"):
            for u in range(2):
                ln[name, u] = (sb(f"{name}_r{u}", [P, D]), sb(f"{name}_st{u}", [P, 6]), sb(f"{name}_mv{u}", [P, 2]),
                               sb(f"{name}_ve{u}", [P, 1]), sb(f"{name}_rs{u}", [P, 1]), sb(f"{name}_y{u}", [P, D]))
        xb = [sb(f"xb{u}", [P, D]) for u in range(2)]
        xbt = [sb(f"xbt{u}", [P, 2, P]) for u in range(2)]
        cbt = [sb(f"cbt{u}", [P, 2, 2, 2, S]) for u in range(2)]
        mxt = [sb(f"mxt{u}", [P, RH, P]) for u in range(2)]
        araw = sb("araw", [P, RH, S])
        afloor = sb("afloor", [P, RH, S])
        abd = sb("abd", [P, RH, P])
        cn = [sb(f"cn{u}", [P, D]) for u in range(2)]
        xct = [sb(f"xct{u}", [P, 2, P]) for u in range(2)]
        xc = [sb(f"xc{u}", [P, D]) for u in range(2)]
        zt = [sb(f"zt{u}", [P, RH, P]) for u in range(2)]
        wt = [sb(f"wt{u}", [P, 2, P]) for u in range(2)]
        yt = [sb(f"yt{u}", [P, 2, P]) for u in range(2)]
        gt = [sb(f"gt{u}", [P, 2, P]) for u in range(2)]
        x2t = [sb(f"x2t{u}", [P, 2, P]) for u in range(2)]
        lg = [sb(f"lg{u}", [P, E]) for u in range(2)]
        top = [sb(f"top{u}", [P, 8]) for u in range(2)]
        topi = [sb(f"topi{u}", [P, 8], U32) for u in range(2)]
        tope = [sb(f"tope{u}", [P, K]) for u in range(2)]
        ntop = [sb(f"ntop{u}", [P, 1]) for u in range(2)]
        wexp = [sb(f"wexp{u}", [P, K]) for u in range(2)]
        wsum = [sb(f"wsum{u}", [P, 1]) for u in range(2)]
        winv = [sb(f"winv{u}", [P, 1]) for u in range(2)]
        weights = sb("weights", [P, NT, K])
        hot = [sb(f"hot{u}", [P, K, E], BF16) for u in range(2)]
        rank = [sb(f"rank{u}", [P, E]) for u in range(2)]
        pick = sb("pick", [P, K, E])
        destf = [sb(f"destf{u}", [P, K]) for u in range(2)]
        dest = [sb(f"dest{u}", [P, K], I32) for u in range(2)]
        nextrow = [sb(f"nextrow{g}", [P, E]) for g in range(G)]
        row = [sb(f"row{u}", [P, ROW]) for u in range(2)]
        th = [sb(f"th{u}", [IC, SC, P]) for u in range(2)]
        sg = [sb(f"sg{u}", [IC, SC, P]) for u in range(2)]
        sh = [sb(f"sh{u}", [IC, SC, P]) for u in range(2)]
        xs = [sb(f"xs{u}", [P, D]) for u in range(2)]
        xsh = [sb(f"xsh{u}", [P, D]) for u in range(2)]
        cntf = sb("cntf", [1, 4, E * G])
        cnti = sb("cnti", [1, 2, E * G], I32)
        n_rows = sb("n_rows", [1, E * G], I32)
        n_units = sb("n_units", [1, E * G], I32)
        unit0 = sb("unit0", [1, E * G + 1], I32)
        w1 = [sb(f"w1_{u}", [P, 2, I]) for u in range(2)]
        w2 = [sb(f"w2_{u}", [IC, 2, D]) for u in range(2)]
        ur = sb("ur", [P, 2, ROW])
        meta = sb("meta", [P, 2, 2 * K])
        uxt = sb("uxt", [P, 2, UNIT])
        uh = sb("uh", [IC, 2, UNIT])
        uy = sb("uy", [P, 2, D])
        uplace = sb("uplace", [P, 2, K])
        uplace_s = sb("uplace_s", [P, 2])
        udest = sb("udest", [P, 2], I32)
        y6 = [sb(f"y6_{u}", [P, K, D]) for u in range(2)]
        xe = [sb(f"xe{u}", [P, D]) for u in range(2)]

        psum = ctx.enter_context(nc.psum_tensor("psum", [P, 8, 512], F32))

        def bank(i, n=2):
            return psum[:, i, 0:n * P].rearrange("p (c n) -> p c n", c=n)

        ps_q, ps_k, ps_v = bank(0), bank(1), psum[:, 2, :].rearrange("p (b n) -> p b n", b=2)
        ps_s = psum[:, 3:5, :].rearrange("p a n -> p (a n)")
        ps_pt = psum[:, 5:7, :].rearrange("p a (c n) -> p (a c) n", c=4)
        ps_o = ps_r = psum[:, 7, 0:D]
        ps_ot = bank(7)
        ps_bt, ps_bm, ps_a = bank(0), bank(1), psum[:, 3:5, 0:S]
        ps_z, ps_w = bank(0), psum[:, 0, D:2 * D].rearrange("p (c n) -> p c n", c=2)
        ps_co, ps_ct, ps_x2t = psum[:, 1, 0:D], bank(2), bank(2)
        ps_cr = ps_sd = psum[:, 3, 0:D]
        ps_lg = psum[:, 4, 0:E]
        ps_g, ps_u = psum[0:IC, 5, :].rearrange("p (c n) -> p c n", c=SC), psum[0:IC, 6, :].rearrange("p (c n) -> p c n", c=SC)
        ps_before, ps_total = psum[:, 7, 0:E], psum[:, 7, E:2 * E]
        ps_ux = [psum[:, c, 0:UNIT] for c in range(2)]
        ps_uh = psum[0:IC, 2, :].rearrange("p (c n) -> p c n", c=2)
        ps_uy = [psum[:, 5 + h, 0:D] for h in range(2)]

        block = ctx.enter_context(nc.Block())

        def rows(k, u):
            return bass.ds((2 * k + u) * P, P)

        def load(eng, dst, src, name):
            eng.dma_start(dst, src).then_inc(sem(name), 16)

        def ld(name, k, u, n=1):
            return sem(f"{name}{u}"), 16 * n * (k + 1)

        def stored(name, k, u):
            return sem(f"{name}{u}"), 16 * (k + 1)

        def prime(eng, *names):
            for name in names:
                n = primed[0]
                primed[0] += 1
                eng.dma_start(junk[0:1, n:n + 1], a["ident"][0:1, n:n + 1]).then_inc(sem(name), 16)

        def list_units(eng, v):
            return (eng.value_load(n_units[0:1, bass.ds(v, 1)], min_val=1, max_val=T // G // UNIT),
                    eng.value_load(unit0[0:1, bass.ds(v, 1)], min_val=0, max_val=E * G * (T // G // UNIT)))

        primed = [0]
        n_const = 16 * len(consts)

        def settle(eng):
            eng.sem_inc(sem("waits_passed"), 1)

        @block.sync
        def _(sp):
            for t_, src in consts.values():
                sp.dma_start(t_[:], src).then_inc(sem("consts"), 16)
            prime(sp, "x1_st0", "x1_st1", "x1t_st0", "x1t_st1", "x2_st0", "x2_st1", "xsh_st0", "xsh_st1",
                  "out_st0", "out_st1")

            def load_twice(dst, src, t, name):
                for copy in range(2):
                    for c in range(2):
                        sp.dma_start(dst[:, c, :, copy, :], src[c * P:(c + 1) * P, bass.ds(t * P, P)]
                                     .rearrange("p (b s) -> p b s", b=2)).then_inc(sem(name), 16)

            def load_a(k, u):
                t = 2 * k + u
                sp.wait_ge(*ev("v_ready", t - 2))
                load_twice(xt[u], a["x_t"], t, f"xt_ld{u}")
                sp.wait_ge(*ev("xnb_done", t - 2))
                load(sp, xn[u][:], a["x"][rows(k, u), :], f"xn_ld{u}")

            def store_a(k, u):
                sp.wait_ge(*ev("ln1_done", 2 * k + u))
                sp.dma_start(x1d[rows(k, u), :], ln["ln1", u][5][:]).then_inc(sem(f"x1_st{u}"), 16)

            tiles(sp, [(0, load_a), (3, store_a)])

            for u in range(2):
                sp.wait_ge(sem(f"x1_st{u}"), 16 * (NT // 2 + 1))

            def load_b(k, u):
                t = 2 * k + u
                sp.wait_ge(*ev("xbt_ready", t - 2))
                load(sp, xb[u][:], x1d[rows(k, u), :], f"xb_ld{u}")
                sp.wait_ge(*ev("a_added", t - 2))
                settle(sp)
                load_twice(cbt[u], a["ctx_t"], t, f"cbt_ld{u}")

            def store_b(k, u):
                sp.wait_ge(*ev("xbt_evac", 2 * k + u))
                sp.dma_start(x1td[bass.ds(2 * k + u, 1)].rearrange("a p n -> p (a n)"),
                             xbt[u][:].rearrange("p c n -> p (c n)")).then_inc(sem(f"x1t_st{u}"), 16)

            tiles(sp, [(0, load_b), (2, store_b)])

            for u in range(2):
                sp.wait_ge(sem(f"x1t_st{u}"), 16 * (NT // 2 + 1))

            def load_c(k, u):
                t = 2 * k + u
                sp.wait_ge(*ev("zw_ready", t - 2))
                load(sp, cn[u][:], a["ctx"][rows(k, u), :], f"cn_ld{u}")
                sp.wait_ge(*ev("zw_ready", t - 2))
                load(sp, xct[u][:].rearrange("p c n -> p (c n)"),
                     x1td[bass.ds(t, 1)].rearrange("a p n -> p (a n)"), f"xct_ld{u}")

            def load_residual(k, u):
                sp.wait_ge(*ev("ln2_sum", 2 * k + u - 2))
                load(sp, xc[u][:], x1d[rows(k, u), :], f"xc_ld{u}")

            def store_x2(k, u):
                sp.wait_ge(*ev("ln2_done", 2 * k + u))
                sp.dma_start(x2d[rows(k, u), :], ln["ln2", u][5][:]).then_inc(sem(f"x2_st{u}"), 16)

            def load_row(k, u):
                t = 2 * k + u
                sp.wait_ge(sem(f"x2_st{u}"), 16 * (k + 2))
                settle(sp)
                sp.wait_ge(*ev("scattered", t - 2))
                settle(sp)
                load(sp, row[u][:, 0:D], x2d[rows(k, u), :], f"row_ld{u}")
                sp.wait_ge(*ev("xsh_done", t - 2))
                load(sp, xs[u][:], x2d[rows(k, u), :], f"xs_ld{u}")

            def store_shared(k, u):
                sp.wait_ge(*ev("xsh_done", 2 * k + u))
                sp.dma_start(shd[rows(k, u), :], xsh[u][:]).then_inc(sem(f"xsh_st{u}"), 16)

            tiles(sp, [(0, load_c), (2, load_residual), (5, store_x2), (6, load_row), (8, store_shared)])

            sp.wait_ge(sem("tables"), 1)
            sp.wait_ge(*ev("scattered", NT - 1))

            def pad(e, u):
                for g in range(G):
                    n = sp.value_load(n_rows[0:1, bass.ds(e * G + g, 1)], min_val=0, max_val=T // G)
                    sp.dma_start(listd[g][bass.ds(n + e * RC, UNIT), :].rearrange("(h p) n -> p h n", p=P),
                                 zeros[:]).then_inc(sem(f"pad_st{u}"), 16)

            pad(0, 0)
            pad(1, 1)

            def load_units(i, u, more):
                e = 2 * i + u
                sp.wait_ge(sem(f"pad_st{u}"), 16 * G * (i + 1))
                for g in range(G):
                    n, first = list_units(sp, e * G + g)
                    with sp.Fori(0, n) as j:
                        sp.wait_ge(*ev("ux_ready", first + j - 1))
                        sp.wait_ge(*ev("meta_done", first + j - 1))
                        sp.dma_start(ur[:], listd[g][bass.ds(e * RC + j * UNIT, UNIT), :]
                                     .rearrange("(h p) n -> p h n", p=P)).then_inc(sem("ur_ld"), 16)
                if more:
                    pad(e + 2, u)

            with sp.Fori(0, E // 2 - 1) as i:
                for u in range(2):
                    load_units(i, u, True)
            for u in range(2):
                load_units(E // 2 - 1, u, False)
            last = sp.value_load(unit0[0:1, E * G:E * G + 1], min_val=1, max_val=T)
            sp.wait_ge(*ev("ux_ready", last - 1))
            sp.wait_ge(*ev("meta_done", last - 1))
            sp.dma_start(ur[:], listd[0][0:UNIT, :].rearrange("(h p) n -> p h n", p=P)).then_inc(sem("ur_ld"), 16)

            for u in range(2):
                sp.wait_ge(sem(f"xsh_st{u}"), 16 * (NT // 2 + 1))
            for h in range(2):
                sp.wait_ge(sem(f"y_out{h}"), 16 * (last + 1))

            def load_e(k, u):
                t = 2 * k + u
                sp.wait_ge(*ev("ln3_sum", t - 2))
                load(sp, xe[u][:], shd[rows(k, u), :], f"xe_ld{u}")
                load(sp, y6[u][:].rearrange("p k n -> p (k n)"),
                     yd.rearrange("(t k) n -> t (k n)", k=K)[rows(k, u), :], f"y6_ld{u}")

            def store_e(k, u):
                sp.wait_ge(*ev("ln3_done", 2 * k + u))
                sp.dma_start(out[rows(k, u), :], ln["ln3", u][5][:]).then_inc(sem(f"out_st{u}"), 16)

            tiles(sp, [(0, load_e), (2, store_e)])
            for u in range(2):
                sp.wait_ge(sem(f"out_st{u}"), 16 * (NT // 2 + 1))

        @block.tensor
        def _(pe):
            pe.wait_ge(sem("consts"), n_const)
            credit(pe, "s_half", "qk_ready", "v_ready", "s_ready", "pt_ready", "o_ready", "ot_ready", "r_ready",
                   "xbt_ready", "mxt_ready", "a_added", "zw_ready", "co_ready", "ct_ready",
                   "cr_ready", "x2t_ready", "lg_ready", "gu_ready", "rank_ready", "sd_ready",
                   "ux_ready", "uh_ready", "uy_ready")
            for h in range(RH):
                m = pe.matmul(ps_ot[:, h, :], wht[:, h, :], wht[:, h, :], start=True, stop=True)
            m.then_inc(sem("m2_ready"), 1)
            pe.wait_ge(sem("m2_done"), 1)

            def project(k, u):
                t = 2 * k + u
                pe.wait_ge(*ld("xt_ld", k, u, 4))
                pe.wait_ge(*ev("q_evac", t - 1))
                pe.wait_ge(*ev("k_evac", t - 1))
                for m in range(4):
                    for c in range(2):
                        q = pe.matmul((ps_q if m < 2 else ps_k)[:, m % 2, :], wqkv[:, c, m * P:(m + 1) * P], xt[u][:, c, :, 0, :],
                                      start=c == 0, stop=c == 1)
                q.then_inc(sem("qk_ready"), 1)
                pe.wait_ge(*ev("v_evac", t - 1))
                for b in range(2):
                    for c in range(2):
                        x_b = xt[u][:, c, b, :, :].rearrange("p a s -> p (a s)")
                        q = pe.matmul(ps_v[:, b, :], x_b, wqkv[:, c, 2 * D:3 * D], start=c == 0, stop=c == 1)
                q.then_inc(sem("v_ready"), 1)

            def out_transpose(k, u):
                t = 2 * k + u
                pe.wait_ge(*ev("o_norm", t))
                for c in range(2):
                    q = pe.transpose(ps_ot[:, c, :], on[u][:, c * P:(c + 1) * P], ident[:])
                q.then_inc(sem("ot_ready"), 1)

            def prob_transpose(k, u):
                t = 2 * k + u
                pe.wait_ge(*ev("exp_done", t))
                for h in range(2):
                    pe.wait_ge(*half("pt_evac", t - 1, h))
                    for g in range(4):
                        g2 = 4 * h + g
                        q = pe.transpose(ps_pt[:, g2, :], prob[u][:, 2 * g2:2 * g2 + 2, :]
                                         .rearrange("p a s -> p (a s)"), ident[:])
                    q.then_inc(sem("pt_ready"), 1)

            def out_project(k, u):
                t = 2 * k + u
                pe.wait_ge(*ev("ot_evac", t))
                for c in range(2):
                    q = pe.matmul(ps_r, ot[u][:, c, :], wout[:, c, :], start=c == 0, stop=c == 1)
                q.then_inc(sem("r_ready"), 1)

            def scores(k, u):
                t = 2 * k + u
                pe.wait_ge(*ev("q_evac", t))
                pe.wait_ge(*ev("k_evac", t))
                pe.wait_ge(*ev("s_read", t - 1))
                for g2 in range(2):
                    if g2:
                        pe.wait_ge(*ev("s_half", t))
                    for m in range(2):
                        for b in range(2):
                            for g1 in range(2):
                                g, col = 2 * g2 + g1, 512 * g1 + 256 * g2 + 128 * m
                                q = pe.matmul(ps_s[b * S:(b + 1) * S, col:col + 2 * S],
                                              qt[u][32 * g:32 * g + 32, m, b * S:(b + 1) * S],
                                              kt[u][32 * g:32 * g + 32, m, :, b * S:(b + 1) * S],
                                              start=True, stop=True)
                    q.then_inc(sem("s_ready" if g2 else "s_half"), 1)

            def attend(k, u):
                t = 2 * k + u
                pe.wait_ge(*ev("pt_evac", t))
                pe.wait_ge(*ev("v_evac", t))
                pe.wait_ge(*ev("ln1_sum", t - 1))
                for g in range(8):
                    for b in range(2):
                        q = pe.matmul(ps_o[b * S:(b + 1) * S, 32 * g:32 * g + 32],
                                      pt[u][:, g, b * S:(b + 1) * S], vbd[u][:, b, 32 * g:32 * g + 32],
                                      start=True, stop=True)
                q.then_inc(sem("o_ready"), 1)

            tiles(pe, [(0, project), (2, out_transpose), (1, prob_transpose), (2, out_project),
                       (0, scores), (1, attend)])

            pe.wait_ge(*ev("ln1_sum", NT - 1))

            def b_transpose(k, u):
                t = 2 * k + u
                pe.wait_ge(*ld("xb_ld", k, u))
                pe.wait_ge(*ev("xbt_evac", t - 1))
                for c in range(2):
                    q = pe.transpose(ps_bt[:, c, :], xb[u][:, c * P:(c + 1) * P], ident[:])
                q.then_inc(sem("xbt_ready"), 1)

            def b_mix(k, u):
                t = 2 * k + u
                pe.wait_ge(*ev("xbt_evac", t))
                pe.wait_ge(*ev("mxt_evac", t - 1))
                for h in range(RH):
                    q = pe.matmul(ps_bm[:, h, :], m2[:, h, :], xbt[u][:, h, :], start=True, stop=True)
                q.then_inc(sem("mxt_ready"), 1)

            def b_scores(k, u):
                t = 2 * k + u
                pe.wait_ge(*ev("mxt_evac", t))
                pe.wait_ge(*ld("cbt_ld", k, u, 4))
                for h in range(RH):
                    for b in range(2):
                        c_b = cbt[u][:, h, b, :, :].rearrange("p a s -> p (a s)")
                        q = pe.matmul(ps_a[:, h, :], c_b, mxt[u][:, h, b * S:(b + 1) * S],
                                      start=False, stop=False)
                q.then_inc(sem("a_added"), 1)

            def b_add_zero(start):
                for h in range(RH):
                    q = pe.matmul(ps_a[:, h, :], zeros[:, 0, 0:P], zeros[:, 0, 0:S], start=start, stop=not start)
                return q

            pe.wait_ge(sem("zeroed"), 4)
            b_add_zero(True)
            tiles(pe, [(0, b_transpose), (1, b_mix), (2, b_scores)])
            b_add_zero(False).then_inc(sem("a_summed"), 1)

            pe.wait_ge(sem("abd_done"), 2)

            def c_z_gate(k, u):
                t = 2 * k + u
                pe.wait_ge(*ld("cn_ld", k, u))
                pe.wait_ge(*ld("xct_ld", k, u))
                pe.wait_ge(*ev("z_evac", t - 1))
                pe.wait_ge(*ev("w_evac", t - 1))
                for h in range(RH):
                    q = pe.matmul(ps_z[:, h, :], cn[u][:, h * P:(h + 1) * P], abd[:, h, :], start=True, stop=True)
                for m in range(2):
                    for c in range(2):
                        q = pe.matmul(ps_w[:, m, :], wg[:, c, m * P:(m + 1) * P], xct[u][:, c, :],
                                      start=c == 0, stop=c == 1)
                q.then_inc(sem("zw_ready"), 1)

            def c_out(k, u):
                t = 2 * k + u
                pe.wait_ge(*ev("z_evac", t))
                pe.wait_ge(*ev("gn_done", t - 1))
                for h in range(RH):
                    q = pe.matmul(ps_co[:, h * P:(h + 1) * P], zt[u][:, h, :], wh[:, h, :], start=True, stop=True)
                q.then_inc(sem("co_ready"), 1)

            def c_transpose(k, u):
                t = 2 * k + u
                pe.wait_ge(*ev("gn_done", t))
                pe.wait_ge(*ev("x2t_evac", t - 3))
                for c in range(2):
                    q = pe.transpose(ps_ct[:, c, :], ln["gn", u][5][:, c * P:(c + 1) * P], ident[:])
                q.then_inc(sem("ct_ready"), 1)

            def c_project(k, u):
                t = 2 * k + u
                pe.wait_ge(*ev("gt_done", t))
                pe.wait_ge(*ev("xsh_done", t - 5))
                for c in range(2):
                    q = pe.matmul(ps_cr, gt[u][:, c, :], wo[:, c, :], start=c == 0, stop=c == 1)
                q.then_inc(sem("cr_ready"), 1)

            def x2_transpose(k, u):
                t = 2 * k + u
                pe.wait_ge(*ev("ln2_done", t))
                pe.wait_ge(*clipped("yt_done", t + 2))
                pe.wait_ge(*ev("x2t_evac", t - 1))
                for c in range(2):
                    q = pe.transpose(ps_x2t[:, c, :], ln["ln2", u][5][:, c * P:(c + 1) * P], ident[:])
                q.then_inc(sem("x2t_ready"), 1)

            def router(k, u):
                t = 2 * k + u
                pe.wait_ge(*ev("x2t_evac", t))
                pe.wait_ge(*ev("lg_evac", t - 1))
                for c in range(2):
                    q = pe.matmul(ps_lg, x2t[u][:, c, :], wgate[:, c, :], start=c == 0, stop=c == 1)
                q.then_inc(sem("lg_ready"), 1)

            def shared_up(k, u):
                t = 2 * k + u
                pe.wait_ge(*ev("sh_done", t - 1))
                for g, ps in enumerate((ps_g, ps_u)):
                    for m in range(SC):
                        for c in range(2):
                            col = g * SH + m * IC
                            q = pe.matmul(ps[:, m, :], sgu[:, c, col:col + IC], x2t[u][:, c, :],
                                          start=c == 0, stop=c == 1)
                q.then_inc(sem("gu_ready"), 1)

            def ranks(k, u):
                t = 2 * k + u
                pe.wait_ge(*ev("hot_done", t))
                pe.wait_ge(*ev("rank_read", t - 1))
                for ps, w in ((ps_before, tri), (ps_total, ones)):
                    for j in range(K):
                        q = pe.matmul(ps, w[:], hot[u][:, j, :], start=j == 0, stop=j == K - 1)
                q.then_inc(sem("rank_ready"), 1)

            def shared_down(k, u):
                t = 2 * k + u
                pe.wait_ge(*ev("sh_done", t))
                pe.wait_ge(*clipped("ln2_sum", t + 4))
                pe.wait_ge(*ev("xsh_done", t - 1))
                for m in range(SC):
                    q = pe.matmul(ps_sd, sh[u][:, m, :], sdn[:, m, :], start=m == 0, stop=m == SC - 1)
                q.then_inc(sem("sd_ready"), 1)

            tiles(pe, [(0, c_z_gate), (1, c_out), (2, c_transpose), (3, c_project),
                       (4, x2_transpose), (5, router), (5, shared_up), (6, ranks), (7, shared_down)])

            pe.wait_ge(sem("tables"), 1)

            def unit_transpose(n):
                pe.wait_ge(sem("ur_ld"), 16 * (n + 1))
                pe.wait_ge(*ev("uxa_evac", n - 1))
                pe.wait_ge(*ev("uxb_evac", n - 1))
                for h in range(2):
                    for c in range(2):
                        q = pe.transpose(ps_ux[c][:, h * P:(h + 1) * P], ur[:, h, c * P:(c + 1) * P], ident[:])
                q.then_inc(sem("ux_ready"), 1)

            def unit(n, u):
                pe.wait_ge(*ev("uxa_evac", n))
                pe.wait_ge(*ev("uxb_evac", n))
                pe.wait_ge(*ev("uh_done", n - 1))
                for m in range(2):
                    for c in range(2):
                        q = pe.matmul(ps_uh[:, m, :], w1[u][:, c, m * IC:(m + 1) * IC], uxt[:, c, :],
                                      start=c == 0, stop=c == 1)
                q.then_inc(sem("uh_ready"), 1)
                unit_transpose(n + 1)
                pe.wait_ge(*ev("uh_done", n))
                pe.wait_ge(*ev("uya_evac", n - 1))
                pe.wait_ge(*ev("uyb_evac", n - 1))
                for h in range(2):
                    for m in range(2):
                        q = pe.matmul(ps_uy[h], uh[:, m, h * P:(h + 1) * P], w2[u][:, m, :],
                                      start=m == 0, stop=m == 1)
                q.then_inc(sem("uy_ready"), 1)

            def expert(i, u):
                e = 2 * i + u
                pe.wait_ge(sem(f"w_ld{u}"), 32 * (i + 1))
                for g in range(G):
                    n_u, first = list_units(pe, e * G + g)
                    with pe.Fori(0, n_u) as j:
                        unit(first + j, u)

            unit_transpose(0)
            with pe.Fori(0, E // 2) as i:
                for u in range(2):
                    expert(i, u)

        @block.scalar
        def _(act):
            act.preload_act_table(ACT.Exp)
            act.wait_ge(sem("consts"), n_const)
            credit(act, "q_evac", "exp_done", "pt_evac", "ot_evac", "xbt_evac", "z_evac", "w_evac", "yt_done",
                   "x2t_evac", "lg_evac", "wexp_done", "th_done", "uxb_evac", "uh_done", "uyb_evac")
            act.activation(bqs[:], bqk[:, 0:2], ACT.Copy, scale=float(HD) ** -0.5).then_inc(sem("bqs_done"), 1)
            act.wait_ge(sem("bqs_done"), 1)
            act.wait_ge(sem("m2_ready"), 1)
            act.activation(m2[:], ps_ot, ACT.Copy).then_inc(sem("m2_done"), 1)

            def q_evac(k, u):
                t = 2 * k + u
                act.wait_ge(*ev("qk_ready", t))
                act.wait_ge(*ev("s_ready", t - 2))
                for m in range(2):
                    q = act.activation(qt[u][:, m, :], ps_q[:, m, :], ACT.Identity, bias=bqs[:, m:m + 1],
                                       scale=float(HD) ** -0.5)
                q.then_inc(sem("q_evac"), 1)

            def exps(k, u):
                t = 2 * k + u
                act.wait_ge(*ev("centred", t))
                act.activation(prob[u][:], prob[u][:], ACT.Exp).then_inc(sem("exp_done"), 1)

            def pt_evac(k, u):
                t = 2 * k + u
                act.wait_ge(*ev("o_ready", t - 2))
                for h in range(2):
                    act.wait_ge(*half("pt_ready", t, h))
                    act.activation(pt[u][:, 4 * h:4 * h + 4, :], ps_pt[:, 4 * h:4 * h + 4, :],
                                   ACT.Copy).then_inc(sem("pt_evac"), 1)

            def ot_evac(k, u):
                t = 2 * k + u
                act.wait_ge(*ev("ot_ready", t))
                act.wait_ge(*ev("r_ready", t - 2))
                for c in range(2):
                    q = act.activation(ot[u][:, c, :], ps_ot[:, c, :], ACT.Identity, bias=bv[:, c:c + 1])
                q.then_inc(sem("ot_evac"), 1)

            tiles(act, [(1, exps), (0, q_evac), (2, ot_evac), (1, pt_evac)])

            def xbt_evac(k, u):
                t = 2 * k + u
                act.wait_ge(*ev("xbt_ready", t))
                act.wait_ge(*ev("mxt_ready", t - 2))
                act.wait_ge(*stored("x1t_st", k, u))
                act.activation(xbt[u][:], ps_bt, ACT.Copy).then_inc(sem("xbt_evac"), 1)

            tiles(act, [(0, xbt_evac)])

            def z_evac(k, u):
                t = 2 * k + u
                act.wait_ge(*ev("zw_ready", t))
                act.wait_ge(*ev("co_ready", t - 2))
                act.activation(zt[u][:], ps_z, ACT.Copy).then_inc(sem("z_evac"), 1)

            def w_evac(k, u):
                t = 2 * k + u
                act.wait_ge(*ev("zw_ready", t))
                act.wait_ge(*ev("gt_done", t - 2))
                act.activation(wt[u][:], ps_w, ACT.Relu).then_inc(sem("w_evac"), 1)

            def scale_shift(k, u):
                t = 2 * k + u
                act.wait_ge(*ev("ct_ready", t))
                act.wait_ge(*ev("gt_done", t - 2))
                for c in range(2):
                    q = act.activation(yt[u][:, c, :], ps_ct[:, c, :], ACT.Identity, bias=beta[:, c:c + 1],
                                       scale=gamma[:, c:c + 1])
                q.then_inc(sem("yt_done"), 1)

            def x2t_evac(k, u):
                t = 2 * k + u
                act.wait_ge(*ev("x2t_ready", t))
                act.wait_ge(*ev("gu_ready", t - 2))
                act.activation(x2t[u][:], ps_x2t, ACT.Copy).then_inc(sem("x2t_evac"), 1)

            def lg_evac(k, u):
                t = 2 * k + u
                act.wait_ge(*ev("lg_ready", t))
                act.wait_ge(*ev("topi_done", t - 2))
                act.activation(lg[u][:], ps_lg, ACT.Copy).then_inc(sem("lg_evac"), 1)

            def th_g(k, u):
                t = 2 * k + u
                act.wait_ge(*ev("gu_ready", t))
                act.wait_ge(*ev("sg_done", t - 2))
                act.activation(th[u][:], ps_g, ACT.Tanh, scale=0.5).then_inc(sem("th_done"), 1)

            def w_exp(k, u):
                t = 2 * k + u
                act.wait_ge(*ev("ntop_done", t))
                act.wait_ge(*ev("weights_done", t - 2))
                act.activation(wexp[u][:], top[u][:, 0:K], ACT.Exp, bias=ntop[u][:],
                               accum_out=wsum[u][:]).then_inc(sem("wexp_done"), 1)

            tiles(act, [(2, scale_shift), (0, z_evac), (0, w_evac), (4, x2t_evac), (5, lg_evac), (5, th_g),
                        (6, w_exp)])

            act.preload_act_table(ACT.Silu)
            act.wait_ge(sem("tables"), 1)

            def uxb_evac(n):
                act.wait_ge(*ev("ux_ready", n))
                act.activation(uxt[:, 1, :], ps_ux[1], ACT.Copy).then_inc(sem("uxb_evac"), 1)

            uxb_evac(0)
            with act.Fori(0, E * G) as v:
                n_u, first = list_units(act, v)
                with act.Fori(0, n_u) as j:
                    n = first + j
                    act.wait_ge(*ev("uh_ready", n))
                    act.activation(uh[:], ps_uh, ACT.Silu).then_inc(sem("uh_done"), 1)
                    uxb_evac(n + 1)
                    act.wait_ge(*ev("uy_ready", n))
                    act.wait_ge(sem("y_out1"), 16 * (n + 1))
                    act.activation(uy[:, 1, :], ps_uy[1], ACT.Copy).then_inc(sem("uyb_evac"), 1)

        @block.gpsimd
        def _(pool):
            pool.memset(eps[:, 0:1], LN_EPS).then_inc(sem("pool_const"), 1)
            pool.memset(eps[:, 1:2], GN_EPS).then_inc(sem("pool_const"), 1)
            pool.memset(mhalf[:], -0.5).then_inc(sem("pool_const"), 1)
            for h in range(2):
                pool.dma_start(junk[0:1, 12 + h:13 + h], a["ident"][0:1, h:h + 1]).then_inc(sem(f"y_out{h}"), 16)
            pool.wait_ge(sem("consts"), n_const)
            pool.wait_ge(sem("pool_const"), 3)
            credit(pool, "xnb_done", "rsum_done", "ln1_rstd", "gn_rstd", "ln2_rstd", "ln3_rstd", "scattered",
                   "ln1_var", "gn_var", "ln2_var", "ln3_var", "place_done")

            def rstd(name, col):
                def stage(k, u):
                    t = 2 * k + u
                    _, _, mv, ve, rs, _ = ln[name, u]
                    pool.wait_ge(*ev(name + "_mv", t))
                    pool.tensor_tensor(ve[:], mv[:, 1:2], eps[:, col:col + 1], ALU.add).then_inc(sem(name + "_var"), 1)
                    pool.wait_ge(*ev(name + "_var", t))
                    pool.wait_ge(*ev(name + "_done", t - 2))
                    pool.tensor_tensor(rs[:], ve[:], mhalf[:], ALU.pow).then_inc(sem(name + "_rstd"), 1)
                return stage

            def add_bias(k, u):
                t = 2 * k + u
                pool.wait_ge(*ld("xn_ld", k, u))
                pool.wait_ge(*ev("ln1_sum", t - 2))
                pool.tensor_tensor(xnb[u][:], xn[u][:], bout[:], ALU.add).then_inc(sem("xnb_done"), 1)

            tiles(pool, [(0, add_bias), (2, rstd("ln1", 0))])

            def scatter(k, u):
                t = 2 * k + u
                pool.wait_ge(*ld("row_ld", k, u))
                pool.tensor_copy(row[u][:, D + K:ROW], places[:, bass.ds(t, 1), :].rearrange("p a k -> p (a k)"))\
                    .then_inc(sem("place_done"), 1)
                pool.wait_ge(*ev("place_done", t))
                pool.wait_ge(*ev("dest_done", t))
                settle(pool)
                for j in range(K):
                    pool.indirect_dma_start(listd[u], bass.IndirectOffsetOnAxis(ap=dest[u][:, j:j + 1], axis=0),
                                            row[u][:], None).then_inc(sem(f"scatter{u}"), 16)

            def scatter_end(k, u):
                pool.wait_ge(sem(f"scatter{u}"), 16 * K * (k + 1))
                pool.sem_inc(sem("scattered"), 1)

            tiles(pool, [(1, rstd("gn", 1)), (3, rstd("ln2", 0)), (8, scatter_end), (7, scatter)])

            def load_weights(e, u):
                pool.dma_start(w1[u][:], a["w1_t"][bass.ds(e, 1)].rearrange("a (c p) n -> p (a c) n", p=P))\
                    .then_inc(sem(f"w_ld{u}"), 16)
                pool.dma_start(w2[u][:], a["w2_t"][bass.ds(e, 1)].rearrange("a (c p) n -> p (a c) n", p=IC))\
                    .then_inc(sem(f"w_ld{u}"), 16)

            load_weights(0, 0)
            load_weights(1, 1)
            pool.wait_ge(sem("tables"), 1)

            def scatter_results(i, u, more):
                e = 2 * i + u
                for g in range(G):
                    n_u, first = list_units(pool, e * G + g)
                    with pool.Fori(0, n_u) as j:
                        n = first + j
                        pool.wait_ge(*ev("udest_done", n))
                        pool.wait_ge(*ev("uya_evac", n))
                        for h, evac in enumerate(("uya_evac", "uyb_evac")):
                            if h:
                                pool.wait_ge(*ev(evac, n))
                            settle(pool)
                            pool.indirect_dma_start(yd, bass.IndirectOffsetOnAxis(ap=udest[:, h:h + 1], axis=0),
                                                    uy[:, h, :], None, bounds_check=T * K - 1,
                                                    oob_is_err=False).then_inc(sem(f"y_out{h}"), 16)
                if more:
                    load_weights(e + 2, u)

            with pool.Fori(0, E // 2 - 1) as i:
                for u in range(2):
                    scatter_results(i, u, True)
            for u in range(2):
                scatter_results(E // 2 - 1, u, False)

            tiles(pool, [(1, rstd("ln3", 0))])

        @block.vector
        def _(dve):
            dve.memset(zeros[:], 0.0).then_inc(sem("zeroed"), 1)
            dve.memset(abd[:], 0.0).then_inc(sem("zeroed"), 1)
            dve.memset(ones[:], 1.0).then_inc(sem("zeroed"), 1)
            dve.wait_ge(sem("consts"), n_const)
            credit(dve, "k_evac", "v_evac", "s_read", "max_done", "centred", "rinv_done", "o_norm", "ln1_sum",
                   "ln1_stat", "ln1_mv", "ln1_done", "mxt_evac", "gn_stat", "gn_mv", "gn_done", "gt_done",
                   "ln2_sum", "ln2_stat", "ln2_mv", "ln2_done", "top_done", "topi_done", "tope_done",
                   "ntop_done", "hot_done", "winv_done", "weights_done", "rank_read", "rank_done", "pick_done",
                   "destf_done", "dest_done", "sg_done", "sh_done", "xsh_done", "uxa_evac", "uya_evac",
                   "meta_done", "udest_done", "uplace_done", "uplaces_done", "ln3_sum", "ln3_stat", "ln3_mv",
                   "ln3_done")
            dve.tensor_copy(tri[:], tri_f[:]).then_inc(sem("zeroed"), 1)
            for h in range(H):
                q = dve.scalar_tensor_tensor(bias[:, h, :], rel[:], slopes[:, h:h + 1], causal[:], ALU.mult, ALU.add)
            q.then_inc(sem("bias_done"), 1)
            for g in range(G):
                dve.tensor_scalar(nextrow[g][:], iota_e[:], float(RC), None, ALU.mult).then_inc(sem("bias_done"), 1)
            dve.wait_ge(sem("bias_done"), 1 + G)
            dve.wait_ge(sem("zeroed"), 4)

            def norm_stats(name, t, u, src):
                _, st, mv, _, _, _ = ln[name, u]
                dve.bn_stats(st[:], src).then_inc(sem(name + "_stat"), 1)
                dve.wait_ge(*ev(name + "_stat", t))
                dve.wait_ge(*ev(name + "_rstd", t - 2))
                settle(dve)
                dve.bn_aggr(mv[:], st[:]).then_inc(sem(name + "_mv"), 1)

            def norm_apply(name, t, u, src):
                _, _, mv, _, rs, y = ln[name, u]
                dve.wait_ge(*ev(name + "_rstd", t))
                dve.tensor_scalar(y[:], src, mv[:, 0:1], rs[:, 0:1], ALU.subtract, ALU.mult)\
                   .then_inc(sem(name + "_done"), 1)

            def o_norm(k, u):
                t = 2 * k + u
                dve.wait_ge(*ev("rsum_done", t))
                dve.reciprocal(rinv[u][:], rsum[u][:]).then_inc(sem("rinv_done"), 1)
                dve.wait_ge(*ev("rinv_done", t))
                dve.wait_ge(*ev("o_ready", t))
                dve.wait_ge(*ev("ot_ready", t - 2))
                dve.tensor_tensor(on[u][:].rearrange("p (h d) -> p h d", h=H),
                                  ps_o.rearrange("p (h d) -> p h d", h=H),
                                  rinv[u][:].unsqueeze(2).to_broadcast([P, H, HD]), ALU.mult)\
                   .then_inc(sem("o_norm"), 1)

            def kv_evac(k, u):
                t = 2 * k + u
                dve.wait_ge(*ev("qk_ready", t))
                dve.wait_ge(*ev("s_ready", t - 2))
                for m in range(2):
                    for par in range(2):
                        q = dve.tensor_scalar(kt[u][:, m, par, :], ps_k[:, m, :], bqk[:, 2 + m:3 + m],
                                              kpar[:, par:par + 1], ALU.add, ALU.mult)
                q.then_inc(sem("k_evac"), 1)
                dve.wait_ge(*ev("v_ready", t))
                dve.wait_ge(*ev("o_ready", t - 2))
                dve.tensor_tensor(vbd[u][:], ps_v, vpar[:].unsqueeze(1).to_broadcast([P, 2, D]), ALU.mult)\
                   .then_inc(sem("v_evac"), 1)

            def residual1(k, u):
                t = 2 * k + u
                r = ln["ln1", u][0]
                dve.wait_ge(*ev("r_ready", t))
                dve.wait_ge(*ev("xnb_done", t))
                dve.tensor_tensor(r[:], ps_r, xnb[u][:], ALU.add).then_inc(sem("ln1_sum"), 1)
                dve.wait_ge(*ev("ln1_sum", t))
                norm_stats("ln1", t, u, r[:])

            def softmax(k, u):
                t = 2 * k + u
                dve.wait_ge(*ev("s_ready", t))
                dve.wait_ge(*ev("pt_ready", t - 2))
                dve.tensor_tensor(prob[u][:], ps_s.rearrange("p (h s) -> p h s", h=H), bias[:], ALU.add)\
                   .then_inc(sem("s_read"), 1)
                dve.wait_ge(*ev("s_read", t))
                dve.tensor_reduce(mx[u][:], prob[u][:], AX, ALU.max).then_inc(sem("max_done"), 1)
                dve.wait_ge(*ev("max_done", t))
                dve.tensor_tensor(prob[u][:], prob[u][:], mx[u][:].unsqueeze(2).to_broadcast([P, H, S]),
                                  ALU.subtract).then_inc(sem("centred"), 1)

            def row_sums(k, u):
                t = 2 * k + u
                dve.wait_ge(*ev("exp_done", t))
                dve.tensor_reduce(rsum[u][:], prob[u][:], AX, ALU.add).then_inc(sem("rsum_done"), 1)

            def apply1(k, u):
                t = 2 * k + u
                dve.wait_ge(*stored("x1_st", k, u))
                norm_apply("ln1", t, u, ln["ln1", u][0][:])

            tiles(dve, [(2, o_norm), (0, kv_evac), (1, row_sums), (2, residual1), (0, softmax), (2, apply1)])

            def mxt_evac(k, u):
                t = 2 * k + u
                dve.wait_ge(*ev("mxt_ready", t))
                dve.wait_ge(*ev("a_added", t - 2))
                dve.tensor_copy(mxt[u][:], ps_bm).then_inc(sem("mxt_evac"), 1)

            tiles(dve, [(1, mxt_evac)])
            dve.wait_ge(sem("a_summed"), 1)
            dve.tensor_tensor(araw[:], ps_a, decay[:], ALU.mult).then_inc(sem("araw_done"), 1)
            dve.wait_ge(sem("araw_done"), 1)
            dve.tensor_scalar(afloor[:], araw[:], 1.0, None, ALU.max).then_inc(sem("araw_done"), 1)
            dve.wait_ge(sem("araw_done"), 2)
            for b in range(2):
                half_ = slice(b * S, (b + 1) * S)
                dve.scalar_tensor_tensor(abd[half_, :, half_], araw[half_, :, :], -1.0, afloor[half_, :, :],
                                         ALU.mult, ALU.max)\
                   .then_inc(sem("abd_done"), 1)

            def group_norm(k, u):
                t = 2 * k + u
                dve.wait_ge(*ev("co_ready", t))
                norm_stats("gn", t, u, ps_co)

            def group_apply(k, u):
                t = 2 * k + u
                dve.wait_ge(*ev("ct_ready", t - 2))
                norm_apply("gn", t, u, ps_co)

            def gated(k, u):
                t = 2 * k + u
                dve.wait_ge(*ev("yt_done", t))
                dve.wait_ge(*ev("w_evac", t))
                dve.wait_ge(*ev("cr_ready", t - 2))
                dve.tensor_tensor(gt[u][:], yt[u][:], wt[u][:], ALU.mult).then_inc(sem("gt_done"), 1)

            def residual2(k, u):
                t = 2 * k + u
                r = ln["ln2", u][0]
                dve.wait_ge(*ev("cr_ready", t))
                dve.wait_ge(*ld("xc_ld", k, u))
                dve.tensor_tensor(r[:], ps_cr, xc[u][:], ALU.add).then_inc(sem("ln2_sum"), 1)
                dve.wait_ge(*ev("ln2_sum", t))
                norm_stats("ln2", t, u, r[:])

            def apply2(k, u):
                t = 2 * k + u
                dve.wait_ge(*stored("x2_st", k, u))
                dve.wait_ge(*ev("x2t_ready", t - 2))
                norm_apply("ln2", t, u, ln["ln2", u][0][:])

            def top6(k, u):
                t = 2 * k + u
                dve.wait_ge(*ev("lg_evac", t))
                dve.wait_ge(*ev("wexp_done", t - 2))
                settle(dve)
                dve.max(top[u][:], lg[u][:]).then_inc(sem("top_done"), 1)
                dve.wait_ge(*ev("top_done", t))
                settle(dve)
                dve.max_index(topi[u][:], top[u][:], lg[u][:]).then_inc(sem("topi_done"), 1)
                dve.tensor_scalar(ntop[u][:], top[u][:, 0:1], -1.0, None, ALU.mult).then_inc(sem("ntop_done"), 1)
                dve.wait_ge(*ev("topi_done", t))
                dve.wait_ge(*ev("dest_done", t - 2))
                dve.tensor_copy(tope[u][:], topi[u][:, 0:K]).then_inc(sem("tope_done"), 1)
                dve.wait_ge(*ev("tope_done", t))
                dve.wait_ge(*ev("rank_ready", t - 2))
                dve.tensor_tensor(hot[u][:], iota_e[:].unsqueeze(1).to_broadcast([P, K, E]),
                                  tope[u][:].unsqueeze(2).to_broadcast([P, K, E]), ALU.is_equal)\
                   .then_inc(sem("hot_done"), 1)

            def gate_weights(k, u):
                t = 2 * k + u
                dve.wait_ge(*ev("wexp_done", t))
                dve.reciprocal(winv[u][:], wsum[u][:]).then_inc(sem("winv_done"), 1)
                dve.wait_ge(*ev("winv_done", t))
                dve.tensor_scalar(weights[:, bass.ds(t, 1), :].rearrange("p a k -> p (a k)"), wexp[u][:],
                                  winv[u][:, 0:1], None, ALU.mult).then_inc(sem("weights_done"), 1)

            def destinations(k, u):
                t = 2 * k + u
                dve.wait_ge(*ev("rank_ready", t))
                dve.tensor_tensor(rank[u][:], ps_before, nextrow[u][:], ALU.add).then_inc(sem("rank_done"), 1)
                dve.wait_ge(*ev("rank_done", t))
                dve.tensor_tensor(nextrow[u][:], ps_total, nextrow[u][:], ALU.add).then_inc(sem("rank_read"), 1)
                dve.tensor_tensor(pick[:], hot[u][:], rank[u][:].unsqueeze(1).to_broadcast([P, K, E]), ALU.mult)\
                   .then_inc(sem("pick_done"), 1)
                dve.wait_ge(*ev("pick_done", t))
                dve.tensor_reduce(destf[u][:], pick[:], AX, ALU.add).then_inc(sem("destf_done"), 1)
                dve.wait_ge(*ev("destf_done", t))
                dve.wait_ge(*ev("scattered", t - 2))
                dve.tensor_copy(dest[u][:], destf[u][:])
                dve.tensor_copy(row[u][:, D:D + K], tope[u][:]).then_inc(sem("dest_done"), 1)
                dve.wait_ge(*ev("rank_read", t))

            def shared_gate(k, u):
                t = 2 * k + u
                dve.wait_ge(*ev("th_done", t))
                dve.scalar_tensor_tensor(sg[u][:], th[u][:], 1.0, ps_g, ALU.add, ALU.mult).then_inc(sem("sg_done"), 1)
                dve.wait_ge(*ev("sg_done", t))
                dve.wait_ge(*ev("sd_ready", t - 2))
                dve.scalar_tensor_tensor(sh[u][:], sg[u][:], 0.5, ps_u, ALU.mult, ALU.mult).then_inc(sem("sh_done"), 1)

            def add_shared(k, u):
                t = 2 * k + u
                dve.wait_ge(*ev("sd_ready", t))
                dve.wait_ge(*ld("xs_ld", k, u))
                dve.wait_ge(*stored("xsh_st", k, u))
                dve.tensor_tensor(xsh[u][:], ps_sd, xs[u][:], ALU.add).then_inc(sem("xsh_done"), 1)

            tiles(dve, [(1, group_norm), (3, residual2), (1, group_apply), (2, gated), (3, apply2), (5, top6),
                        (6, destinations), (6, gate_weights), (5, shared_gate), (7, add_shared)])

            dve.tensor_scalar(cntf[:, 0, 0:E], iota_e[0:1, :], float(RC), None, ALU.mult).then_inc(sem("tab"), 1)
            dve.memset(cntf[:, 3, :], 1.0).then_inc(sem("tab"), 1)
            dve.memset(unit0[:, 0:1], 0).then_inc(sem("tab"), 1)
            dve.wait_ge(sem("tab"), 3)
            for g in range(G):
                q = dve.tensor_tensor(cntf[:, 1, :].rearrange("p (e g) -> p e g", g=G)[:, :, g],
                                      nextrow[g][0:1, :], cntf[:, 0, 0:E], ALU.subtract)
            q.then_inc(sem("tab"), 1)
            dve.wait_ge(sem("tab"), 4)
            dve.tensor_copy(n_rows[:], cntf[:, 1, :]).then_inc(sem("tab"), 1)
            dve.tensor_scalar(cnti[:, 0, :], cntf[:, 1, :], float(UNIT - 1), None, ALU.add).then_inc(sem("tab"), 1)
            dve.wait_ge(sem("tab"), 6)
            dve.tensor_scalar(cnti[:, 1, :], cnti[:, 0, :], UNIT.bit_length() - 1, None, ALU.arith_shift_right)\
               .then_inc(sem("tab"), 1)
            dve.wait_ge(sem("tab"), 7)
            dve.tensor_scalar(n_units[:], cnti[:, 1, :], 1.0, None, ALU.max).then_inc(sem("tab"), 1)
            dve.tensor_scalar(cntf[:, 2, :], cnti[:, 1, :], 1.0, None, ALU.max).then_inc(sem("tab"), 1)
            dve.wait_ge(sem("tab"), 9)
            dve.tensor_tensor_scan(cntf[:, 0, :], cntf[:, 3, :], cntf[:, 2, :], 0.0, ALU.mult, ALU.add)\
               .then_inc(sem("tab"), 1)
            dve.wait_ge(sem("tab"), 10)
            dve.tensor_copy(unit0[:, 1:E * G + 1], cntf[:, 0, :]).then_inc(sem("tables"), 1)
            dve.wait_ge(sem("tables"), 1)

            def uxa_evac(n):
                dve.wait_ge(*ev("ux_ready", n))
                dve.tensor_copy(uxt[:, 0, :], ps_ux[0]).then_inc(sem("uxa_evac"), 1)

            def copy_meta(n):
                dve.wait_ge(*ev("uplace_done", n - 1))
                dve.tensor_copy(meta[:], ur[:, :, D:ROW]).then_inc(sem("meta_done"), 1)

            uxa_evac(0)
            copy_meta(0)
            with dve.Fori(0, E) as e:
                for g in range(G):
                    n_u, first = list_units(dve, e * G + g)
                    with dve.Fori(0, n_u) as j:
                        n = first + j
                        uxa_evac(n + 1)
                        dve.wait_ge(*ev("meta_done", n))
                        dve.wait_ge(*ev("uplaces_done", n - 1))
                        dve.scalar_tensor_tensor(uplace[:], meta[:, :, 0:K], iota_e[:, bass.ds(e, 1)],
                                                 meta[:, :, K:2 * K], ALU.is_equal, ALU.mult)\
                           .then_inc(sem("uplace_done"), 1)
                        dve.wait_ge(*ev("uplace_done", n))
                        dve.wait_ge(*ev("udest_done", n - 1))
                        dve.tensor_reduce(uplace_s[:], uplace[:], AX, ALU.add).then_inc(sem("uplaces_done"), 1)
                        copy_meta(n + 1)
                        dve.wait_ge(*ev("uplaces_done", n))
                        for h in range(2):
                            dve.wait_ge(sem(f"y_out{h}"), 16 * (n + 1))
                        dve.tensor_scalar(udest[:], uplace_s[:], float(NOWHERE), None, ALU.add)\
                           .then_inc(sem("udest_done"), 1)
                        dve.wait_ge(*ev("uy_ready", n))
                        dve.tensor_copy(uy[:, 0, :], ps_uy[0]).then_inc(sem("uya_evac"), 1)

            def combine(k, u):
                t = 2 * k + u
                r = ln["ln3", u][0]
                dve.wait_ge(*ld("xe_ld", k, u))
                dve.wait_ge(*ld("y6_ld", k, u))
                dve.wait_ge(*ev("ln3_done", t - 2))
                for j in range(K):
                    if j:
                        dve.wait_ge(sem("e_chain"), (K - 1) * t + j)
                    src = r if j else xe[u]
                    q = dve.scalar_tensor_tensor(r[:], y6[u][:, j, :], weights[:, bass.ds(t, 1), j:j + 1]
                                                 .rearrange("p a k -> p (a k)"), src[:], ALU.mult, ALU.add)
                    q.then_inc(sem("e_chain" if j < K - 1 else "ln3_sum"), 1)
                dve.wait_ge(*ev("ln3_sum", t))
                norm_stats("ln3", t, u, r[:])

            def apply3(k, u):
                t = 2 * k + u
                dve.wait_ge(*stored("out_st", k, u))
                norm_apply("ln3", t, u, ln["ln3", u][0][:])

            tiles(dve, [(0, combine), (1, apply3)])


def _shape_constants():
    p = np.arange(P)
    q, k = p[:, None] % S, np.arange(S)[None, :]
    seen = k <= q
    gam = (np.float32(1) - np.float32(2) ** (-5 - np.arange(RH, dtype=np.float32))).astype(np.float32)
    expo = (k - np.arange(S)[:, None]).astype(np.float32)
    dec = np.where(expo[None] <= 0, gam[:, None, None] ** expo[None], 0).astype(np.float32)
    dec = dec / np.sqrt(dec.sum(-1))[:, None, :] / np.sqrt(np.float32(D // RH))
    dec_t = np.tile(dec.transpose(2, 0, 1), (2, 1, 1))
    tok = np.arange(NT)[None, :, None] * P + p[:, None, None]
    return {
        "ident": np.eye(P),
        "k_parity": np.stack([(p // HD) % 2 == 0, (p // HD) % 2 == 1], 1),
        "v_parity": (np.arange(D)[None, :] // HD) % 2 == (p // S)[:, None],
        "rel": np.where(seen, k - q, 0),
        "causal": np.where(seen, 0.0, -1e9),
        "decay_t": dec_t,
        "tri": p[:, None] < p[None, :],
        "iota_e": np.broadcast_to(np.arange(E), (P, E)),
        "places": tok * K + np.arange(K) - NOWHERE,
    }


def kernel(x, ctx_2048, L0_attn_qkv_w, L0_attn_qkv_b, L0_attn_out_w, L0_attn_out_b, L0_attn_alibi_slopes,
           L0_xattn_Wh, L0_xattn_wg_w, L0_xattn_wo_w, L0_xattn_gn_gamma, L0_xattn_gn_beta, L0_ffn_gate_w,
           L0_ffn_experts_w1, L0_ffn_experts_w2, L0_ffn_shared_gate_up, L0_ffn_shared_down):
    import concourse.bacc as bacc
    from concourse.bass_utils import run_bass_kernel_spmd

    rows = np.asarray(x).reshape(T, D)
    ctx = np.asarray(ctx_2048).reshape(T, D)
    qkv_b = np.asarray(L0_attn_qkv_b)
    dims = (np.array(ORDER)[:, None] * HD + np.arange(HD)).reshape(-1)
    qkv_rows = np.concatenate([np.arange(2 * D), 2 * D + dims])
    arrays = {
        "x": rows, "x_t": rows.T, "ctx": ctx, "ctx_t": ctx.T,
        "wqkv_t": np.asarray(L0_attn_qkv_w)[qkv_rows].T,
        "b_qk": qkv_b[:2 * D].reshape(4, P).T, "b_v": qkv_b[2 * D + dims].reshape(2, P).T,
        "slopes": np.broadcast_to(np.asarray(L0_attn_alibi_slopes)[np.array(ORDER)], (P, H)),
        "wout_t": np.asarray(L0_attn_out_w).T[dims],
        "b_out": np.broadcast_to(np.asarray(L0_attn_out_b), (P, D)),
        "wh": np.asarray(L0_xattn_Wh), "wh_t": np.asarray(L0_xattn_Wh).transpose(0, 2, 1),
        "wg": np.asarray(L0_xattn_wg_w), "wo": np.asarray(L0_xattn_wo_w),
        "gamma": np.asarray(L0_xattn_gn_gamma).reshape(2, P).T,
        "beta": np.asarray(L0_xattn_gn_beta).reshape(2, P).T,
        "gate_t": np.asarray(L0_ffn_gate_w).T,
        "w1_t": np.asarray(L0_ffn_experts_w1).transpose(0, 2, 1),
        "w2_t": np.asarray(L0_ffn_experts_w2).transpose(0, 2, 1),
        "sgu_t": np.asarray(L0_ffn_shared_gate_up).T,
        "sdn_t": np.asarray(L0_ffn_shared_down).T,
    }
    arrays = {n: np.ascontiguousarray(v) for n, v in arrays.items()}
    arrays.update({n: np.ascontiguousarray(v, dtype=np.float32) for n, v in _shape_constants().items()})
    nc = bacc.Bacc("TRN2", target_bir_lowering=False, num_devices=1)
    aps = {n: nc.dram_tensor("in_" + n, v.shape, F32, kind="ExternalInput").ap() for n, v in arrays.items()}
    out = nc.dram_tensor("out_rows", (T, D), F32, kind="ExternalOutput").ap()
    decoder_layer(nc, aps, out)
    r = run_bass_kernel_spmd(nc, [{"in_" + n: v for n, v in arrays.items()}], core_ids=[0])
    return r.results[0]["out_rows"].reshape(B, S, D)
```

```python
from contextlib import ExitStack

import numpy as np

import concourse.bass as bass
from concourse import mybir

F32 = mybir.dt.float32
BF16 = mybir.dt.bfloat16
I32 = mybir.dt.int32
U32 = mybir.dt.uint32
ACT = mybir.ActivationFunctionType
ALU = mybir.AluOpType
AX = mybir.AxisListType.X

P = 128
B, S, D = 64, 64, 256
T = B * S
NT = T // P
H, HD = 16, 16
RH = 2
E, I, K = 64, 176, 6
IC = I // 2
SH = 2 * I
SC = SH // IC
BLOCKS = T * K // P + E
FILL = 4
BW = BLOCKS + 8
WS = 4
ROW = D + 2 * K
NOWHERE = 1 << 20
ORDER = [8 * m + 2 * (2 * g2 + g1) + par for g1 in range(2) for g2 in range(2) for m in range(2) for par in range(2)]
LN_EPS, GN_EPS = 1e-5, 1e-3

PER_TILE = {"pt_ready": 2, "pt_evac": 2}
CREDIT = 6


def decoder_layer(nc, a, out):
    listd = nc.dram_tensor("expert_rows", ((BLOCKS + 2 * FILL) * P, ROW), F32, kind="Internal").ap()
    yd = nc.dram_tensor("expert_results", (T * K, D), F32, kind="Internal").ap()

    with ExitStack() as ctx:
        def sb(name, shape, dt=F32):
            return ctx.enter_context(nc.sbuf_tensor(name, shape, dt))

        sems = {}

        def sem(name):
            if name not in sems:
                sems[name] = ctx.enter_context(nc.semaphore(name))
            return sems[name]

        def ev(name, t):
            n = PER_TILE.get(name, 1)
            return sem(name), (t + 1 + CREDIT) * n

        def clipped(name, t):
            return ev(name, min(t, NT - 1) if isinstance(t, int) else t)

        def half(name, t, h):
            return sem(name), (t + CREDIT) * 2 + h + 1

        def credit(eng, *names):
            for name in names:
                eng.sem_inc(sem(name), CREDIT * PER_TILE.get(name, 1))

        def tiles(eng, lags, ways=2):
            deep = -(-max(l for l, _ in lags) // ways) * ways
            for s in range(deep):
                for l, f in lags:
                    if s - l >= 0:
                        f((s - l) // ways, (s - l) % ways)
            with eng.Fori(0, (NT - deep) // ways) as i:
                for r in range(ways):
                    for l, f in lags:
                        f(i + (deep + r - l) // ways, (r - l) % ways)
            for s in range(NT, NT + deep):
                for l, f in lags:
                    if 0 <= s - l < NT:
                        f((s - l) // ways, (s - l) % ways)

        def expert_of(group, u):
            return (group >> (6 * u)) & (E - 1)

        def blocks(eng, lags, looked_up=()):
            deep = 8
            looped = eng.value_load(looped_n[0:1, 0:1], min_val=T * K // P // 4 - deep // 4, max_val=BLOCKS // 4 - deep // 4)
            def group_of(k):
                return eng.value_load(packed[0:1, bass.ds(k, 1)], min_val=0, max_val=E ** 4 - 1)

            def run(k_of, wanted):
                known = {}
                for s in range(4):
                    for l, f in lags:
                        if wanted(s - l):
                            k, u = k_of(s - l), (s - l) % 4
                            if f in looked_up:
                                if l not in known:
                                    known[l] = group_of(k)
                                f(k, u, known[l])
                            else:
                                f(k, u)

            for g in range(deep // 4):
                run(lambda x: (x + 4 * g) // 4, lambda x: x + 4 * g >= 0)
            with eng.Fori(0, looped) as i:
                run(lambda x: i + (deep + x) // 4, lambda x: True)
            for g in range(deep // 4):
                run(lambda x: looped + (deep + x + 4 * g) // 4, lambda x: x + 4 * g < 0)

        consts = {}

        def const(name, src, shape, dt=F32):
            consts[name] = (sb("c_" + name, shape, dt), src)
            return consts[name][0]

        kc = "(c p) n -> p c n"
        ident = const("ident", a["ident"], [P, P])
        wqkv = const("wqkv", a["wqkv_t"].rearrange(kc, p=P), [P, 2, 3 * D])
        bqk = const("bqk", a["b_qk"], [P, 4])
        bv = const("bv", a["b_v"], [P, 2])
        kpar = const("kpar", a["k_parity"], [P, 2])
        vpar = const("vpar", a["v_parity"], [P, D])
        rel = const("rel", a["rel"], [P, S])
        causal = const("causal", a["causal"], [P, S])
        slopes = const("slopes", a["slopes"], [P, H])
        wout = const("wout", a["wout_t"].rearrange(kc, p=P), [P, 2, D])
        bout = const("bout", a["b_out"], [P, D])
        wht = const("wht", a["wh_t"].rearrange("h e d -> e h d"), [P, RH, P])
        wh = const("wh", a["wh"].rearrange("h d e -> d h e"), [P, RH, P])
        decay = const("decay", a["decay_t"], [P, RH, S])
        wg = const("wg", a["wg"].rearrange(kc, p=P), [P, 2, D])
        wo = const("wo", a["wo"].rearrange(kc, p=P), [P, 2, D])
        gamma = const("gamma", a["gamma"], [P, 2])
        beta = const("beta", a["beta"], [P, 2])
        wgate = const("wgate", a["gate_t"].rearrange(kc, p=P), [P, 2, E])
        pair = const("pair", a["pair"], [P, P])
        tri_f = const("tri_f", a["tri"], [P, P])
        iota_e = const("iota_e", a["iota_e"], [P, E])
        iota_b = const("iota_b", a["iota_b"], [E, BW])
        places = const("places", a["places"], [P, NT, K])
        sgu = const("sgu", a["sgu_t"].rearrange(kc, p=P), [P, 2, 2 * SH])
        sdn = const("sdn", a["sdn_t"].rearrange("(c p) n -> p c n", p=IC), [IC, SC, D])
        tri = sb("tri", [P, P], BF16)
        ones = sb("ones", [P, P], BF16)
        bqs = sb("bqs", [P, 2])
        bias = sb("bias", [P, H, S])
        m2 = sb("m2", [P, RH, P])
        eps = sb("eps", [P, 2])
        mhalf = sb("mhalf", [P, 1])
        zeros = sb("zeros", [P, FILL, ROW])
        junk = sb("junk", [1, 16])

        xall = sb("xall", [P, NT, D])
        xtall = sb("xtall", [P, NT, 2, P])

        xt = [sb(f"xt{u}", [P, 2, 2, 2, S]) for u in range(2)]
        xn = [sb(f"xn{u}", [P, D]) for u in range(2)]
        xnb = [sb(f"xnb{u}", [P, D]) for u in range(2)]
        qt = [sb(f"qt{u}", [P, 2, P]) for u in range(2)]
        kt = [sb(f"kt{u}", [P, 2, 2, P]) for u in range(2)]
        vbd = [sb(f"vbd{u}", [P, 2, D]) for u in range(2)]
        prob = [sb(f"prob{u}", [P, H, S]) for u in range(2)]
        mx = [sb(f"mx{u}", [P, H]) for u in range(2)]
        rsum = [sb(f"rsum{u}", [P, H]) for u in range(2)]
        rinv = [sb(f"rinv{u}", [P, H]) for u in range(2)]
        pt = [sb(f"pt{u}", [P, H // 2, P]) for u in range(2)]
        on = [sb(f"on{u}", [P, D]) for u in range(2)]
        ot = [sb(f"ot{u}", [P, 2, P]) for u in range(2)]
        ln = {}
        for name in ("ln1", "gn", "ln2", "ln3"):
            for u in range(2):
                ln[name, u] = (sb(f"{name}_r{u}", [P, D]), sb(f"{name}_st{u}", [P, 6]), sb(f"{name}_mv{u}", [P, 2]),
                               sb(f"{name}_ve{u}", [P, 1]), sb(f"{name}_rs{u}", [P, 1]), sb(f"{name}_y{u}", [P, D]))
        for u in range(2):
            ln["ln3", 2 + u] = ln["gn", u]
        xb = [sb(f"xb{u}", [P, D]) for u in range(2)]
        cbt = [sb(f"cbt{u}", [P, 2, P]) for u in range(4)]
        mxt = [sb(f"mxt{u}", [P, RH, P]) for u in range(2)]
        adiag = sb("adiag", [P, RH, S])
        araw = sb("araw", [P, RH, S])
        afloor = sb("afloor", [P, RH, S])
        abd = sb("abd", [P, RH, P])
        cn = [sb(f"cn{u}", [P, D]) for u in range(4)]
        zt = [sb(f"zt{u}", [P, RH, P]) for u in range(2)]
        wt = [sb(f"wt{u}", [P, 2, P]) for u in range(2)] + [kt[0][:, :, par, :] for par in range(2)]
        yt = [sb(f"yt{u}", [P, 2, P]) for u in range(2)]
        gt = [sb(f"gt{u}", [P, 2, P]) for u in range(2)]
        x2t = [sb(f"x2t{u}", [P, 2, P]) for u in range(2)]
        lg = [sb(f"lg{u}", [P, E]) for u in range(2)]
        top = [sb(f"top{u}", [P, 8]) for u in range(2)]
        topi = [sb(f"topi{u}", [P, 8], U32) for u in range(2)]
        tope = sb("tope", [P, NT, K])
        ntop = [sb(f"ntop{u}", [P, 1]) for u in range(2)]
        wexp = [sb(f"wexp{u}", [P, K]) for u in range(2)]
        wsum = [sb(f"wsum{u}", [P, 1]) for u in range(2)]
        winv = [sb(f"winv{u}", [P, 1]) for u in range(2)]
        weights = sb("weights", [P, NT, K])
        hot = [sb(f"hot{u}", [P, K, E], BF16) for u in range(2)]
        rank = sb("rank", [P, NT, E])
        count = sb("count", [P, E])
        start = sb("start", [P, E])
        scan = sb("scan", [P, 3, E])
        hot_s, pick = (kt[u][:].rearrange("p m par n -> p (m par n)")[:, 0:K * E]
                       .rearrange("p (k n) -> p k n", k=K) for u in range(2))
        place_s = sb("place_s", [P, E])
        destf = sb("destf", [P, K])
        dest = [sb(f"dest{u}", [P, K], I32) for u in range(2)]
        row = [sb(f"row{u}", [P, ROW]) for u in range(2)]
        blocks_i = sb("blocks_i", [P, 2, E], I32)
        cum_t = sb("cum_t", [E, 1])
        before_b = vbd[0][0:E].rearrange("p b n -> p (b n)")[:, 0:BW]
        of_block = sb("of_block", [1, BW])
        quarter = sb("quarter", [1, 1], I32)
        packed_f = sb("packed_f", [1, BW // 4])
        packed = sb("packed", [1, BW // 4], I32)
        first = sb("first", [1, E + 1], I32)
        groups_n = sb("groups_n", [1, 1], I32)
        looped_n = sb("looped_n", [1, 1], I32)
        p_flat = [prob[u][0:IC].rearrange("p (a c) s -> p a (c s)", a=2) for u in range(2)]
        th = [p_flat[u][:, 0, :].rearrange("p (c n) -> p c n", c=SC) for u in range(2)]
        sg = [p_flat[u][:, 1, :].rearrange("p (c n) -> p c n", c=SC) for u in range(2)]
        sh = [pt[u][0:IC, 0:SC, :] for u in range(2)]
        d_flat = xtall[:].rearrange("p t c n -> p (t c n)")
        d_used = [0]

        def carve(parts, count, n):
            i = d_used[0]
            d_used[0] += count * n
            return d_flat[0:parts, i:i + count * n].rearrange("p (b n) -> p b n", b=count)

        w1 = carve(P, WS, 2 * I)
        w2 = carve(IC, WS, 2 * D)
        ur = carve(P, 4, ROW)
        uxt = carve(P, 4, P)
        uh = carve(P, 2, I)
        uht = carve(IC, 4, P)
        uy = carve(P, 4, D)
        uplace = sb("uplace", [P, K])
        uplace_s = [sb(f"uplace_s{u}", [P, 1]) for u in range(4)]
        udest = [sb(f"udest{u}", [P, 1], I32) for u in range(4)]
        y6_flat = xtall[:].rearrange("p t c n -> p (t c n)")[:, 0:4 * K * D].rearrange("p (b n) -> p b n", b=4)
        y6 = [y6_flat[:, b, :].rearrange("p (k n) -> p k n", k=K) for b in range(4)]

        psum = ctx.enter_context(nc.psum_tensor("psum", [P, 8, 512], F32))

        def bank(i, n=2):
            return psum[:, i, 0:n * P].rearrange("p (c n) -> p c n", c=n)

        ps_q, ps_k, ps_v = bank(0), bank(1), psum[:, 2, :].rearrange("p (b n) -> p b n", b=2)
        ps_s = psum[:, 3:5, :].rearrange("p a n -> p (a n)")
        ps_pt = psum[:, 5:7, :].rearrange("p a (c n) -> p (a c) n", c=4)
        ps_o = ps_r = psum[:, 7, 0:D]
        ps_ot = bank(7)
        ps_bt, ps_bm, ps_a, ps_ad = bank(0), bank(1), psum[:, 3:5, 0:P], psum[:, 5, 0:RH * S].rearrange("p (h s) -> p h s", h=RH)
        ps_z, ps_w = bank(0), psum[:, 0, D:2 * D].rearrange("p (c n) -> p c n", c=2)
        ps_co, ps_ct, ps_cr, ps_lg, ps_x2t = [psum[:, i, 0:D] for i in (1, 6)], bank(2), psum[:, 3, 0:D], psum[:, 4, 0:E], bank(5)
        ps_before, ps_total = psum[:, 7, 0:E], psum[:, 7, E:2 * E]
        ps_g, ps_u = ([psum[0:IC, i, :].rearrange("p (c n) -> p c n", c=SC) for i in b] for b in ((0, 5), (1, 6)))
        ps_sd = psum[:, 3, 0:D]
        ps_lg_t, ps_exp = psum[0:E, 4, 0:P], psum[0:E, 7, 0:BW]
        ps_ux, ps_uh, ps_uht, ps_uy = ([psum[:, 2 * i + u, :] for u in range(2)] for i in range(4))

        block = ctx.enter_context(nc.Block())

        def rows(t):
            return bass.ds(t * P, P)

        def slot(buf, t):
            names = "bcd"[:len(buf.shape) - 2]
            spaced = " ".join(names)
            return buf[:, bass.ds(t, 1)].rearrange(f"p a {spaced} -> p (a {names[0]}) {' '.join(names[1:])}")

        def load(eng, dst, src, name):
            eng.dma_start(dst, src).then_inc(sem(name), 16)

        def ld(name, k, u, n=1):
            return sem(f"{name}{u}"), 16 * n * (k + 1)

        def stored(name, k, u):
            return sem(f"{name}{u}"), 16 * (k + 1)

        def prime(eng, *names):
            for name in names:
                n = primed[0]
                primed[0] += 1
                eng.dma_start(junk[0:1, n:n + 1], a["ident"][0:1, n:n + 1]).then_inc(sem(name), 16)

        def two(stage):
            return lambda k, u: stage(2 * k + u // 2, u % 2)

        primed = [0]
        n_const = 16 * len(consts)

        def settle(eng):
            eng.sem_inc(sem("waits_passed"), 1)

        @block.sync
        def _(sp):
            for t_, src in consts.values():
                sp.dma_start(t_[:], src).then_inc(sem("consts"), 16)
            prime(sp, "out_st0", "out_st1", "out_st2", "out_st3")
            sp.wait_ge(sem("zeroed"), 4)

            def load_twice(dst, src, t, name):
                for copy in range(2):
                    for c in range(2):
                        sp.dma_start(dst[:, c, :, copy, :], src[c * P:(c + 1) * P, bass.ds(t * P, P)]
                                     .rearrange("p (b s) -> p b s", b=2)).then_inc(sem(name), 16)

            def load_a(k, u):
                t = 2 * k + u
                sp.wait_ge(*ev("v_ready", t - 2))
                load_twice(xt[u], a["x_t"], t, f"xt_ld{u}")
                sp.wait_ge(*ev("xnb_done", t - 2))
                load(sp, xn[u][:], a["x"][rows(2 * k + u), :], f"xn_ld{u}")

            def fill(k, u):
                for i in range(2):
                    sp.dma_start(listd[bass.ds((2 * (2 * k + u) + i) * FILL * P, FILL * P), :]
                                 .rearrange("(h p) n -> p h n", p=P), zeros[:]).then_inc(sem("filled"), 16)

            tiles(sp, [(0, load_a), (0, fill)])
            sp.dma_start(listd[BLOCKS * P:(BLOCKS + FILL) * P, :].rearrange("(h p) n -> p h n", p=P), zeros[:])\
              .then_inc(sem("filled"), 16)

            def load_b(k, u):
                t = 4 * k + u
                sp.wait_ge(*ev("a_added", t - 4))
                load(sp, cbt[u][:], a["ctx_t"][:, bass.ds(t * P, P)].rearrange("(c p) n -> p c n", p=P), f"cbt_ld{u}")

            tiles(sp, [(0, load_b)], ways=4)

            def load_c(k, u):
                t = 4 * k + u
                sp.wait_ge(*ev("zw_ready", t - 4))
                load(sp, cn[u][:], a["ctx"][rows(t), :], f"cn_ld{u}")

            tiles(sp, [(0, load_c)], ways=4)

            sp.wait_ge(*ev("gu_ready", NT - 1))
            sp.wait_ge(*ev("x2t_kept", NT - 1))

            def load_weights(e, i):
                sp.dma_start(w1[:, i:i + 1, :].rearrange("p a (c n) -> p (a c) n", c=2),
                             a["w1_t"][bass.ds(e, 1)].rearrange("a (c p) n -> p (a c) n", p=P))\
                  .then_inc(sem("w_ld"), 16)
                sp.dma_start(w2[:, i:i + 1, :].rearrange("p a (c n) -> p (a c) n", c=2),
                             a["w2_t"][bass.ds(e, 1)].rearrange("a (c p) n -> p (a c) n", p=IC))\
                  .then_inc(sem("w_ld"), 16)

            for i in range(WS):
                if i:
                    sp.wait_ge(sem("w_ld"), 32 * i)
                load_weights(i, i)
            sp.wait_ge(sem("tables"), 1)
            with sp.Fori(1, E // WS) as k:
                for i in range(WS):
                    e = WS * k + i
                    done = sp.value_load(first[0:1, bass.ds(e - WS + 1, 1)], min_val=0, max_val=BLOCKS)
                    sp.wait_ge(sem("w_ld"), 32 * e)
                    settle(sp)
                    sp.wait_ge(sem("y_ready"), done + CREDIT)
                    settle(sp)
                    load_weights(e, i)

            groups = sp.value_load(groups_n[0:1, 0:1], min_val=1, max_val=BLOCKS // 4)
            for u in range(4):
                sp.wait_ge(sem(f"y_out{u}"), (groups + 1) * 16)
                settle(sp)

            def load_e(k, u):
                t = 4 * k + u
                sp.wait_ge(*ev("ln3_sum", t - 4))
                load(sp, y6[u].rearrange("p k n -> p (k n)"),
                     yd.rearrange("(t k) n -> t (k n)", k=K)[rows(t), :], f"y6_ld{u}")

            def store_e(k, u):
                t = 4 * k + u
                sp.wait_ge(*ev("ln3_done", t))
                sp.dma_start(out[rows(t), :], ln["ln3", u][5][:]).then_inc(sem(f"out_st{u}"), 16)

            tiles(sp, [(0, load_e), (4, store_e)], ways=4)
            for u in range(4):
                sp.wait_ge(sem(f"out_st{u}"), 16 * (NT // 4 + 1))

        @block.tensor
        def _(pe):
            pe.wait_ge(sem("consts"), n_const)
            credit(pe, "s_half", "qk_ready", "v_ready", "s_ready", "pt_ready", "o_ready", "ot_ready", "r_ready",
                   "xbt_ready", "mxt_ready", "a_added", "zw_ready", "co_ready", "ct_ready",
                   "cr_ready", "x2t_ready", "lg_ready", "gu_ready", "rank_ready", "sd_ready",
                   "ux_ready", "h_ready", "ht_ready", "y_ready")
            for h in range(RH):
                m = pe.matmul(ps_ot[:, h, :], wht[:, h, :], wht[:, h, :], start=True, stop=True)
            m.then_inc(sem("m2_ready"), 1)
            pe.wait_ge(sem("m2_done"), 1)

            def project(k, u):
                t = 2 * k + u
                pe.wait_ge(*ld("xt_ld", k, u, 4))
                pe.wait_ge(*ev("q_evac", t - 1))
                pe.wait_ge(*ev("k_evac", t - 1))
                for m in range(4):
                    for c in range(2):
                        q = pe.matmul((ps_q if m < 2 else ps_k)[:, m % 2, :], wqkv[:, c, m * P:(m + 1) * P], xt[u][:, c, :, 0, :],
                                      start=c == 0, stop=c == 1)
                q.then_inc(sem("qk_ready"), 1)
                pe.wait_ge(*ev("v_evac", t - 1))
                for b in range(2):
                    for c in range(2):
                        x_b = xt[u][:, c, b, :, :].rearrange("p a s -> p (a s)")
                        q = pe.matmul(ps_v[:, b, :], x_b, wqkv[:, c, 2 * D:3 * D], start=c == 0, stop=c == 1)
                q.then_inc(sem("v_ready"), 1)

            def out_transpose(k, u):
                t = 2 * k + u
                pe.wait_ge(*ev("o_norm", t))
                for c in range(2):
                    q = pe.transpose(ps_ot[:, c, :], on[u][:, c * P:(c + 1) * P], ident[:])
                q.then_inc(sem("ot_ready"), 1)

            def prob_transpose(k, u):
                t = 2 * k + u
                pe.wait_ge(*ev("exp_done", t))
                for h in range(2):
                    pe.wait_ge(*half("pt_evac", t - 1, h))
                    for g in range(4):
                        g2 = 4 * h + g
                        q = pe.transpose(ps_pt[:, g2, :], prob[u][:, 2 * g2:2 * g2 + 2, :]
                                         .rearrange("p a s -> p (a s)"), ident[:])
                    q.then_inc(sem("pt_ready"), 1)

            def out_project(k, u):
                t = 2 * k + u
                pe.wait_ge(*ev("ot_evac", t))
                for c in range(2):
                    q = pe.matmul(ps_r, ot[u][:, c, :], wout[:, c, :], start=c == 0, stop=c == 1)
                q.then_inc(sem("r_ready"), 1)

            def scores(k, u):
                t = 2 * k + u
                pe.wait_ge(*ev("q_evac", t))
                pe.wait_ge(*ev("k_evac", t))
                pe.wait_ge(*ev("s_read", t - 1))
                for g2 in range(2):
                    if g2:
                        pe.wait_ge(*ev("s_half", t))
                    for m in range(2):
                        for b in range(2):
                            for g1 in range(2):
                                g, col = 2 * g2 + g1, 512 * g1 + 256 * g2 + 128 * m
                                q = pe.matmul(ps_s[b * S:(b + 1) * S, col:col + 2 * S],
                                              qt[u][32 * g:32 * g + 32, m, b * S:(b + 1) * S],
                                              kt[u][32 * g:32 * g + 32, m, :, b * S:(b + 1) * S],
                                              start=True, stop=True)
                    q.then_inc(sem("s_ready" if g2 else "s_half"), 1)

            def attend(k, u):
                t = 2 * k + u
                pe.wait_ge(*ev("pt_evac", t))
                pe.wait_ge(*ev("v_evac", t))
                pe.wait_ge(*ev("ln1_sum", t - 1))
                for g in range(8):
                    for b in range(2):
                        q = pe.matmul(ps_o[b * S:(b + 1) * S, 32 * g:32 * g + 32],
                                      pt[u][:, g, b * S:(b + 1) * S], vbd[u][:, b, 32 * g:32 * g + 32],
                                      start=True, stop=True)
                q.then_inc(sem("o_ready"), 1)

            tiles(pe, [(0, project), (2, out_transpose), (1, prob_transpose), (2, out_project),
                       (0, scores), (1, attend)])

            pe.wait_ge(*ev("ln1_sum", NT - 1))

            def b_transpose(k, u):
                t = 2 * k + u
                pe.wait_ge(*ev("xb_done", t))
                pe.wait_ge(*ev("xbt_evac", t - 1))
                for c in range(2):
                    q = pe.transpose(ps_bt[:, c, :], xb[u][:, c * P:(c + 1) * P], ident[:])
                q.then_inc(sem("xbt_ready"), 1)

            def b_mix(k, u):
                t = 2 * k + u
                pe.wait_ge(*ev("xbt_evac", t))
                pe.wait_ge(*ev("mxt_evac", t - 1))
                for h in range(RH):
                    q = pe.matmul(ps_bm[:, h, :], m2[:, h, :], slot(xtall, t)[:, h, :], start=True, stop=True)
                q.then_inc(sem("mxt_ready"), 1)

            def b_scores(k, u):
                t = 4 * k + u
                pe.wait_ge(*ev("mxt_evac", t))
                pe.wait_ge(*ld("cbt_ld", k, u))
                for h in range(RH):
                    q = pe.matmul(ps_a[:, h, :], cbt[u][:, h, :], mxt[u % 2][:, h, :], start=False, stop=False)
                q.then_inc(sem("a_added"), 1)

            def b_add_zero(start):
                for h in range(RH):
                    q = pe.matmul(ps_a[:, h, :], zeros[:, 0, 0:P], zeros[:, 0, 0:P], start=start, stop=not start)
                return q

            pe.wait_ge(sem("zeroed"), 4)
            b_add_zero(True)
            tiles(pe, [(0, two(b_transpose)), (1, two(b_mix)), (2, b_scores)], ways=4)
            b_add_zero(False).then_inc(sem("a_summed"), 1)
            pe.wait_ge(sem("adiag_done"), 2)
            for h in range(RH):
                q = pe.matmul(ps_ad[:, h, :], pair[:], adiag[:, h, :], start=True, stop=True)
            q.then_inc(sem("ad_ready"), 1)

            pe.wait_ge(sem("abd_done"), 2)

            def c_z_gate(k, u):
                t = 4 * k + u
                pe.wait_ge(*ld("cn_ld", k, u))
                pe.wait_ge(*ev("z_evac", t - 1))
                pe.wait_ge(*ev("w_evac", t - 1))
                for h in range(RH):
                    q = pe.matmul(ps_z[:, h, :], cn[u][:, h * P:(h + 1) * P], abd[:, h, :], start=True, stop=True)
                for m in range(2):
                    for c in range(2):
                        q = pe.matmul(ps_w[:, m, :], wg[:, c, m * P:(m + 1) * P], slot(xtall, t)[:, c, :],
                                      start=c == 0, stop=c == 1)
                q.then_inc(sem("zw_ready"), 1)

            def c_out(k, u):
                t = 2 * k + u
                pe.wait_ge(*ev("z_evac", t))
                pe.wait_ge(*ev("gn_done", t - 2))
                for h in range(RH):
                    q = pe.matmul(ps_co[u][:, h * P:(h + 1) * P], zt[u][:, h, :], wh[:, h, :], start=True, stop=True)
                q.then_inc(sem("co_ready"), 1)

            def c_transpose(k, u):
                t = 2 * k + u
                pe.wait_ge(*ev("gn_done", t))
                pe.wait_ge(*ev("yt_done", t - 1))
                for c in range(2):
                    q = pe.transpose(ps_ct[:, c, :], ln["gn", u][5][:, c * P:(c + 1) * P], ident[:])
                q.then_inc(sem("ct_ready"), 1)

            def c_project(k, u):
                t = 2 * k + u
                pe.wait_ge(*ev("gt_done", t))
                pe.wait_ge(*ev("ln2_sum", t - 1))
                for c in range(2):
                    q = pe.matmul(ps_cr, gt[u][:, c, :], wo[:, c, :], start=c == 0, stop=c == 1)
                q.then_inc(sem("cr_ready"), 1)

            def x2_transpose(k, u):
                t = 2 * k + u
                pe.wait_ge(*ev("ln2_done", t))
                pe.wait_ge(*ev("x2t_evac", t - 1))
                for c in range(2):
                    q = pe.transpose(ps_x2t[:, c, :], ln["ln2", u][5][:, c * P:(c + 1) * P], ident[:])
                q.then_inc(sem("x2t_ready"), 1)

            def router(k, u):
                t = 2 * k + u
                pe.wait_ge(*ev("x2t_evac", t))
                pe.wait_ge(*ev("lg_evac", t - 1))
                for c in range(2):
                    q = pe.matmul(ps_lg, x2t[u][:, c, :], wgate[:, c, :], start=c == 0, stop=c == 1)
                q.then_inc(sem("lg_ready"), 1)

            def ranks(k, u):
                t = 2 * k + u
                pe.wait_ge(*ev("hot_done", t))
                pe.wait_ge(*ev("rank_read", t - 1))
                for ps, w in ((ps_before, tri), (ps_total, ones)):
                    for j in range(K):
                        q = pe.matmul(ps, w[:], hot[u][:, j, :], start=j == 0, stop=j == K - 1)
                q.then_inc(sem("rank_ready"), 1)

            tiles(pe, [(8, two(ranks)), (7, two(router)), (6, two(x2_transpose)), (4, two(c_project)),
                       (3, two(c_transpose)), (0, c_z_gate), (1, two(c_out))], ways=4)

            pe.wait_ge(*ev("x2t_kept", NT - 1))
            pe.wait_ge(sem("cum_done"), 1)
            pe.transpose(ps_lg_t, scan[:, 1, :], ident[:]).then_inc(sem("cum_t_ready"), 1)
            pe.wait_ge(sem("before_b_done"), 1)
            pe.matmul(ps_exp, scan[0:E, 2, :], before_b, start=True, stop=True).then_inc(sem("experts_ready"), 1)

            def shared_up(k, u):
                t = 2 * k + u
                pe.wait_ge(*ev("sh_done", t - 2))
                for g, ps in enumerate((ps_g[u], ps_u[u])):
                    for m in range(SC):
                        for c in range(2):
                            col = g * SH + m * IC
                            q = pe.matmul(ps[:, m, :], sgu[:, c, col:col + IC], slot(xtall, t)[:, c, :],
                                          start=c == 0, stop=c == 1)
                q.then_inc(sem("gu_ready"), 1)

            def shared_down(k, u):
                t = 2 * k + u
                pe.wait_ge(*ev("sh_done", t))
                pe.wait_ge(*ev("xsh_done", t - 1))
                for m in range(SC):
                    q = pe.matmul(ps_sd, sh[u][:, m, :], sdn[:, m, :], start=m == 0, stop=m == SC - 1)
                q.then_inc(sem("sd_ready"), 1)

            tiles(pe, [(0, shared_up), (1, shared_down)])

            pe.wait_ge(sem("tables"), 1)

            def b_x_t(k, u):
                n = 4 * k + u
                pe.wait_ge(sem(f"ur_ld{u}"), 16 * (k + 1))
                pe.wait_ge(*ev("ux_evac", n - 2))
                for c in range(2):
                    q = pe.transpose(ps_ux[u % 2][:, c * P:(c + 1) * P], ur[:, u, c * P:(c + 1) * P], ident[:])
                q.then_inc(sem("ux_ready"), 1)

            def b_up(k, u, group):
                n = 4 * k + u
                e = expert_of(group, u)
                at = e & (WS - 1)
                pe.wait_ge(sem("w_ld"), 32 * e + 32)
                pe.wait_ge(*ev("ux_evac", n))
                pe.wait_ge(*ev("silu_done", n - 2))
                for c in range(2):
                    q = pe.matmul(ps_uh[u % 2][:, 0:I], uxt[:, 2 * (u % 2) + c, :],
                                  w1[:, bass.ds(at, 1), c * I:(c + 1) * I].rearrange("p a n -> p (a n)"),
                                  start=c == 0, stop=c == 1)
                q.then_inc(sem("h_ready"), 1)

            def b_h_t(k, u):
                n = 4 * k + u
                pe.wait_ge(*ev("silu_done", n))
                pe.wait_ge(*ev("ht_evac", n - 2))
                for m in range(2):
                    q = pe.transpose(ps_uht[u % 2][0:IC, m * P:(m + 1) * P], uh[:, u % 2, m * IC:(m + 1) * IC], ident[:])
                q.then_inc(sem("ht_ready"), 1)

            def b_down(k, u, group):
                n = 4 * k + u
                at = expert_of(group, u) & (WS - 1)
                pe.wait_ge(*ev("ht_evac", n))
                pe.wait_ge(*ev("y_evac", n - 2))
                for m in range(2):
                    q = pe.matmul(ps_uy[u % 2][:, 0:D], uht[:, 2 * (u % 2) + m, :],
                                  w2[:, bass.ds(at, 1), m * D:(m + 1) * D].rearrange("p a n -> p (a n)"),
                                  start=m == 0, stop=m == 1)
                q.then_inc(sem("y_ready"), 1)

            blocks(pe, [(8, b_down), (6, b_h_t), (3, b_x_t), (4, b_up)], (b_up, b_down))

        @block.scalar
        def _(act):
            act.preload_act_table(ACT.Exp)
            act.wait_ge(sem("consts"), n_const)
            credit(act, "q_evac", "exp_done", "pt_evac", "ot_evac", "xbt_evac", "z_evac", "w_evac", "yt_done",
                   "x2t_evac", "x2_kept", "lg_evac", "wexp_done", "th_done", "row_x_done",
                   "silu_done", "y_evac")
            act.activation(bqs[:], bqk[:, 0:2], ACT.Copy, scale=float(HD) ** -0.5).then_inc(sem("bqs_done"), 1)
            act.wait_ge(sem("bqs_done"), 1)
            act.wait_ge(sem("m2_ready"), 1)
            act.activation(m2[:], ps_ot, ACT.Copy).then_inc(sem("m2_done"), 1)

            def q_evac(k, u):
                t = 2 * k + u
                act.wait_ge(*ev("qk_ready", t))
                act.wait_ge(*ev("s_ready", t - 2))
                for m in range(2):
                    q = act.activation(qt[u][:, m, :], ps_q[:, m, :], ACT.Identity, bias=bqs[:, m:m + 1],
                                       scale=float(HD) ** -0.5)
                q.then_inc(sem("q_evac"), 1)

            def exps(k, u):
                t = 2 * k + u
                act.wait_ge(*ev("centred", t))
                act.activation(prob[u][:], prob[u][:], ACT.Exp).then_inc(sem("exp_done"), 1)

            def pt_evac(k, u):
                t = 2 * k + u
                act.wait_ge(*ev("o_ready", t - 2))
                for h in range(2):
                    act.wait_ge(*half("pt_ready", t, h))
                    act.activation(pt[u][:, 4 * h:4 * h + 4, :], ps_pt[:, 4 * h:4 * h + 4, :],
                                   ACT.Copy).then_inc(sem("pt_evac"), 1)

            def ot_evac(k, u):
                t = 2 * k + u
                act.wait_ge(*ev("ot_ready", t))
                act.wait_ge(*ev("r_ready", t - 2))
                for c in range(2):
                    q = act.activation(ot[u][:, c, :], ps_ot[:, c, :], ACT.Identity, bias=bv[:, c:c + 1])
                q.then_inc(sem("ot_evac"), 1)

            tiles(act, [(1, exps), (0, q_evac), (2, ot_evac), (1, pt_evac)])

            def xbt_evac(k, u):
                t = 2 * k + u
                act.wait_ge(*ev("xbt_ready", t))
                act.activation(slot(xtall, t), ps_bt, ACT.Copy).then_inc(sem("xbt_evac"), 1)

            tiles(act, [(0, xbt_evac)])

            def z_evac(k, u):
                t = 2 * k + u
                act.wait_ge(*ev("zw_ready", t))
                act.wait_ge(*ev("co_ready", t - 2))
                act.activation(zt[u][:], ps_z, ACT.Copy).then_inc(sem("z_evac"), 1)

            def w_evac(k, u):
                t = 4 * k + u
                act.wait_ge(*ev("zw_ready", t))
                act.wait_ge(*ev("gt_done", t - 4))
                act.activation(wt[u][:, :, :], ps_w, ACT.Relu).then_inc(sem("w_evac"), 1)

            def scale_shift(k, u):
                t = 2 * k + u
                act.wait_ge(*ev("ct_ready", t))
                act.wait_ge(*ev("gt_done", t - 2))
                for c in range(2):
                    q = act.activation(yt[u][:, c, :], ps_ct[:, c, :], ACT.Identity, bias=beta[:, c:c + 1],
                                       scale=gamma[:, c:c + 1])
                q.then_inc(sem("yt_done"), 1)

            def x2t_evac(k, u):
                t = 2 * k + u
                act.wait_ge(*ev("x2t_ready", t))
                act.wait_ge(*ev("lg_ready", t - 2))
                act.wait_ge(*ev("x2t_kept", t - 2))
                act.activation(x2t[u][:], ps_x2t, ACT.Copy).then_inc(sem("x2t_evac"), 1)

            def lg_evac(k, u):
                t = 2 * k + u
                act.wait_ge(*ev("lg_ready", t))
                act.wait_ge(*ev("topi_done", t - 2))
                act.activation(lg[u][:], ps_lg, ACT.Copy).then_inc(sem("lg_evac"), 1)

            def keep_x2(k, u):
                t = 2 * k + u
                act.wait_ge(*ev("ln2_done", t))
                act.activation(slot(xall, t), ln["ln2", u][5][:], ACT.Copy).then_inc(sem("x2_kept"), 1)

            def w_exp(k, u):
                t = 2 * k + u
                act.wait_ge(*ev("ntop_done", t))
                act.wait_ge(*ev("weights_done", t - 2))
                act.activation(wexp[u][:], top[u][:, 0:K], ACT.Exp, bias=ntop[u][:],
                               accum_out=wsum[u][:]).then_inc(sem("wexp_done"), 1)

            tiles(act, [(8, two(w_exp)), (7, two(lg_evac)), (6, two(x2t_evac)), (5, two(keep_x2)),
                        (3, two(scale_shift)), (0, two(z_evac)), (0, w_evac)], ways=4)

            def row_x(k, u):
                t = 2 * k + u
                act.wait_ge(*ev("x2_kept", t))
                act.wait_ge(*ev("scattered", t - 2))
                act.activation(row[u][:, 0:D], slot(xall, t), ACT.Copy).then_inc(sem("row_x_done"), 1)

            def th_g(k, u):
                t = 2 * k + u
                act.wait_ge(*ev("gu_ready", t))
                act.wait_ge(*ev("sg_done", t - 2))
                act.activation(th[u], ps_g[u], ACT.Tanh, scale=0.5).then_inc(sem("th_done"), 1)

            tiles(act, [(0, row_x), (0, th_g)])

            act.preload_act_table(ACT.Silu)
            act.wait_ge(sem("tables"), 1)

            act.wait_ge(*ev("scattered", NT - 1))
            act.wait_ge(*ev("sh_done", NT - 1))
            act.wait_ge(*ev("x2t_kept", NT - 1))

            def load_rows(k, u):
                n = 4 * k + u
                act.wait_ge(*ev("ux_ready", n - 4))
                act.wait_ge(*ev("uplace_done", n - 4))
                settle(act)
                act.dma_start(ur[:, u, :], listd[bass.ds(n * P, P), :]).then_inc(sem(f"ur_ld{u}"), 16)

            def silu(k, u):
                n = 4 * k + u
                act.wait_ge(*ev("h_ready", n))
                act.wait_ge(*ev("ht_ready", n - 2))
                act.activation(uh[:, u % 2, :], ps_uh[u % 2][:, 0:I], ACT.Silu).then_inc(sem("silu_done"), 1)

            def y_evac(k, u):
                n = 4 * k + u
                act.wait_ge(*ev("y_ready", n))
                act.wait_ge(sem(f"y_out{u}"), 16 * (k + 1))
                act.activation(uy[:, u, :], ps_uy[u % 2][:, 0:D], ACT.Copy).then_inc(sem("y_evac"), 1)

            blocks(act, [(8, y_evac), (4, silu), (0, load_rows)])

        @block.gpsimd
        def _(pool):
            pool.memset(eps[:, 0:1], LN_EPS).then_inc(sem("pool_const"), 1)
            pool.memset(eps[:, 1:2], GN_EPS).then_inc(sem("pool_const"), 1)
            pool.memset(mhalf[:], -0.5).then_inc(sem("pool_const"), 1)
            for h in range(4):
                pool.dma_start(junk[0:1, 12 + h:13 + h], a["ident"][0:1, h:h + 1]).then_inc(sem(f"y_out{h}"), 16)
            pool.wait_ge(sem("consts"), n_const)
            pool.wait_ge(sem("pool_const"), 3)
            credit(pool, "xnb_done", "rsum_done", "ln1_rstd", "gn_rstd", "ln2_rstd", "ln3_rstd", "scattered",
                   "ln1_var", "gn_var", "ln2_var", "ln3_var", "x2t_kept")

            def rstd(name, col, ways=2):
                def stage(k, u):
                    t = ways * k + u
                    _, _, mv, ve, rs, _ = ln[name, u]
                    pool.wait_ge(*ev(name + "_mv", t))
                    pool.tensor_tensor(ve[:], mv[:, 1:2], eps[:, col:col + 1], ALU.add).then_inc(sem(name + "_var"), 1)
                    pool.wait_ge(*ev(name + "_var", t))
                    pool.wait_ge(*ev(name + "_done", t - ways))
                    pool.tensor_tensor(rs[:], ve[:], mhalf[:], ALU.pow).then_inc(sem(name + "_rstd"), 1)
                return stage

            def add_bias(k, u):
                t = 2 * k + u
                pool.wait_ge(*ld("xn_ld", k, u))
                pool.wait_ge(*ev("ln1_sum", t - 2))
                pool.tensor_tensor(xnb[u][:], xn[u][:], bout[:], ALU.add).then_inc(sem("xnb_done"), 1)

            tiles(pool, [(0, add_bias), (2, rstd("ln1", 0))])

            def keep_x2t(k, u):
                t = 2 * k + u
                pool.wait_ge(*ev("x2t_evac", t))
                pool.tensor_copy(slot(xtall, t), x2t[u][:]).then_inc(sem("x2t_kept"), 1)

            tiles(pool, [(6, keep_x2t), (4, rstd("ln2", 0)), (1, rstd("gn", 1))])

            pool.wait_ge(sem("filled"), 16 * (2 * NT + 1))

            def scatter(k, u):
                t = 2 * k + u
                pool.wait_ge(*ev("row_x_done", t))
                pool.wait_ge(*ev("dest_done", t))
                settle(pool)
                for j in range(K):
                    pool.indirect_dma_start(listd, bass.IndirectOffsetOnAxis(ap=dest[u][:, j:j + 1], axis=0),
                                            row[u][:], None).then_inc(sem(f"scatter{u}"), 16)

            def scatter_end(k, u):
                pool.wait_ge(sem(f"scatter{u}"), 16 * K * (k + 1))
                pool.sem_inc(sem("scattered"), 1)

            tiles(pool, [(0, scatter), (1, scatter_end)])

            pool.wait_ge(sem("tables"), 1)

            def scatter_result(k, u):
                n = 4 * k + u
                pool.wait_ge(*ev("udest_done", n))
                pool.wait_ge(*ev("y_evac", n))
                settle(pool)
                pool.indirect_dma_start(yd, bass.IndirectOffsetOnAxis(ap=udest[u][:, 0:1], axis=0), uy[:, u, :], None,
                                        bounds_check=T * K - 1, oob_is_err=False).then_inc(sem(f"y_out{u}"), 16)

            blocks(pool, [(8, scatter_result)])

            tiles(pool, [(0, rstd("ln3", 0, 4))], ways=4)

        @block.vector
        def _(dve):
            dve.memset(zeros[:], 0.0).then_inc(sem("zeroed"), 1)
            dve.memset(abd[:], 0.0).then_inc(sem("zeroed"), 1)
            dve.memset(ones[:], 1.0).then_inc(sem("zeroed"), 1)
            dve.wait_ge(sem("consts"), n_const)
            credit(dve, "k_evac", "v_evac", "s_read", "max_done", "centred", "rinv_done", "o_norm", "ln1_sum",
                   "ln1_stat", "ln1_mv", "ln1_done", "mxt_evac", "gn_stat", "gn_mv", "gn_done", "gt_done",
                   "ln2_sum", "ln2_stat", "ln2_mv", "ln2_done", "top_done", "topi_done", "tope_done",
                   "ntop_done", "hot_done", "winv_done", "weights_done", "rank_read", "hot_s_done", "pick_done",
                   "destf_done", "dest_done", "sg_done", "sh_done", "xsh_done", "xb_done", "ux_evac", "ht_evac",
                   "udest_done", "uplace_done", "uplaces_done", "ln3_sum", "ln3_stat", "ln3_mv",
                   "ln3_done")
            dve.tensor_copy(tri[:], tri_f[:]).then_inc(sem("zeroed"), 1)
            for h in range(H):
                q = dve.scalar_tensor_tensor(bias[:, h, :], rel[:], slopes[:, h:h + 1], causal[:], ALU.mult, ALU.add)
            q.then_inc(sem("bias_done"), 1)
            dve.memset(count[:], 0.0).then_inc(sem("bias_done"), 1)
            dve.wait_ge(sem("bias_done"), 2)
            dve.wait_ge(sem("zeroed"), 4)

            def norm_stats(name, t, u, src, ways=2):
                _, st, mv, _, _, _ = ln[name, u]
                dve.bn_stats(st[:], src).then_inc(sem(name + "_stat"), 1)
                dve.wait_ge(*ev(name + "_stat", t))
                dve.wait_ge(*ev(name + "_done", t - ways))
                settle(dve)
                dve.bn_aggr(mv[:], st[:]).then_inc(sem(name + "_mv"), 1)

            def norm_apply(name, t, u, src, dst=None):
                _, _, mv, _, rs, y = ln[name, u]
                dve.wait_ge(*ev(name + "_rstd", t))
                dve.tensor_scalar(y[:] if dst is None else dst, src, mv[:, 0:1], rs[:, 0:1], ALU.subtract, ALU.mult)\
                   .then_inc(sem(name + "_done"), 1)

            def o_norm(k, u):
                t = 2 * k + u
                dve.wait_ge(*ev("rsum_done", t))
                dve.reciprocal(rinv[u][:], rsum[u][:]).then_inc(sem("rinv_done"), 1)
                dve.wait_ge(*ev("rinv_done", t))
                dve.wait_ge(*ev("o_ready", t))
                dve.wait_ge(*ev("ot_ready", t - 2))
                dve.tensor_tensor(on[u][:].rearrange("p (h d) -> p h d", h=H),
                                  ps_o.rearrange("p (h d) -> p h d", h=H),
                                  rinv[u][:].unsqueeze(2).to_broadcast([P, H, HD]), ALU.mult)\
                   .then_inc(sem("o_norm"), 1)

            def kv_evac(k, u):
                t = 2 * k + u
                dve.wait_ge(*ev("qk_ready", t))
                dve.wait_ge(*ev("s_ready", t - 2))
                for m in range(2):
                    for par in range(2):
                        q = dve.tensor_scalar(kt[u][:, m, par, :], ps_k[:, m, :], bqk[:, 2 + m:3 + m],
                                              kpar[:, par:par + 1], ALU.add, ALU.mult)
                q.then_inc(sem("k_evac"), 1)
                dve.wait_ge(*ev("v_ready", t))
                dve.wait_ge(*ev("o_ready", t - 2))
                dve.tensor_tensor(vbd[u][:], ps_v, vpar[:].unsqueeze(1).to_broadcast([P, 2, D]), ALU.mult)\
                   .then_inc(sem("v_evac"), 1)

            def residual1(k, u):
                t = 2 * k + u
                r = ln["ln1", u][0]
                dve.wait_ge(*ev("r_ready", t))
                dve.wait_ge(*ev("xnb_done", t))
                dve.tensor_tensor(r[:], ps_r, xnb[u][:], ALU.add).then_inc(sem("ln1_sum"), 1)
                dve.wait_ge(*ev("ln1_sum", t))
                norm_stats("ln1", t, u, r[:])

            def softmax(k, u):
                t = 2 * k + u
                dve.wait_ge(*ev("s_ready", t))
                dve.wait_ge(*ev("pt_ready", t - 2))
                dve.tensor_tensor(prob[u][:], ps_s.rearrange("p (h s) -> p h s", h=H), bias[:], ALU.add)\
                   .then_inc(sem("s_read"), 1)
                dve.wait_ge(*ev("s_read", t))
                dve.tensor_reduce(mx[u][:], prob[u][:], AX, ALU.max).then_inc(sem("max_done"), 1)
                dve.wait_ge(*ev("max_done", t))
                dve.tensor_tensor(prob[u][:], prob[u][:], mx[u][:].unsqueeze(2).to_broadcast([P, H, S]),
                                  ALU.subtract).then_inc(sem("centred"), 1)

            def row_sums(k, u):
                t = 2 * k + u
                dve.wait_ge(*ev("exp_done", t))
                dve.tensor_reduce(rsum[u][:], prob[u][:], AX, ALU.add).then_inc(sem("rsum_done"), 1)

            def apply1(k, u):
                t = 2 * k + u
                norm_apply("ln1", t, u, ln["ln1", u][0][:], slot(xall, t))

            tiles(dve, [(2, o_norm), (0, kv_evac), (1, row_sums), (2, residual1), (0, softmax), (2, apply1)])

            def copy_x1(k, u):
                t = 2 * k + u
                dve.wait_ge(*ev("ln1_done", t))
                dve.wait_ge(*ev("xbt_ready", t - 2))
                dve.tensor_copy(xb[u][:], slot(xall, t)).then_inc(sem("xb_done"), 1)

            def mxt_evac(k, u):
                t = 2 * k + u
                dve.wait_ge(*ev("mxt_ready", t))
                dve.wait_ge(*ev("a_added", t - 2))
                dve.tensor_copy(mxt[u][:], ps_bm).then_inc(sem("mxt_evac"), 1)

            tiles(dve, [(0, copy_x1), (2, mxt_evac)])
            dve.wait_ge(sem("a_summed"), 1)
            for b in range(2):
                half_ = slice(b * S, (b + 1) * S)
                dve.tensor_copy(adiag[half_, :, :], ps_a[half_, :, half_]).then_inc(sem("adiag_done"), 1)
            dve.wait_ge(sem("ad_ready"), 1)
            dve.tensor_tensor(araw[:], ps_ad, decay[:], ALU.mult).then_inc(sem("araw_done"), 1)
            dve.wait_ge(sem("araw_done"), 1)
            dve.tensor_scalar(afloor[:], araw[:], 1.0, None, ALU.max).then_inc(sem("araw_done"), 1)
            dve.wait_ge(sem("araw_done"), 2)
            for b in range(2):
                half_ = slice(b * S, (b + 1) * S)
                dve.scalar_tensor_tensor(abd[half_, :, half_], araw[half_, :, :], -1.0, afloor[half_, :, :],
                                         ALU.mult, ALU.max)\
                   .then_inc(sem("abd_done"), 1)

            def group_norm(k, u):
                t = 2 * k + u
                dve.wait_ge(*ev("co_ready", t))
                norm_stats("gn", t, u, ps_co[u])

            def group_apply(k, u):
                t = 2 * k + u
                dve.wait_ge(*ev("ct_ready", t - 2))
                norm_apply("gn", t, u, ps_co[u])

            def gated(k, u):
                t = 4 * k + u
                dve.wait_ge(*ev("yt_done", t))
                dve.wait_ge(*ev("w_evac", t))
                dve.wait_ge(*ev("cr_ready", t - 2))
                dve.tensor_tensor(gt[u % 2][:], yt[u % 2][:], wt[u][:, :, :], ALU.mult).then_inc(sem("gt_done"), 1)

            def residual2(k, u):
                t = 2 * k + u
                r = ln["ln2", u][0]
                dve.wait_ge(*ev("cr_ready", t))
                dve.wait_ge(*ev("ln2_done", t - 2))
                dve.tensor_tensor(r[:], ps_cr, slot(xall, t), ALU.add).then_inc(sem("ln2_sum"), 1)
                dve.wait_ge(*ev("ln2_sum", t))
                norm_stats("ln2", t, u, r[:])

            def apply2(k, u):
                t = 2 * k + u
                dve.wait_ge(*ev("x2_kept", t - 2))
                dve.wait_ge(*ev("x2t_ready", t - 2))
                norm_apply("ln2", t, u, ln["ln2", u][0][:])

            def top6(k, u):
                t = 2 * k + u
                dve.wait_ge(*ev("lg_evac", t))
                dve.wait_ge(*ev("wexp_done", t - 2))
                settle(dve)
                dve.max(top[u][:], lg[u][:]).then_inc(sem("top_done"), 1)
                dve.wait_ge(*ev("top_done", t))
                settle(dve)
                dve.max_index(topi[u][:], top[u][:], lg[u][:]).then_inc(sem("topi_done"), 1)
                dve.tensor_scalar(ntop[u][:], top[u][:, 0:1], -1.0, None, ALU.mult).then_inc(sem("ntop_done"), 1)
                dve.wait_ge(*ev("topi_done", t))
                dve.tensor_copy(slot(tope, t), topi[u][:, 0:K]).then_inc(sem("tope_done"), 1)
                dve.wait_ge(*ev("tope_done", t))
                dve.wait_ge(*ev("rank_ready", t - 2))
                dve.tensor_tensor(hot[u][:], iota_e[:].unsqueeze(1).to_broadcast([P, K, E]),
                                  slot(tope, t).unsqueeze(2).to_broadcast([P, K, E]), ALU.is_equal)\
                   .then_inc(sem("hot_done"), 1)

            def gate_weights(k, u):
                t = 2 * k + u
                dve.wait_ge(*ev("wexp_done", t))
                dve.reciprocal(winv[u][:], wsum[u][:]).then_inc(sem("winv_done"), 1)
                dve.wait_ge(*ev("winv_done", t))
                dve.tensor_scalar(weights[:, bass.ds(t, 1), :].rearrange("p a k -> p (a k)"), wexp[u][:],
                                  winv[u][:, 0:1], None, ALU.mult).then_inc(sem("weights_done"), 1)

            def token_ranks(k, u):
                t = 2 * k + u
                dve.wait_ge(*ev("rank_ready", t))
                dve.wait_ge(*ev("rank_read", t - 1))
                dve.tensor_tensor(slot(rank, t), ps_before, count[:], ALU.add)
                dve.tensor_tensor(count[:], ps_total, count[:], ALU.add).then_inc(sem("rank_read"), 1)

            tiles(dve, [(8, two(token_ranks)), (5, two(apply2)), (2, two(group_apply)), (7, two(top6)),
                        (8, two(gate_weights)), (4, two(residual2)), (3, gated), (1, two(group_norm))], ways=4)

            dve.wait_ge(*ev("rank_read", NT - 1))
            steps = [0]

            def done(q):
                steps[0] += 1
                q.then_inc(sem("tab"), 1)
                dve.wait_ge(sem("tab"), steps[0])

            done(dve.memset(scan[:, 2, :], 1.0))
            done(dve.memset(start[:, 0:1], 0.0))
            done(dve.memset(first[:, 0:1], 0))
            done(dve.tensor_scalar(blocks_i[:, 0, :], count[:], float(P - 1), None, ALU.add))
            done(dve.tensor_scalar(blocks_i[:, 1, :], blocks_i[:, 0, :], P.bit_length() - 1, None, ALU.arith_shift_right))
            done(dve.tensor_copy(scan[:, 0, :], blocks_i[:, 1, :]))
            dve.tensor_tensor_scan(scan[:, 1, :], scan[:, 2, :], scan[:, 0, :], 0.0, ALU.mult, ALU.add)\
               .then_inc(sem("cum_done"), 1)
            dve.wait_ge(sem("cum_done"), 1)
            done(dve.tensor_scalar(start[:, 1:E], scan[:, 1, 0:E - 1], float(P), None, ALU.mult))
            done(dve.tensor_copy(first[:, 1:E + 1], scan[0:1, 1, :]))
            done(dve.tensor_scalar(quarter[:, 0:1], scan[0:1, 1, E - 1:E], 3.0, None, ALU.add))
            done(dve.tensor_scalar(groups_n[:], quarter[:, 0:1], 2, None, ALU.arith_shift_right))
            done(dve.tensor_scalar(looped_n[:], groups_n[:], -2.0, None, ALU.add))
            dve.wait_ge(sem("cum_t_ready"), 1)
            done(dve.tensor_copy(cum_t[:], ps_lg_t[:, 0:1]))
            dve.tensor_scalar(before_b, iota_b[:], cum_t[:, 0:1], None, ALU.is_ge).then_inc(sem("before_b_done"), 1)
            dve.wait_ge(sem("experts_ready"), 1)
            done(dve.tensor_scalar(of_block[:], ps_exp[0:1, :], float(E - 1), None, ALU.min))
            of_group = of_block[:].rearrange("p (g f) -> p f g", f=4)
            done(dve.tensor_copy(packed_f[:], of_group[:, 3, :]))
            for f in (2, 1, 0):
                done(dve.scalar_tensor_tensor(packed_f[:], packed_f[:], float(E), of_group[:, f, :],
                                              ALU.mult, ALU.add))
            done(dve.tensor_copy(packed[:], packed_f[:]))
            dve.sem_inc(sem("tables"), 1)

            def destinations(k, u):
                t = 2 * k + u
                dve.wait_ge(*ev("pick_done", t - 1))
                dve.tensor_tensor(place_s[:], slot(rank, t), start[:], ALU.add)
                dve.tensor_tensor(hot_s, iota_e[:].unsqueeze(1).to_broadcast([P, K, E]),
                                  slot(tope, t).unsqueeze(2).to_broadcast([P, K, E]), ALU.is_equal)\
                   .then_inc(sem("hot_s_done"), 1)
                dve.wait_ge(*ev("hot_s_done", t))
                dve.wait_ge(*ev("destf_done", t - 1))
                dve.tensor_tensor(pick, hot_s, place_s[:].unsqueeze(1).to_broadcast([P, K, E]), ALU.mult)\
                   .then_inc(sem("pick_done"), 1)
                dve.wait_ge(*ev("pick_done", t))
                dve.wait_ge(*ev("dest_done", t - 1))
                dve.tensor_reduce(destf[:], pick, AX, ALU.add).then_inc(sem("destf_done"), 1)
                dve.wait_ge(*ev("destf_done", t))
                dve.wait_ge(*ev("scattered", t - 2))
                dve.tensor_copy(dest[u][:], destf[:])
                dve.tensor_copy(row[u][:, D:D + K], slot(tope, t))
                dve.tensor_copy(row[u][:, D + K:ROW], slot(places, t)).then_inc(sem("dest_done"), 1)

            def shared_gate(k, u):
                t = 2 * k + u
                dve.wait_ge(*ev("th_done", t))
                dve.wait_ge(*ev("sh_done", t - 2))
                dve.scalar_tensor_tensor(sg[u], th[u], 1.0, ps_g[u], ALU.add, ALU.mult).then_inc(sem("sg_done"), 1)
                dve.wait_ge(*ev("sg_done", t))
                dve.wait_ge(*ev("sd_ready", t - 2))
                dve.scalar_tensor_tensor(sh[u], sg[u], 0.5, ps_u[u], ALU.mult, ALU.mult).then_inc(sem("sh_done"), 1)

            def add_shared(k, u):
                t = 2 * k + u
                dve.wait_ge(*ev("sd_ready", t))
                dve.wait_ge(*ev("row_x_done", t))
                dve.tensor_tensor(slot(xall, t), ps_sd, slot(xall, t), ALU.add).then_inc(sem("xsh_done"), 1)

            tiles(dve, [(0, destinations), (0, shared_gate), (1, add_shared)])

            dve.wait_ge(*ev("x2t_kept", NT - 1))

            def place_mul(k, u, group):
                n = 4 * k + u
                e = expert_of(group, u)
                dve.wait_ge(sem(f"ur_ld{u}"), 16 * (k + 1))
                dve.wait_ge(*ev("uplaces_done", n - 1))
                dve.scalar_tensor_tensor(uplace[:], ur[:, u, D:D + K], iota_e[:, bass.ds(e, 1)],
                                         ur[:, u, D + K:ROW], ALU.is_equal, ALU.mult).then_inc(sem("uplace_done"), 1)

            def place_sum(k, u):
                n = 4 * k + u
                dve.wait_ge(*ev("uplace_done", n))
                dve.wait_ge(*ev("udest_done", n - 4))
                dve.tensor_reduce(uplace_s[u][:], uplace[:], AX, ALU.add).then_inc(sem("uplaces_done"), 1)

            def place_int(k, u):
                n = 4 * k + u
                dve.wait_ge(*ev("uplaces_done", n))
                dve.wait_ge(sem(f"y_out{u}"), 16 * (k + 1))
                dve.tensor_scalar(udest[u][:], uplace_s[u][:], float(NOWHERE), None, ALU.add)\
                   .then_inc(sem("udest_done"), 1)

            def ux_evac(k, u):
                n = 4 * k + u
                dve.wait_ge(*ev("ux_ready", n))
                dve.wait_ge(*ev("h_ready", n - 2))
                dve.tensor_copy(uxt[:, 2 * (u % 2):2 * (u % 2) + 2, :],
                                ps_ux[u % 2][:, 0:D].rearrange("p (c n) -> p c n", c=2)).then_inc(sem("ux_evac"), 1)

            def ht_evac(k, u):
                n = 4 * k + u
                dve.wait_ge(*ev("ht_ready", n))
                dve.wait_ge(*ev("y_ready", n - 2))
                dve.tensor_copy(uht[:, 2 * (u % 2):2 * (u % 2) + 2, :],
                                ps_uht[u % 2][0:IC, 0:D].rearrange("p (c n) -> p c n", c=2)).then_inc(sem("ht_evac"), 1)

            blocks(dve, [(6, ht_evac), (4, place_mul), (3, ux_evac), (4, place_sum), (7, place_int)], (place_mul,))

            def combine(k, u):
                if u % 2:
                    return
                pair_ = [(4 * k + u + v, u + v, ln["ln3", u + v][0]) for v in range(2)]
                for j in range(K):
                    for v, (t, b, r) in enumerate(pair_):
                        if j == 0:
                            dve.wait_ge(*ld("y6_ld", k, b))
                            dve.wait_ge(*ev("ln3_done", t - 4))
                        else:
                            dve.wait_ge(sem(f"e_chain{v}"), (K - 1) * (2 * k + u // 2) + j)
                        dve.scalar_tensor_tensor(r[:], y6[b][:, j, :], weights[:, bass.ds(t, 1), j:j + 1]
                                                 .rearrange("p a k -> p (a k)"), r[:] if j else slot(xall, t),
                                                 ALU.mult, ALU.add)\
                           .then_inc(sem(f"e_chain{v}" if j < K - 1 else "ln3_sum"), 1)
                for v, (t, b, r) in enumerate(pair_):
                    dve.wait_ge(*ev("ln3_sum", t))
                    norm_stats("ln3", t, u + v, r[:], 4)

            def apply3(k, u):
                t = 4 * k + u
                dve.wait_ge(*stored("out_st", k, u))
                norm_apply("ln3", t, u, ln["ln3", u][0][:])

            tiles(dve, [(0, combine), (2, apply3)], ways=4)


def _shape_constants():
    p = np.arange(P)
    q, k = p[:, None] % S, np.arange(S)[None, :]
    seen = k <= q
    gam = (np.float32(1) - np.float32(2) ** (-5 - np.arange(RH, dtype=np.float32))).astype(np.float32)
    expo = (k - np.arange(S)[:, None]).astype(np.float32)
    dec = np.where(expo[None] <= 0, gam[:, None, None] ** expo[None], 0).astype(np.float32)
    dec = dec / np.sqrt(dec.sum(-1))[:, None, :] / np.sqrt(np.float32(D // RH))
    dec_t = np.tile(dec.transpose(2, 0, 1), (2, 1, 1))
    tok = np.arange(NT)[None, :, None] * P + p[:, None, None]
    return {
        "ident": np.eye(P),
        "k_parity": np.stack([(p // HD) % 2 == 0, (p // HD) % 2 == 1], 1),
        "v_parity": (np.arange(D)[None, :] // HD) % 2 == (p // S)[:, None],
        "rel": np.where(seen, k - q, 0),
        "causal": np.where(seen, 0.0, -1e9),
        "decay_t": dec_t,
        "pair": p[:, None] % S == p[None, :] % S,
        "tri": p[:, None] < p[None, :],
        "iota_b": np.broadcast_to(np.arange(BW), (E, BW)),
        "iota_e": np.broadcast_to(np.arange(E), (P, E)),
        "places": tok * K + np.arange(K) - NOWHERE,
    }


def kernel(x, ctx_2048, L0_attn_qkv_w, L0_attn_qkv_b, L0_attn_out_w, L0_attn_out_b, L0_attn_alibi_slopes,
           L0_xattn_Wh, L0_xattn_wg_w, L0_xattn_wo_w, L0_xattn_gn_gamma, L0_xattn_gn_beta, L0_ffn_gate_w,
           L0_ffn_experts_w1, L0_ffn_experts_w2, L0_ffn_shared_gate_up, L0_ffn_shared_down):
    import concourse.bacc as bacc
    from concourse.bass_utils import run_bass_kernel_spmd

    rows = np.asarray(x).reshape(T, D)
    ctx = np.asarray(ctx_2048).reshape(T, D)
    qkv_b = np.asarray(L0_attn_qkv_b)
    dims = (np.array(ORDER)[:, None] * HD + np.arange(HD)).reshape(-1)
    qkv_rows = np.concatenate([np.arange(2 * D), 2 * D + dims])
    arrays = {
        "x": rows, "x_t": rows.T, "ctx": ctx, "ctx_t": ctx.T,
        "wqkv_t": np.asarray(L0_attn_qkv_w)[qkv_rows].T,
        "b_qk": qkv_b[:2 * D].reshape(4, P).T, "b_v": qkv_b[2 * D + dims].reshape(2, P).T,
        "slopes": np.broadcast_to(np.asarray(L0_attn_alibi_slopes)[np.array(ORDER)], (P, H)),
        "wout_t": np.asarray(L0_attn_out_w).T[dims],
        "b_out": np.broadcast_to(np.asarray(L0_attn_out_b), (P, D)),
        "wh": np.asarray(L0_xattn_Wh), "wh_t": np.asarray(L0_xattn_Wh).transpose(0, 2, 1),
        "wg": np.asarray(L0_xattn_wg_w), "wo": np.asarray(L0_xattn_wo_w),
        "gamma": np.asarray(L0_xattn_gn_gamma).reshape(2, P).T,
        "beta": np.asarray(L0_xattn_gn_beta).reshape(2, P).T,
        "gate_t": np.asarray(L0_ffn_gate_w).T,
        "w1_t": np.asarray(L0_ffn_experts_w1).transpose(0, 2, 1),
        "w2_t": np.asarray(L0_ffn_experts_w2).transpose(0, 2, 1),
        "sgu_t": np.asarray(L0_ffn_shared_gate_up).T,
        "sdn_t": np.asarray(L0_ffn_shared_down).T,
    }
    arrays = {n: np.ascontiguousarray(v) for n, v in arrays.items()}
    arrays.update({n: np.ascontiguousarray(v, dtype=np.float32) for n, v in _shape_constants().items()})
    nc = bacc.Bacc("TRN2", target_bir_lowering=False, num_devices=1)
    aps = {n: nc.dram_tensor("in_" + n, v.shape, F32, kind="ExternalInput").ap() for n, v in arrays.items()}
    out = nc.dram_tensor("out_rows", (T, D), F32, kind="ExternalOutput").ap()
    decoder_layer(nc, aps, out)
    r = run_bass_kernel_spmd(nc, [{"in_" + n: v for n, v in arrays.items()}], core_ids=[0])
    return r.results[0]["out_rows"].reshape(B, S, D)
```

```python
from contextlib import ExitStack

import numpy as np

import concourse.bass as bass
from concourse import mybir

F32 = mybir.dt.float32
BF16 = mybir.dt.bfloat16
I32 = mybir.dt.int32
U32 = mybir.dt.uint32
ACT = mybir.ActivationFunctionType
ALU = mybir.AluOpType
AX = mybir.AxisListType.X

P = 128
B, S, D = 64, 64, 256
T = B * S
NT = T // P
H, HD = 16, 16
RH = 2
E, I, K = 64, 176, 6
IC = I // 2
SH = 2 * I
SC = SH // IC
BLOCKS = T * K // P + E
FILL = 4
BW = BLOCKS + 8
WS = 4
ROW = D + 2 * K
NOWHERE = 1 << 20
ORDER = [8 * m + 2 * (2 * g2 + g1) + par for g1 in range(2) for g2 in range(2) for m in range(2) for par in range(2)]
LN_EPS, GN_EPS = 1e-5, 1e-3

PER_TILE = {"pt_ready": 2, "pt_evac": 2}
CREDIT = 6


def decoder_layer(nc, a, out):
    listd = nc.dram_tensor("expert_rows", ((BLOCKS + 2 * FILL) * P, ROW), F32, kind="Internal").ap()
    yd = nc.dram_tensor("expert_results", (T * K, D), F32, kind="Internal").ap()

    with ExitStack() as ctx:
        def sb(name, shape, dt=F32):
            return ctx.enter_context(nc.sbuf_tensor(name, shape, dt))

        sems = {}

        def sem(name):
            if name not in sems:
                sems[name] = ctx.enter_context(nc.semaphore(name))
            return sems[name]

        def ev(name, t):
            n = PER_TILE.get(name, 1)
            return sem(name), (t + 1 + CREDIT) * n

        def half(name, t, h):
            return sem(name), (t + CREDIT) * 2 + h + 1

        def credit(eng, *names):
            for name in names:
                eng.sem_inc(sem(name), CREDIT * PER_TILE.get(name, 1))

        def tiles(eng, lags, ways=2):
            deep = -(-max(l for l, _ in lags) // ways) * ways
            for s in range(deep):
                for l, f in lags:
                    if s - l >= 0:
                        f((s - l) // ways, (s - l) % ways)
            with eng.Fori(0, (NT - deep) // ways) as i:
                for r in range(ways):
                    for l, f in lags:
                        f(i + (deep + r - l) // ways, (r - l) % ways)
            for s in range(NT, NT + deep):
                for l, f in lags:
                    if 0 <= s - l < NT:
                        f((s - l) // ways, (s - l) % ways)

        def expert_of(group, u):
            return (group & (E - 1)) + ((group >> (4 + 2 * u)) & 3) if u else group & (E - 1)

        def place_before(group, u):
            return (group >> (12 + 2 * u)) & (WS - 1)

        def blocks(eng, lags, looked_up=()):
            deep = 8
            looped = eng.value_load(looped_n[0:1, 0:1], min_val=T * K // P // 4 - deep // 4, max_val=BLOCKS // 4 - deep // 4)
            def group_of(k):
                return eng.value_load(packed[0:1, bass.ds(k, 1)], min_val=0, max_val=(1 << 20) - 1)

            def run(k_of, wanted, known=(), then=None):
                known = list(known)
                for s in range(4):
                    for l, f in lags:
                        if wanted(s - l):
                            k, u = k_of(s - l), (s - l) % 4
                            if f in looked_up:
                                if not known:
                                    known.append(group_of(k + l // 4 - 1))
                                f(k, u, known[0])
                            else:
                                f(k, u)
                            if then is not None:
                                then()
                                then = None

            for g in range(deep // 4):
                run(lambda x: (x + 4 * g) // 4, lambda x: x + 4 * g >= 0)
            if looked_up:
                ahead = eng.alloc_register()
                eng.reg_load(ahead, packed[0:1, 1:2])
            with eng.Fori(0, looped) as i:
                if looked_up:
                    group = eng.snap(ahead, min_val=0, max_val=(1 << 20) - 1)
                    run(lambda x: i + (deep + x) // 4, lambda x: True, [group],
                        lambda: eng.reg_load(ahead, packed[0:1, bass.ds(i + 2, 1)]))
                else:
                    run(lambda x: i + (deep + x) // 4, lambda x: True)
            for g in range(deep // 4):
                run(lambda x: looped + (deep + x + 4 * g) // 4, lambda x: x + 4 * g < 0)

        consts = {}

        def const(name, src, shape, dt=F32):
            consts[name] = (sb("c_" + name, shape, dt), src)
            return consts[name][0]

        first_consts = ("ident", "wht", "wqkv", "bqk", "bv", "kpar", "vpar", "rel", "causal", "slopes", "wout", "bout",
                        "tri_f")

        kc = "(c p) n -> p c n"
        ident = const("ident", a["ident"], [P, P])
        wqkv = const("wqkv", a["wqkv_t"].rearrange(kc, p=P), [P, 2, 3 * D])
        bqk = const("bqk", a["b_qk"], [P, 4])
        bv = const("bv", a["b_v"], [P, 2])
        kpar = const("kpar", a["k_parity"], [P, 2])
        vpar = const("vpar", a["v_parity"], [P, D])
        rel = const("rel", a["rel"], [P, S])
        causal = const("causal", a["causal"], [P, S])
        slopes = const("slopes", a["slopes"], [P, H])
        wout = const("wout", a["wout_t"].rearrange(kc, p=P), [P, 2, D])
        bout = const("bout", a["b_out"], [P, D])
        wht = const("wht", a["wh_t"].rearrange("h e d -> e h d"), [P, RH, P])
        wh = const("wh", a["wh"].rearrange("h d e -> d h e"), [P, RH, P])
        decay = const("decay", a["decay_t"], [P, RH, S])
        wg = const("wg", a["wg"].rearrange(kc, p=P), [P, 2, D])
        wo = const("wo", a["wo"].rearrange(kc, p=P), [P, 2, D])
        gamma = const("gamma", a["gamma"], [P, 2])
        beta = const("beta", a["beta"], [P, 2])
        wgate = const("wgate", a["gate_t"].rearrange(kc, p=P), [P, 2, E])
        pair = const("pair", a["pair"], [P, P])
        tri_f = const("tri_f", a["tri"], [P, P])
        iota_e = const("iota_e", a["iota_e"], [P, E + 4])
        iota_b = const("iota_b", a["iota_b"], [E, BW])
        places = const("places", a["places"], [P, NT, K])
        sgu = const("sgu", a["sgu_t"].rearrange(kc, p=P), [P, 2, 2 * SH])
        sdn = const("sdn", a["sdn_t"].rearrange("(c p) n -> p c n", p=IC), [IC, SC, D])
        tri = sb("tri", [P, P], BF16)
        ones = sb("ones", [P, P], BF16)
        bqs = sb("bqs", [P, 2])
        bkp = sb("bkp", [P, 2])
        bias = sb("bias", [P, H, S])
        m2 = sb("m2", [P, RH, P])
        eps = sb("eps", [P, 2])
        mhalf = sb("mhalf", [P, 1])
        minus = sb("minus", [P, 1])
        zeros = sb("zeros", [P, FILL, ROW])
        junk = sb("junk", [1, 16])

        xall = sb("xall", [P, NT, D])
        xtall = sb("xtall", [P, NT, 2, P])

        xt = [sb(f"xt{u}", [P, 2, 2, 2, S]) for u in range(2)]
        xn = [sb(f"xn{u}", [P, D]) for u in range(2)]
        xnb = [sb(f"xnb{u}", [P, D]) for u in range(2)]
        qt = [sb(f"qt{u}", [P, 2, P]) for u in range(2)]
        kt = [sb(f"kt{u}", [P, 2, 2, P]) for u in range(2)]
        vbd = [sb(f"vbd{u}", [P, 2, D]) for u in range(2)]
        prob = [sb(f"prob{u}", [P, H, S]) for u in range(2)]
        mx = [sb(f"mx{u}", [P, H]) for u in range(2)]
        rsum = [sb(f"rsum{u}", [P, H]) for u in range(2)]
        rinv = [sb(f"rinv{u}", [P, H]) for u in range(2)]
        pt = [sb(f"pt{u}", [P, H // 2, P]) for u in range(2)]
        on = [sb(f"on{u}", [P, D]) for u in range(2)]
        ot = [sb(f"ot{u}", [P, 2, P]) for u in range(2)]
        ln = {}
        for name in ("ln1", "gn", "ln2", "ln3"):
            for u in range(2):
                ln[name, u] = (sb(f"{name}_r{u}", [P, D]), sb(f"{name}_st{u}", [P, 6]), sb(f"{name}_mv{u}", [P, 2]),
                               sb(f"{name}_ve{u}", [P, 1]), sb(f"{name}_rs{u}", [P, 1]), sb(f"{name}_y{u}", [P, D]))
        shift = {(name, u): (sb(f"{name}_nm{u}", [P, 1]), sb(f"{name}_sh{u}", [P, 1]))
                 for name in ("ln1", "gn", "ln2", "ln3") for u in range(2)}
        for u in range(2):
            ln["ln3", 2 + u] = ln["gn", u]
            shift["ln3", 2 + u] = shift["gn", u]
        xb = [sb(f"xb{u}", [P, D]) for u in range(2)]
        cbt = [sb(f"cbt{u}", [P, 2, P]) for u in range(4)]
        mxt = [sb(f"mxt{u}", [P, RH, P]) for u in range(2)]
        adiag = sb("adiag", [P, RH, S])
        araw = sb("araw", [P, RH, S])
        afloor = sb("afloor", [P, RH, S])
        abd = sb("abd", [P, RH, P])
        cn = [sb(f"cn{u}", [P, D]) for u in range(4)]
        zt = [sb(f"zt{u}", [P, RH, P]) for u in range(2)]
        wt = [sb(f"wt{u}", [P, 2, P]) for u in range(2)] + [kt[0][:, :, par, :] for par in range(2)]
        yt = [sb(f"yt{u}", [P, 2, P]) for u in range(2)]
        gt = [sb(f"gt{u}", [P, 2, P]) for u in range(2)]
        x2t = [sb(f"x2t{u}", [P, 2, P]) for u in range(2)]
        lg = [sb(f"lg{u}", [P, E]) for u in range(2)]
        top = [sb(f"top{u}", [P, 8]) for u in range(2)]
        topi = [sb(f"topi{u}", [P, 8], U32) for u in range(2)]
        tope = sb("tope", [P, NT, K])
        ntop = [sb(f"ntop{u}", [P, 1]) for u in range(2)]
        wexp = [sb(f"wexp{u}", [P, K]) for u in range(2)]
        wsum = [sb(f"wsum{u}", [P, 1]) for u in range(2)]
        winv = [sb(f"winv{u}", [P, 1]) for u in range(2)]
        weights = sb("weights", [P, NT, K])
        hot = [sb(f"hot{u}", [P, K, E], BF16) for u in range(2)]
        rank = sb("rank", [P, NT, E])
        count = sb("count", [P, E])
        start = sb("start", [P, E])
        scan = sb("scan", [P, 3, E])
        hot_s, pick = (kt[u][:].rearrange("p m par n -> p (m par n)")[:, 0:K * E]
                       .rearrange("p (k n) -> p k n", k=K) for u in range(2))
        place_s = sb("place_s", [P, E])
        destf = sb("destf", [P, K])
        dest = [sb(f"dest{u}", [P, K], I32) for u in range(2)]
        row = [sb(f"row{u}", [P, ROW]) for u in range(2)]
        blocks_i = sb("blocks_i", [P, 2, E], I32)
        cum_t = sb("cum_t", [E, 1])
        before_b = vbd[0][0:E].rearrange("p b n -> p (b n)")[:, 0:BW]
        of_block = sb("of_block", [1, BW])
        quarter = sb("quarter", [1, BW], I32)
        at_block = sb("at_block", [1, BW])
        steps_f = sb("steps_f", [1, BW // 4])
        packed_f = sb("packed_f", [1, BW // 4])
        packed = sb("packed", [1, BW // 4], I32)
        first = sb("first", [1, E + 1], I32)
        groups_n = sb("groups_n", [1, 1], I32)
        looped_n = sb("looped_n", [1, 1], I32)
        p_flat = [prob[u][0:IC].rearrange("p (a c) s -> p a (c s)", a=2) for u in range(2)]
        th = [p_flat[u][:, 0, :].rearrange("p (c n) -> p c n", c=SC) for u in range(2)]
        sg = [p_flat[u][:, 1, :].rearrange("p (c n) -> p c n", c=SC) for u in range(2)]
        sh = [pt[u][0:IC, 0:SC, :] for u in range(2)]
        d_flat = xtall[:].rearrange("p t c n -> p (t c n)")
        d_used = [0]

        def carve(parts, count, n):
            i = d_used[0]
            d_used[0] += count * n
            return d_flat[0:parts, i:i + count * n].rearrange("p (b n) -> p b n", b=count)

        w1 = carve(P, WS, 2 * I)
        w2 = carve(IC, WS, 2 * D)
        ur = carve(P, 4, ROW)
        uxt = carve(P, 4, P)
        uh = carve(P, 2, I)
        uht = carve(IC, 4, P)
        uy = carve(P, 4, D)
        uplace = sb("uplace", [P, K])
        uplace_s = [sb(f"uplace_s{u}", [P, 1]) for u in range(4)]
        udest = [sb(f"udest{u}", [P, 1], I32) for u in range(4)]
        y6_flat = xtall[:].rearrange("p t c n -> p (t c n)")[:, 0:4 * K * D].rearrange("p (b n) -> p b n", b=4)
        y6 = [y6_flat[:, b, :].rearrange("p (k n) -> p k n", k=K) for b in range(4)]

        psum = ctx.enter_context(nc.psum_tensor("psum", [P, 8, 512], F32))

        def bank(i, n=2):
            return psum[:, i, 0:n * P].rearrange("p (c n) -> p c n", c=n)

        ps_q, ps_k = [bank(m)[:, 0, :] for m in range(2)], [bank(m)[:, 1, :] for m in range(2)]
        ps_v = psum[:, 2, :].rearrange("p (b n) -> p b n", b=2)
        ps_s = psum[:, 3:5, :].rearrange("p a n -> p (a n)")
        ps_pt = psum[:, 5:7, :].rearrange("p a (c n) -> p (a c) n", c=4)
        ps_o = ps_r = psum[:, 7, 0:D]
        ps_ot = bank(7)
        ps_bt, ps_bm, ps_a, ps_ad = bank(0), bank(1), psum[:, 3:5, 0:P], psum[:, 5, 0:RH * S].rearrange("p (h s) -> p h s", h=RH)
        ps_z, ps_w = bank(0), psum[:, 0, D:2 * D].rearrange("p (c n) -> p c n", c=2)
        ps_co, ps_ct, ps_cr, ps_lg, ps_x2t = [psum[:, i, 0:D] for i in (1, 6)], bank(2), psum[:, 3, 0:D], psum[:, 4, 0:E], bank(5)
        ps_before, ps_total = psum[:, 7, 0:E], psum[:, 7, E:2 * E]
        ps_g, ps_u = ([psum[0:IC, i, :].rearrange("p (c n) -> p c n", c=SC) for i in b] for b in ((0, 5), (1, 6)))
        ps_sd = psum[:, 3, 0:D]
        ps_lg_t, ps_exp = psum[0:E, 4, 0:P], psum[0:E, 7, 0:BW]
        ps_ux, ps_uh, ps_uht, ps_uy = ([psum[:, 2 * i + u, :] for u in range(2)] for i in range(4))

        block = ctx.enter_context(nc.Block())

        def rows(t):
            return bass.ds(t * P, P)

        def slot(buf, t):
            names = "bcd"[:len(buf.shape) - 2]
            spaced = " ".join(names)
            return buf[:, bass.ds(t, 1)].rearrange(f"p a {spaced} -> p (a {names[0]}) {' '.join(names[1:])}")

        def load(eng, dst, src, name):
            eng.dma_start(dst, src).then_inc(sem(name), 16)

        def ld(name, k, u, n=1):
            return sem(f"{name}{u}"), 16 * n * (k + 1)

        def stored(name, k, u):
            return sem(f"{name}{u}"), 16 * (k + 1)

        def prime(eng, *names):
            for name in names:
                n = primed[0]
                primed[0] += 1
                eng.dma_start(junk[0:1, n:n + 1], a["ident"][0:1, n:n + 1]).then_inc(sem(name), 16)

        def two(stage):
            return lambda k, u: stage(2 * k + u // 2, u % 2)

        primed = [0]
        n_first, n_late = 16 * len(first_consts), 16 * (len(consts) - len(first_consts))

        def settle(eng):
            eng.sem_inc(sem("waits_passed"), 1)

        @block.sync
        def _(sp):
            for name in first_consts:
                sp.dma_start(consts[name][0][:], consts[name][1]).then_inc(sem("first_consts"), 16)
            prime(sp, "out_st0", "out_st1", "out_st2", "out_st3")
            sp.wait_ge(sem("zeroed"), 4)

            def load_twice(dst, src, t, name):
                for copy in range(2):
                    for c in range(2):
                        sp.dma_start(dst[:, c, :, copy, :], src[c * P:(c + 1) * P, bass.ds(t * P, P)]
                                     .rearrange("p (b s) -> p b s", b=2)).then_inc(sem(name), 16)

            def load_a(k, u):
                t = 2 * k + u
                sp.wait_ge(*ev("v_ready", t - 2))
                load_twice(xt[u], a["x_t"], t, f"xt_ld{u}")
                sp.wait_ge(*ev("xnb_done", t - 2))
                load(sp, xn[u][:], a["x"][rows(2 * k + u), :], f"xn_ld{u}")

            def fill(k, u):
                for i in range(2):
                    sp.dma_start(listd[bass.ds((2 * (2 * k + u) + i) * FILL * P, FILL * P), :]
                                 .rearrange("(h p) n -> p h n", p=P), zeros[:]).then_inc(sem("filled"), 16)

            tiles(sp, [(0, load_a), (0, fill)])
            sp.dma_start(listd[BLOCKS * P:(BLOCKS + FILL) * P, :].rearrange("(h p) n -> p h n", p=P), zeros[:])\
              .then_inc(sem("filled"), 16)

            def load_b(k, u):
                t = 4 * k + u
                sp.wait_ge(*ev("a_added", t - 4))
                load(sp, cbt[u][:], a["ctx_t"][:, bass.ds(t * P, P)].rearrange("(c p) n -> p c n", p=P), f"cbt_ld{u}")

            tiles(sp, [(0, load_b)], ways=4)

            def load_c(k, u):
                t = 4 * k + u
                sp.wait_ge(*ev("zw_ready", t - 4))
                load(sp, cn[u][:], a["ctx"][rows(t), :], f"cn_ld{u}")

            tiles(sp, [(0, load_c)], ways=4)

            sp.wait_ge(*ev("gu_ready", NT - 1))
            sp.wait_ge(*ev("x2t_kept", NT - 1))

            def load_weights(e, i):
                sp.dma_start(w1[:, i:i + 1, :].rearrange("p a (c n) -> p (a c) n", c=2),
                             a["w1_t"][bass.ds(e, 1)].rearrange("a (c p) n -> p (a c) n", p=P))\
                  .then_inc(sem("w_ld"), 16)
                sp.dma_start(w2[:, i:i + 1, :].rearrange("p a (c n) -> p (a c) n", c=2),
                             a["w2_t"][bass.ds(e, 1)].rearrange("a (c p) n -> p (a c) n", p=IC))\
                  .then_inc(sem("w_ld"), 16)

            for i in range(WS):
                if i:
                    sp.wait_ge(sem("w_ld"), 32 * i)
                load_weights(i, i)
            sp.wait_ge(sem("tables"), 1)
            with sp.Fori(1, E // WS) as k:
                for i in range(WS):
                    e = WS * k + i
                    done = sp.value_load(first[0:1, bass.ds(e - WS + 1, 1)], min_val=0, max_val=BLOCKS)
                    sp.wait_ge(sem("w_ld"), 32 * e)
                    settle(sp)
                    sp.wait_ge(sem("y_ready"), done + CREDIT)
                    settle(sp)
                    load_weights(e, i)

            groups = sp.value_load(groups_n[0:1, 0:1], min_val=1, max_val=BLOCKS // 4)
            for u in range(4):
                sp.wait_ge(sem(f"y_out{u}"), (groups + 1) * 16)
                settle(sp)

            def load_e(k, u):
                t = 4 * k + u
                sp.wait_ge(*ev("ln3_sum", t - 4))
                load(sp, y6[u].rearrange("p k n -> p (k n)"),
                     yd.rearrange("(t k) n -> t (k n)", k=K)[rows(t), :], f"y6_ld{u}")

            tiles(sp, [(0, load_e)], ways=4)

        @block.tensor
        def _(pe):
            credit(pe, "s_half", "qk0_ready", "qk1_ready", "v_ready", "s_ready", "pt_ready", "o_ready", "ot_ready",
                   "r_ready", "xbt_ready", "mxt_ready", "a_added", "zw_ready", "co_ready", "ct_ready",
                   "cr_ready", "x2t_ready", "lg_ready", "gu_ready", "rank_ready", "sd_ready",
                   "ux_ready", "h_ready", "ht_ready", "y_ready")
            pe.wait_ge(sem("first_consts"), n_first)
            for h in range(RH):
                m = pe.matmul(ps_ot[:, h, :], wht[:, h, :], wht[:, h, :], start=True, stop=True)
            m.then_inc(sem("m2_ready"), 1)
            pe.wait_ge(sem("m2_done"), 1)

            def project(k, u):
                t = 2 * k + u
                pe.wait_ge(*ld("xt_ld", k, u, 4))
                pe.wait_ge(*ev("qk0_evac", t - 1))
                pe.wait_ge(*ev("qk1_evac", t - 1))
                for m in range(2):
                    for ps, first_col in ((ps_q, 0), (ps_k, D)):
                        for c in range(2):
                            col = first_col + m * P
                            q = pe.matmul(ps[m], wqkv[:, c, col:col + P], xt[u][:, c, :, 0, :],
                                          start=c == 0, stop=c == 1)
                    q.then_inc(sem(f"qk{m}_ready"), 1)
                pe.wait_ge(*ev("v_evac", t - 1))
                for b in range(2):
                    for c in range(2):
                        x_b = xt[u][:, c, b, :, :].rearrange("p a s -> p (a s)")
                        q = pe.matmul(ps_v[:, b, :], x_b, wqkv[:, c, 2 * D:3 * D], start=c == 0, stop=c == 1)
                q.then_inc(sem("v_ready"), 1)

            def out_transpose(k, u):
                t = 2 * k + u
                pe.wait_ge(*ev("o_norm", t))
                for c in range(2):
                    q = pe.transpose(ps_ot[:, c, :], on[u][:, c * P:(c + 1) * P], ident[:])
                q.then_inc(sem("ot_ready"), 1)

            def prob_transpose(k, u):
                t = 2 * k + u
                pe.wait_ge(*ev("exp_done", t))
                for h in range(2):
                    pe.wait_ge(*half("pt_evac", t - 1, h))
                    for g in range(4):
                        g2 = 4 * h + g
                        q = pe.transpose(ps_pt[:, g2, :], prob[u][:, 2 * g2:2 * g2 + 2, :]
                                         .rearrange("p a s -> p (a s)"), ident[:])
                    q.then_inc(sem("pt_ready"), 1)

            def out_project(k, u):
                t = 2 * k + u
                pe.wait_ge(*ev("ot_evac", t))
                for c in range(2):
                    q = pe.matmul(ps_r, ot[u][:, c, :], wout[:, c, :], start=c == 0, stop=c == 1)
                q.then_inc(sem("r_ready"), 1)

            def scores(k, u):
                t = 2 * k + u
                pe.wait_ge(*ev("qk0_evac", t))
                pe.wait_ge(*ev("qk1_evac", t))
                pe.wait_ge(*ev("s_read", t - 1))
                score_half(t, u, 0)

            def score_half(t, u, g2):
                for m in range(2):
                    for b in range(2):
                        for g1 in range(2):
                            g, col = 2 * g2 + g1, 512 * g1 + 256 * g2 + 128 * m
                            q = pe.matmul(ps_s[b * S:(b + 1) * S, col:col + 2 * S],
                                          qt[u][32 * g:32 * g + 32, m, b * S:(b + 1) * S],
                                          kt[u][32 * g:32 * g + 32, m, :, b * S:(b + 1) * S],
                                          start=True, stop=True)
                q.then_inc(sem("s_ready" if g2 else "s_half"), 1)

            def scores_rest(k, u):
                t = 2 * k + u
                pe.wait_ge(*ev("s_half", t))
                score_half(t, u, 1)

            def attend(k, u):
                t = 2 * k + u
                pe.wait_ge(*ev("pt_evac", t))
                pe.wait_ge(*ev("v_evac", t))
                pe.wait_ge(*ev("ln1_sum", t - 1))
                for g in range(8):
                    for b in range(2):
                        q = pe.matmul(ps_o[b * S:(b + 1) * S, 32 * g:32 * g + 32],
                                      pt[u][:, g, b * S:(b + 1) * S], vbd[u][:, b, 32 * g:32 * g + 32],
                                      start=True, stop=True)
                q.then_inc(sem("o_ready"), 1)

            tiles(pe, [(0, project), (2, out_transpose), (1, prob_transpose), (0, scores), (2, out_project),
                       (0, scores_rest), (1, attend)])

            pe.wait_ge(sem("late_consts"), n_late)
            pe.wait_ge(*ev("ln1_sum", NT - 1))

            def b_transpose(k, u):
                t = 2 * k + u
                pe.wait_ge(*ev("xb_done", t))
                pe.wait_ge(*ev("xbt_evac", t - 1))
                for c in range(2):
                    q = pe.transpose(ps_bt[:, c, :], xb[u][:, c * P:(c + 1) * P], ident[:])
                q.then_inc(sem("xbt_ready"), 1)

            def b_mix(k, u):
                t = 2 * k + u
                pe.wait_ge(*ev("xbt_evac", t))
                pe.wait_ge(*ev("mxt_evac", t - 1))
                for h in range(RH):
                    q = pe.matmul(ps_bm[:, h, :], m2[:, h, :], slot(xtall, t)[:, h, :], start=True, stop=True)
                q.then_inc(sem("mxt_ready"), 1)

            def b_scores(k, u):
                t = 4 * k + u
                pe.wait_ge(*ev("mxt_evac", t))
                pe.wait_ge(*ld("cbt_ld", k, u))
                for h in range(RH):
                    q = pe.matmul(ps_a[:, h, :], cbt[u][:, h, :], mxt[u % 2][:, h, :], start=False, stop=False)
                q.then_inc(sem("a_added"), 1)

            def b_add_zero(start):
                for h in range(RH):
                    q = pe.matmul(ps_a[:, h, :], zeros[:, 0, 0:P], zeros[:, 0, 0:P], start=start, stop=not start)
                return q

            pe.wait_ge(sem("zeroed"), 4)
            b_add_zero(True)
            tiles(pe, [(0, two(b_transpose)), (1, two(b_mix)), (2, b_scores)], ways=4)
            b_add_zero(False).then_inc(sem("a_summed"), 1)
            pe.wait_ge(sem("adiag_done"), 2)
            for h in range(RH):
                q = pe.matmul(ps_ad[:, h, :], pair[:], adiag[:, h, :], start=True, stop=True)
            q.then_inc(sem("ad_ready"), 1)

            pe.wait_ge(sem("abd_done"), 2)

            def c_z_gate(k, u):
                t = 4 * k + u
                pe.wait_ge(*ld("cn_ld", k, u))
                pe.wait_ge(*ev("z_evac", t - 1))
                pe.wait_ge(*ev("w_evac", t - 1))
                for h in range(RH):
                    q = pe.matmul(ps_z[:, h, :], cn[u][:, h * P:(h + 1) * P], abd[:, h, :], start=True, stop=True)
                for m in range(2):
                    for c in range(2):
                        q = pe.matmul(ps_w[:, m, :], wg[:, c, m * P:(m + 1) * P], slot(xtall, t)[:, c, :],
                                      start=c == 0, stop=c == 1)
                q.then_inc(sem("zw_ready"), 1)

            def c_out(k, u):
                t = 2 * k + u
                pe.wait_ge(*ev("z_evac", t))
                pe.wait_ge(*ev("gn_done", t - 2))
                for h in range(RH):
                    q = pe.matmul(ps_co[u][:, h * P:(h + 1) * P], zt[u][:, h, :], wh[:, h, :], start=True, stop=True)
                q.then_inc(sem("co_ready"), 1)

            def c_transpose(k, u):
                t = 2 * k + u
                pe.wait_ge(*ev("gn_done", t))
                pe.wait_ge(*ev("yt_done", t - 1))
                for c in range(2):
                    q = pe.transpose(ps_ct[:, c, :], ln["gn", u][5][:, c * P:(c + 1) * P], ident[:])
                q.then_inc(sem("ct_ready"), 1)

            def c_project(k, u):
                t = 2 * k + u
                pe.wait_ge(*ev("gt_done", t))
                pe.wait_ge(*ev("ln2_sum", t - 1))
                for c in range(2):
                    q = pe.matmul(ps_cr, gt[u][:, c, :], wo[:, c, :], start=c == 0, stop=c == 1)
                q.then_inc(sem("cr_ready"), 1)

            def x2_transpose(k, u):
                t = 2 * k + u
                pe.wait_ge(*ev("ln2_done", t))
                pe.wait_ge(*ev("x2t_evac", t - 1))
                for c in range(2):
                    q = pe.transpose(ps_x2t[:, c, :], ln["ln2", u][5][:, c * P:(c + 1) * P], ident[:])
                q.then_inc(sem("x2t_ready"), 1)

            def router(k, u):
                t = 2 * k + u
                pe.wait_ge(*ev("x2t_evac", t))
                pe.wait_ge(*ev("lg_evac", t - 1))
                for c in range(2):
                    q = pe.matmul(ps_lg, x2t[u][:, c, :], wgate[:, c, :], start=c == 0, stop=c == 1)
                q.then_inc(sem("lg_ready"), 1)

            def ranks(k, u):
                t = 2 * k + u
                pe.wait_ge(*ev("hot_done", t))
                pe.wait_ge(*ev("rank_read", t - 1))
                for ps, w in ((ps_before, tri), (ps_total, ones)):
                    for j in range(K):
                        q = pe.matmul(ps, w[:], hot[u][:, j, :], start=j == 0, stop=j == K - 1)
                q.then_inc(sem("rank_ready"), 1)

            tiles(pe, [(9, two(ranks)), (8, two(router)), (7, two(x2_transpose)), (0, c_z_gate), (1, two(c_out)),
                       (3, two(c_transpose)), (4, two(c_project))], ways=4)

            pe.wait_ge(*ev("x2t_kept", NT - 1))

            def shared_up(k, u):
                t = 2 * k + u
                pe.wait_ge(*ev("sh_done", t - 2))
                for g, ps in enumerate((ps_g[u], ps_u[u])):
                    for m in range(SC):
                        for c in range(2):
                            col = g * SH + m * IC
                            q = pe.matmul(ps[:, m, :], sgu[:, c, col:col + IC], slot(xtall, t)[:, c, :],
                                          start=c == 0, stop=c == 1)
                q.then_inc(sem("gu_ready"), 1)

            def shared_down(k, u):
                t = 2 * k + u
                pe.wait_ge(*ev("sh_done", t))
                pe.wait_ge(*ev("xsh_done", t - 1))
                for m in range(SC):
                    q = pe.matmul(ps_sd, sh[u][:, m, :], sdn[:, m, :], start=m == 0, stop=m == SC - 1)
                q.then_inc(sem("sd_ready"), 1)

            tiles(pe, [(0, shared_up), (1, shared_down)])

            pe.wait_ge(sem("cum_done"), 1)
            pe.transpose(ps_lg_t, scan[:, 1, :], ident[:]).then_inc(sem("cum_t_ready"), 1)
            pe.wait_ge(sem("before_b_done"), 1)
            pe.matmul(ps_exp, scan[0:E, 2, :], before_b, start=True, stop=True).then_inc(sem("experts_ready"), 1)
            pe.wait_ge(sem("tables"), 1)

            def b_x_t(k, u):
                n = 4 * k + u
                pe.wait_ge(sem(f"ur_ld{u}"), 16 * (k + 1))
                pe.wait_ge(*ev("ux_evac", n - 2))
                for c in range(2):
                    q = pe.transpose(ps_ux[u % 2][:, c * P:(c + 1) * P], ur[:, u, c * P:(c + 1) * P], ident[:])
                q.then_inc(sem("ux_ready"), 1)

            def b_up(k, u, group):
                n = 4 * k + u
                e = expert_of(group, u)
                at = e & (WS - 1)
                pe.wait_ge(sem("w_ld"), 32 * e + 32)
                pe.wait_ge(*ev("ux_evac", n))
                pe.wait_ge(*ev("silu_done", n - 2))
                for c in range(2):
                    q = pe.matmul(ps_uh[u % 2][:, 0:I], uxt[:, 2 * (u % 2) + c, :],
                                  w1[:, bass.ds(at, 1), c * I:(c + 1) * I].rearrange("p a n -> p (a n)"),
                                  start=c == 0, stop=c == 1)
                q.then_inc(sem("h_ready"), 1)

            def b_h_t(k, u):
                n = 4 * k + u
                pe.wait_ge(*ev("silu_done", n))
                pe.wait_ge(*ev("ht_evac", n - 2))
                for m in range(2):
                    q = pe.transpose(ps_uht[u % 2][0:IC, m * P:(m + 1) * P], uh[:, u % 2, m * IC:(m + 1) * IC], ident[:])
                q.then_inc(sem("ht_ready"), 1)

            def b_down(k, u, group):
                n = 4 * k + u
                at = place_before(group, u)
                pe.wait_ge(*ev("ht_evac", n))
                pe.wait_ge(*ev("y_evac", n - 2))
                for m in range(2):
                    q = pe.matmul(ps_uy[u % 2][:, 0:D], uht[:, 2 * (u % 2) + m, :],
                                  w2[:, bass.ds(at, 1), m * D:(m + 1) * D].rearrange("p a n -> p (a n)"),
                                  start=m == 0, stop=m == 1)
                q.then_inc(sem("y_ready"), 1)

            blocks(pe, [(8, b_down), (6, b_h_t), (3, b_x_t), (4, b_up)], (b_up, b_down))

        @block.scalar
        def _(act):
            act.preload_act_table(ACT.Exp)
            credit(act, "ln1_done", "gn_done", "ln2_done", "ln3_done", "qk0_evac", "exp_done", "pt_evac", "ot_evac",
                   "xbt_evac", "z_evac", "w_evac", "yt_done", "x2t_evac", "x2_kept", "lg_evac", "wexp_done", "th_done", "row_x_done",
                   "silu_done", "y_evac")
            act.wait_ge(sem("first_consts"), n_first)
            for name, (t_, src) in consts.items():
                if name not in first_consts:
                    act.dma_start(t_[:], src).then_inc(sem("late_consts"), 16)
            act.activation(bqs[:], bqk[:, 0:2], ACT.Copy, scale=float(HD) ** -0.5).then_inc(sem("bqs_done"), 1)
            act.wait_ge(sem("bqs_done"), 1)
            act.wait_ge(sem("bkp_done"), 1)
            act.wait_ge(sem("m2_ready"), 1)
            act.activation(m2[:], ps_ot, ACT.Copy).then_inc(sem("m2_done"), 1)

            def norm_apply(name, t, u, src, dst=None):
                act.wait_ge(*ev(name + "_rstd", t))
                _, _, _, _, rs, y = ln[name, u]
                act.activation(y[:] if dst is None else dst, src, ACT.Identity, bias=shift[name, u][1][:],
                               scale=rs[:]).then_inc(sem(name + "_done"), 1)

            def apply1(k, u):
                norm_apply("ln1", 2 * k + u, u, ln["ln1", u][0][:], slot(xall, 2 * k + u))

            def q_evac(k, u):
                t = 2 * k + u
                act.wait_ge(*ev("qk0_ready", t))
                act.wait_ge(*ev("s_ready", t - 2))
                act.activation(qt[u][:, 0, :], ps_q[0], ACT.Identity, bias=bqs[:, 0:1], scale=float(HD) ** -0.5)
                for par in range(2):
                    q = act.activation(kt[u][:, 0, par, :], ps_k[0], ACT.Identity, bias=bkp[:, par:par + 1],
                                       scale=kpar[:, par:par + 1])
                q.then_inc(sem("qk0_evac"), 1)

            def exps(k, u):
                t = 2 * k + u
                act.wait_ge(*ev("centred", t))
                act.activation(prob[u][:], prob[u][:], ACT.Exp).then_inc(sem("exp_done"), 1)

            def pt_evac(k, u):
                t = 2 * k + u
                act.wait_ge(*ev("o_ready", t - 2))
                for h in range(2):
                    act.wait_ge(*half("pt_ready", t, h))
                    act.activation(pt[u][:, 4 * h:4 * h + 4, :], ps_pt[:, 4 * h:4 * h + 4, :],
                                   ACT.Copy).then_inc(sem("pt_evac"), 1)

            def ot_evac(k, u):
                t = 2 * k + u
                act.wait_ge(*ev("ot_ready", t))
                act.wait_ge(*ev("r_ready", t - 2))
                for c in range(2):
                    q = act.activation(ot[u][:, c, :], ps_ot[:, c, :], ACT.Identity, bias=bv[:, c:c + 1])
                q.then_inc(sem("ot_evac"), 1)

            tiles(act, [(1, exps), (0, q_evac), (2, ot_evac), (1, pt_evac), (3, apply1)])

            act.wait_ge(sem("late_consts"), n_late)

            def xbt_evac(k, u):
                t = 2 * k + u
                act.wait_ge(*ev("xbt_ready", t))
                act.activation(slot(xtall, t), ps_bt, ACT.Copy).then_inc(sem("xbt_evac"), 1)

            tiles(act, [(0, xbt_evac)])

            def z_evac(k, u):
                t = 2 * k + u
                act.wait_ge(*ev("zw_ready", t))
                act.wait_ge(*ev("co_ready", t - 2))
                act.activation(zt[u][:], ps_z, ACT.Copy).then_inc(sem("z_evac"), 1)

            def w_evac(k, u):
                t = 4 * k + u
                act.wait_ge(*ev("zw_ready", t))
                act.wait_ge(*ev("gt_done", t - 4))
                act.activation(wt[u][:, :, :], ps_w, ACT.Relu).then_inc(sem("w_evac"), 1)

            def group_apply(k, u):
                t = 2 * k + u
                act.wait_ge(*ev("ct_ready", t - 2))
                norm_apply("gn", t, u, ps_co[u])

            def apply2(k, u):
                t = 2 * k + u
                act.wait_ge(*ev("x2_kept", t - 2))
                act.wait_ge(*ev("x2t_ready", t - 2))
                norm_apply("ln2", t, u, ln["ln2", u][0][:])

            def scale_shift(k, u):
                t = 2 * k + u
                act.wait_ge(*ev("ct_ready", t))
                act.wait_ge(*ev("gt_done", t - 2))
                for c in range(2):
                    q = act.activation(yt[u][:, c, :], ps_ct[:, c, :], ACT.Identity, bias=beta[:, c:c + 1],
                                       scale=gamma[:, c:c + 1])
                q.then_inc(sem("yt_done"), 1)

            def x2t_evac(k, u):
                t = 2 * k + u
                act.wait_ge(*ev("x2t_ready", t))
                act.wait_ge(*ev("lg_ready", t - 2))
                act.wait_ge(*ev("x2t_kept", t - 2))
                act.activation(x2t[u][:], ps_x2t, ACT.Copy).then_inc(sem("x2t_evac"), 1)

            def lg_evac(k, u):
                t = 2 * k + u
                act.wait_ge(*ev("lg_ready", t))
                act.wait_ge(*ev("topi_done", t - 2))
                act.activation(lg[u][:], ps_lg, ACT.Copy).then_inc(sem("lg_evac"), 1)

            def keep_x2(k, u):
                t = 2 * k + u
                act.wait_ge(*ev("ln2_done", t))
                act.activation(slot(xall, t), ln["ln2", u][5][:], ACT.Copy).then_inc(sem("x2_kept"), 1)

            def w_exp(k, u):
                t = 2 * k + u
                act.wait_ge(*ev("ntop_done", t))
                act.wait_ge(*ev("weights_done", t - 2))
                act.activation(wexp[u][:], top[u][:, 0:K], ACT.Exp, bias=ntop[u][:],
                               accum_out=wsum[u][:]).then_inc(sem("wexp_done"), 1)

            tiles(act, [(9, two(w_exp)), (8, two(lg_evac)), (7, two(x2t_evac)), (6, two(apply2)), (0, two(z_evac)),
                        (0, w_evac), (2, two(group_apply)), (6, two(keep_x2)), (3, two(scale_shift))], ways=4)

            def row_x(k, u):
                t = 2 * k + u
                act.wait_ge(*ev("x2_kept", t))
                act.wait_ge(*ev("scattered", t - 2))
                act.activation(row[u][:, 0:D], slot(xall, t), ACT.Copy).then_inc(sem("row_x_done"), 1)

            def th_g(k, u):
                t = 2 * k + u
                act.wait_ge(*ev("gu_ready", t))
                act.wait_ge(*ev("sg_done", t - 2))
                act.activation(th[u], ps_g[u], ACT.Tanh, scale=0.5).then_inc(sem("th_done"), 1)

            tiles(act, [(0, row_x), (0, th_g)])

            act.preload_act_table(ACT.Silu)
            act.wait_ge(sem("tables"), 1)

            act.wait_ge(*ev("scattered", NT - 1))
            act.wait_ge(*ev("sh_done", NT - 1))
            act.wait_ge(*ev("x2t_kept", NT - 1))

            def load_rows(k, u):
                n = 4 * k + u
                act.wait_ge(*ev("ux_ready", n - 4))
                act.wait_ge(*ev("uplace_done", n - 4))
                settle(act)
                act.dma_start(ur[:, u, :], listd[bass.ds(n * P, P), :]).then_inc(sem(f"ur_ld{u}"), 16)

            def silu(k, u):
                n = 4 * k + u
                act.wait_ge(*ev("h_ready", n))
                act.wait_ge(*ev("ht_ready", n - 2))
                act.activation(uh[:, u % 2, :], ps_uh[u % 2][:, 0:I], ACT.Silu).then_inc(sem("silu_done"), 1)

            def y_evac(k, u):
                n = 4 * k + u
                act.wait_ge(*ev("y_ready", n))
                act.wait_ge(sem(f"y_out{u}"), 16 * (k + 1))
                act.activation(uy[:, u, :], ps_uy[u % 2][:, 0:D], ACT.Copy).then_inc(sem("y_evac"), 1)

            blocks(act, [(8, y_evac), (4, silu), (0, load_rows)])

            def apply3(k, u):
                act.wait_ge(*stored("out_st", k, u))
                norm_apply("ln3", 4 * k + u, u, ln["ln3", u][0][:])

            def store_e(k, u):
                t = 4 * k + u
                act.wait_ge(*ev("ln3_done", t))
                act.dma_start(out[rows(t), :], ln["ln3", u][5][:]).then_inc(sem(f"out_st{u}"), 16)

            tiles(act, [(0, apply3), (0, store_e)], ways=4)
            for u in range(4):
                act.wait_ge(sem(f"out_st{u}"), 16 * (NT // 4 + 1))

        @block.gpsimd
        def _(pool):
            pool.memset(eps[:, 0:1], LN_EPS).then_inc(sem("pool_const"), 1)
            pool.memset(eps[:, 1:2], GN_EPS).then_inc(sem("pool_const"), 1)
            pool.memset(mhalf[:], -0.5).then_inc(sem("pool_const"), 1)
            pool.memset(minus[:], -1.0).then_inc(sem("pool_const"), 1)
            for h in range(4):
                pool.dma_start(junk[0:1, 12 + h:13 + h], a["ident"][0:1, h:h + 1]).then_inc(sem(f"y_out{h}"), 16)
            pool.wait_ge(sem("pool_const"), 4)
            credit(pool, "xnb_done", "rsum_done", "ln1_rstd", "gn_rstd", "ln2_rstd", "ln3_rstd", "scattered",
                   "ln1_var", "gn_var", "ln2_var", "ln3_var", "x2t_kept",
                   "ln1_pow", "gn_pow", "ln2_pow", "ln3_pow")
            pool.wait_ge(sem("first_consts"), n_first)

            def rstd(name, col, ways=2):
                def stage(k, u):
                    t = ways * k + u
                    _, _, mv, ve, rs, _ = ln[name, u]
                    pool.wait_ge(*ev(name + "_mv", t))
                    pool.tensor_tensor(ve[:], mv[:, 1:2], eps[:, col:col + 1], ALU.add).then_inc(sem(name + "_var"), 1)
                    pool.wait_ge(*ev(name + "_var", t))
                    pool.wait_ge(*ev(name + "_done", t - ways))
                    pool.tensor_tensor(rs[:], ve[:], mhalf[:], ALU.pow)
                    nm, sh_ = shift[name, u]
                    pool.tensor_tensor(nm[:], mv[:, 0:1], minus[:], ALU.mult).then_inc(sem(name + "_pow"), 1)
                    pool.wait_ge(*ev(name + "_pow", t))
                    pool.tensor_tensor(sh_[:], nm[:], rs[:], ALU.mult).then_inc(sem(name + "_rstd"), 1)
                return stage

            def add_bias(k, u):
                t = 2 * k + u
                pool.wait_ge(*ld("xn_ld", k, u))
                pool.wait_ge(*ev("ln1_sum", t - 2))
                pool.tensor_tensor(xnb[u][:], xn[u][:], bout[:], ALU.add).then_inc(sem("xnb_done"), 1)

            tiles(pool, [(0, add_bias), (2, rstd("ln1", 0))])

            def keep_x2t(k, u):
                t = 2 * k + u
                pool.wait_ge(*ev("x2t_evac", t))
                pool.tensor_copy(slot(xtall, t), x2t[u][:]).then_inc(sem("x2t_kept"), 1)

            tiles(pool, [(5, rstd("ln2", 0)), (7, keep_x2t), (1, rstd("gn", 1))])

            pool.wait_ge(sem("filled"), 16 * (2 * NT + 1))

            def scatter(k, u):
                t = 2 * k + u
                pool.wait_ge(*ev("row_x_done", t))
                pool.wait_ge(*ev("dest_done", t))
                settle(pool)
                for j in range(K):
                    pool.indirect_dma_start(listd, bass.IndirectOffsetOnAxis(ap=dest[u][:, j:j + 1], axis=0),
                                            row[u][:], None).then_inc(sem(f"scatter{u}"), 16)

            def scatter_end(k, u):
                pool.wait_ge(sem(f"scatter{u}"), 16 * K * (k + 1))
                pool.sem_inc(sem("scattered"), 1)

            tiles(pool, [(0, scatter), (1, scatter_end)])

            pool.wait_ge(sem("tables"), 1)

            def scatter_result(k, u):
                n = 4 * k + u
                pool.wait_ge(*ev("udest_done", n))
                pool.wait_ge(*ev("y_evac", n))
                settle(pool)
                pool.indirect_dma_start(yd, bass.IndirectOffsetOnAxis(ap=udest[u][:, 0:1], axis=0), uy[:, u, :], None,
                                        bounds_check=T * K - 1, oob_is_err=False).then_inc(sem(f"y_out{u}"), 16)

            blocks(pool, [(8, scatter_result)])

            tiles(pool, [(0, rstd("ln3", 0, 4))], ways=4)

        @block.vector
        def _(dve):
            dve.memset(zeros[:], 0.0).then_inc(sem("zeroed"), 1)
            dve.memset(abd[:], 0.0).then_inc(sem("zeroed"), 1)
            dve.memset(ones[:], 1.0).then_inc(sem("zeroed"), 1)
            credit(dve, "qk1_evac", "v_evac", "s_read", "max_done", "centred", "rinv_done", "o_norm", "ln1_sum",
                   "ln1_stat", "ln1_mv", "mxt_evac", "gn_stat", "gn_mv", "gt_done",
                   "ln2_sum", "ln2_stat", "ln2_mv", "top_done", "topi_done", "tope_done",
                   "ntop_done", "hot_done", "winv_done", "weights_done", "rank_read", "hot_s_done", "pick_done",
                   "destf_done", "dest_done", "sg_done", "sh_done", "xsh_done", "xb_done", "ux_evac", "ht_evac",
                   "udest_done", "uplace_done", "uplaces_done", "ln3_sum", "ln3_stat", "ln3_mv")
            dve.wait_ge(sem("first_consts"), n_first)
            dve.tensor_copy(tri[:], tri_f[:]).then_inc(sem("zeroed"), 1)
            for h in range(H):
                q = dve.scalar_tensor_tensor(bias[:, h, :], rel[:], slopes[:, h:h + 1], causal[:], ALU.mult, ALU.add)
            q.then_inc(sem("bias_done"), 1)
            dve.tensor_scalar(bkp[:], kpar[:], bqk[:, 2:3], None, ALU.mult).then_inc(sem("bkp_done"), 1)
            dve.wait_ge(sem("bqs_done"), 1)
            dve.memset(count[:], 0.0).then_inc(sem("bias_done"), 1)
            dve.wait_ge(sem("bias_done"), 2)
            dve.wait_ge(sem("zeroed"), 4)

            def norm_stats(name, t, u, src, ways=2):
                norm_sums(name, t, u, src)
                norm_mean(name, t, u, ways)

            def norm_sums(name, t, u, src):
                dve.bn_stats(ln[name, u][1][:], src).then_inc(sem(name + "_stat"), 1)

            def norm_mean(name, t, u, ways=2):
                _, st, mv, _, _, _ = ln[name, u]
                dve.wait_ge(*ev(name + "_stat", t))
                dve.wait_ge(*ev(name + "_done", t - ways))
                settle(dve)
                dve.bn_aggr(mv[:], st[:]).then_inc(sem(name + "_mv"), 1)

            def o_norm(k, u):
                t = 2 * k + u
                dve.wait_ge(*ev("rsum_done", t))
                dve.reciprocal(rinv[u][:], rsum[u][:]).then_inc(sem("rinv_done"), 1)
                dve.wait_ge(*ev("rinv_done", t))
                dve.wait_ge(*ev("o_ready", t))
                dve.wait_ge(*ev("ot_ready", t - 2))
                dve.tensor_tensor(on[u][:].rearrange("p (h d) -> p h d", h=H),
                                  ps_o.rearrange("p (h d) -> p h d", h=H),
                                  rinv[u][:].unsqueeze(2).to_broadcast([P, H, HD]), ALU.mult)\
                   .then_inc(sem("o_norm"), 1)

            def kv_evac(k, u):
                t = 2 * k + u
                dve.wait_ge(*ev("qk1_ready", t))
                dve.wait_ge(*ev("s_ready", t - 2))
                dve.tensor_scalar(qt[u][:, 1, :], ps_q[1], float(HD) ** -0.5, bqs[:, 1:2], ALU.mult, ALU.add)
                for par in range(2):
                    q = dve.tensor_scalar(kt[u][:, 1, par, :], ps_k[1], bqk[:, 3:4], kpar[:, par:par + 1],
                                          ALU.add, ALU.mult)
                q.then_inc(sem("qk1_evac"), 1)
                dve.wait_ge(*ev("v_ready", t))
                dve.wait_ge(*ev("o_ready", t - 2))
                dve.tensor_tensor(vbd[u][:], ps_v, vpar[:].unsqueeze(1).to_broadcast([P, 2, D]), ALU.mult)\
                   .then_inc(sem("v_evac"), 1)

            def residual1(k, u):
                t = 2 * k + u
                r = ln["ln1", u][0]
                dve.wait_ge(*ev("r_ready", t))
                dve.wait_ge(*ev("xnb_done", t))
                dve.wait_ge(*ev("ln1_done", t - 2))
                dve.tensor_tensor(r[:], ps_r, xnb[u][:], ALU.add).then_inc(sem("ln1_sum"), 1)
                dve.wait_ge(*ev("ln1_sum", t))
                norm_stats("ln1", t, u, r[:])

            def softmax(k, u):
                t = 2 * k + u
                dve.wait_ge(*ev("s_ready", t))
                dve.wait_ge(*ev("pt_ready", t - 2))
                dve.tensor_tensor(prob[u][:], ps_s.rearrange("p (h s) -> p h s", h=H), bias[:], ALU.add)\
                   .then_inc(sem("s_read"), 1)
                dve.wait_ge(*ev("s_read", t))
                dve.tensor_reduce(mx[u][:], prob[u][:], AX, ALU.max).then_inc(sem("max_done"), 1)
                dve.wait_ge(*ev("max_done", t))
                dve.tensor_tensor(prob[u][:], prob[u][:], mx[u][:].unsqueeze(2).to_broadcast([P, H, S]),
                                  ALU.subtract).then_inc(sem("centred"), 1)

            def row_sums(k, u):
                t = 2 * k + u
                dve.wait_ge(*ev("exp_done", t))
                dve.tensor_reduce(rsum[u][:], prob[u][:], AX, ALU.add).then_inc(sem("rsum_done"), 1)

            tiles(dve, [(2, o_norm), (0, kv_evac), (1, row_sums), (2, residual1), (0, softmax)])

            dve.wait_ge(sem("late_consts"), n_late)

            def copy_x1(k, u):
                t = 2 * k + u
                dve.wait_ge(*ev("ln1_done", t))
                dve.wait_ge(*ev("xbt_ready", t - 2))
                dve.tensor_copy(xb[u][:], slot(xall, t)).then_inc(sem("xb_done"), 1)

            def mxt_evac(k, u):
                t = 2 * k + u
                dve.wait_ge(*ev("mxt_ready", t))
                dve.wait_ge(*ev("a_added", t - 2))
                dve.tensor_copy(mxt[u][:], ps_bm).then_inc(sem("mxt_evac"), 1)

            tiles(dve, [(0, copy_x1), (2, mxt_evac)])
            dve.wait_ge(sem("a_summed"), 1)
            for b in range(2):
                half_ = slice(b * S, (b + 1) * S)
                dve.tensor_copy(adiag[half_, :, :], ps_a[half_, :, half_]).then_inc(sem("adiag_done"), 1)
            dve.wait_ge(sem("ad_ready"), 1)
            dve.tensor_tensor(araw[:], ps_ad, decay[:], ALU.mult).then_inc(sem("araw_done"), 1)
            dve.wait_ge(sem("araw_done"), 1)
            dve.tensor_scalar(afloor[:], araw[:], 1.0, None, ALU.max).then_inc(sem("araw_done"), 1)
            dve.wait_ge(sem("araw_done"), 2)
            for b in range(2):
                half_ = slice(b * S, (b + 1) * S)
                dve.scalar_tensor_tensor(abd[half_, :, half_], araw[half_, :, :], -1.0, afloor[half_, :, :],
                                         ALU.mult, ALU.max)\
                   .then_inc(sem("abd_done"), 1)

            def group_sums(k, u):
                t = 2 * k + u
                dve.wait_ge(*ev("co_ready", t))
                dve.wait_ge(*ev("gn_mv", t - 2))
                norm_sums("gn", t, u, ps_co[u])

            def group_mean(k, u):
                norm_mean("gn", 2 * k + u, u)

            def gated(k, u):
                t = 4 * k + u
                dve.wait_ge(*ev("yt_done", t))
                dve.wait_ge(*ev("w_evac", t))
                dve.wait_ge(*ev("cr_ready", t - 2))
                dve.tensor_tensor(gt[u % 2][:], yt[u % 2][:], wt[u][:, :, :], ALU.mult).then_inc(sem("gt_done"), 1)

            def residual2(k, u):
                t = 2 * k + u
                r = ln["ln2", u][0]
                dve.wait_ge(*ev("cr_ready", t))
                dve.wait_ge(*ev("ln2_done", t - 2))
                dve.tensor_tensor(r[:], ps_cr, slot(xall, t), ALU.add).then_inc(sem("ln2_sum"), 1)

            def sums2(k, u):
                t = 2 * k + u
                dve.wait_ge(*ev("ln2_sum", t))
                dve.wait_ge(*ev("ln2_mv", t - 2))
                norm_sums("ln2", t, u, ln["ln2", u][0][:])

            def mean2(k, u):
                norm_mean("ln2", 2 * k + u, u)

            def top6(k, u):
                t = 2 * k + u
                dve.wait_ge(*ev("lg_evac", t))
                dve.wait_ge(*ev("wexp_done", t - 2))
                settle(dve)
                dve.max(top[u][:], lg[u][:]).then_inc(sem("top_done"), 1)

            def top6_index(k, u):
                t = 2 * k + u
                dve.wait_ge(*ev("top_done", t))
                settle(dve)
                dve.max_index(topi[u][:], top[u][:], lg[u][:]).then_inc(sem("topi_done"), 1)
                dve.tensor_scalar(ntop[u][:], top[u][:, 0:1], -1.0, None, ALU.mult).then_inc(sem("ntop_done"), 1)

            def top6_float(k, u):
                t = 2 * k + u
                dve.wait_ge(*ev("topi_done", t))
                dve.tensor_copy(slot(tope, t), topi[u][:, 0:K]).then_inc(sem("tope_done"), 1)

            def one_hot(k, u):
                t = 2 * k + u
                dve.wait_ge(*ev("tope_done", t))
                dve.wait_ge(*ev("rank_ready", t - 2))
                dve.tensor_tensor(hot[u][:], iota_e[:, 0:E].unsqueeze(1).to_broadcast([P, K, E]),
                                  slot(tope, t).unsqueeze(2).to_broadcast([P, K, E]), ALU.is_equal)\
                   .then_inc(sem("hot_done"), 1)

            def weight_sum(k, u):
                t = 2 * k + u
                dve.wait_ge(*ev("wexp_done", t))
                dve.reciprocal(winv[u][:], wsum[u][:]).then_inc(sem("winv_done"), 1)

            def gate_weights(k, u):
                t = 2 * k + u
                dve.wait_ge(*ev("winv_done", t))
                dve.tensor_scalar(weights[:, bass.ds(t, 1), :].rearrange("p a k -> p (a k)"), wexp[u][:],
                                  winv[u][:, 0:1], None, ALU.mult).then_inc(sem("weights_done"), 1)

            def token_ranks(k, u):
                t = 2 * k + u
                dve.wait_ge(*ev("rank_ready", t))
                dve.wait_ge(*ev("rank_read", t - 1))
                dve.tensor_tensor(slot(rank, t), ps_before, count[:], ALU.add)
                dve.tensor_tensor(count[:], ps_total, count[:], ALU.add).then_inc(sem("rank_read"), 1)

            tiles(dve, [(5, two(residual2)), (5, two(sums2)), (8, two(top6)),
                        (9, two(token_ranks)), (5, two(mean2)), (8, two(top6_index)), (9, two(weight_sum)),
                        (8, two(top6_float)), (9, two(gate_weights)), (8, two(one_hot)),
                        (1, two(group_sums)), (3, gated), (1, two(group_mean))], ways=4)

            dve.wait_ge(*ev("rank_read", NT - 1))
            steps = [0]

            def done(q):
                steps[0] += 1
                q.then_inc(sem("tab"), 1)
                dve.wait_ge(sem("tab"), steps[0])

            done(dve.memset(scan[:, 2, :], 1.0))
            done(dve.memset(start[:, 0:1], 0.0))
            done(dve.memset(first[:, 0:1], 0))
            done(dve.tensor_scalar(blocks_i[:, 0, :], count[:], float(P - 1), None, ALU.add))
            done(dve.tensor_scalar(blocks_i[:, 1, :], blocks_i[:, 0, :], P.bit_length() - 1, None, ALU.arith_shift_right))
            done(dve.tensor_scalar(scan[:, 0, :], blocks_i[:, 1, :], 1.0, None, ALU.max))
            dve.tensor_tensor_scan(scan[:, 1, :], scan[:, 2, :], scan[:, 0, :], 0.0, ALU.mult, ALU.add)\
               .then_inc(sem("cum_done"), 1)
            dve.wait_ge(sem("cum_done"), 1)
            done(dve.tensor_scalar(start[:, 1:E], scan[:, 1, 0:E - 1], float(P), None, ALU.mult))

            def destinations(k, u):
                t = 2 * k + u
                dve.wait_ge(*ev("pick_done", t - 1))
                dve.tensor_tensor(place_s[:], slot(rank, t), start[:], ALU.add)
                dve.tensor_tensor(hot_s, iota_e[:, 0:E].unsqueeze(1).to_broadcast([P, K, E]),
                                  slot(tope, t).unsqueeze(2).to_broadcast([P, K, E]), ALU.is_equal)\
                   .then_inc(sem("hot_s_done"), 1)
                dve.wait_ge(*ev("hot_s_done", t))
                dve.wait_ge(*ev("destf_done", t - 1))
                dve.tensor_tensor(pick, hot_s, place_s[:].unsqueeze(1).to_broadcast([P, K, E]), ALU.mult)\
                   .then_inc(sem("pick_done"), 1)
                dve.wait_ge(*ev("pick_done", t))
                dve.wait_ge(*ev("dest_done", t - 1))
                dve.tensor_reduce(destf[:], pick, AX, ALU.add).then_inc(sem("destf_done"), 1)
                dve.wait_ge(*ev("destf_done", t))
                dve.wait_ge(*ev("scattered", t - 2))
                dve.tensor_copy(dest[u][:], destf[:])
                dve.tensor_copy(row[u][:, D:D + K], slot(tope, t))
                dve.tensor_copy(row[u][:, D + K:ROW], slot(places, t)).then_inc(sem("dest_done"), 1)

            def shared_gate(k, u):
                t = 2 * k + u
                dve.wait_ge(*ev("th_done", t))
                dve.wait_ge(*ev("sh_done", t - 2))
                dve.scalar_tensor_tensor(sg[u], th[u], 1.0, ps_g[u], ALU.add, ALU.mult).then_inc(sem("sg_done"), 1)
                dve.wait_ge(*ev("sg_done", t))
                dve.wait_ge(*ev("sd_ready", t - 2))
                dve.scalar_tensor_tensor(sh[u], sg[u], 0.5, ps_u[u], ALU.mult, ALU.mult).then_inc(sem("sh_done"), 1)

            def add_shared(k, u):
                t = 2 * k + u
                dve.wait_ge(*ev("sd_ready", t))
                dve.wait_ge(*ev("row_x_done", t))
                dve.tensor_tensor(slot(xall, t), ps_sd, slot(xall, t), ALU.add).then_inc(sem("xsh_done"), 1)

            tiles(dve, [(0, destinations), (0, shared_gate), (1, add_shared)])

            done(dve.tensor_copy(first[:, 1:E + 1], scan[0:1, 1, :]))
            done(dve.tensor_scalar(quarter[:, 0:1], scan[0:1, 1, E - 1:E], 3.0, None, ALU.add))
            done(dve.tensor_scalar(groups_n[:], quarter[:, 0:1], 2, None, ALU.arith_shift_right))
            done(dve.tensor_scalar(looped_n[:], groups_n[:], -2.0, None, ALU.add))
            dve.wait_ge(sem("cum_t_ready"), 1)
            done(dve.tensor_copy(cum_t[:], ps_lg_t[:, 0:1]))
            dve.tensor_scalar(before_b, iota_b[:], cum_t[:, 0:1], None, ALU.is_ge).then_inc(sem("before_b_done"), 1)
            dve.wait_ge(sem("experts_ready"), 1)
            done(dve.tensor_scalar(of_block[:], ps_exp[0:1, :], float(E - 1), None, ALU.min))
            done(dve.tensor_copy(quarter[:], of_block[:]))
            done(dve.tensor_scalar(quarter[:], quarter[:], WS.bit_length() - 1, None, ALU.arith_shift_right))
            done(dve.tensor_copy(at_block[:], quarter[:]))
            done(dve.scalar_tensor_tensor(at_block[:], at_block[:], -float(WS), of_block[:], ALU.mult, ALU.add))
            of_group, at_group = (x[:].rearrange("p (g f) -> p f g", f=4) for x in (of_block, at_block))
            done(dve.memset(packed_f[:], 0.0))
            done(dve.tensor_copy(packed_f[:, 1:], at_group[:, 3, :-1]))
            for f in (2, 1, 0):
                done(dve.scalar_tensor_tensor(packed_f[:, 1:], packed_f[:, 1:], float(WS), at_group[:, f, :-1],
                                              ALU.mult, ALU.add))
            for f in (3, 2, 1):
                done(dve.tensor_tensor(steps_f[:], of_group[:, f, :], of_group[:, 0, :], ALU.subtract))
                done(dve.scalar_tensor_tensor(packed_f[:], packed_f[:], 4.0, steps_f[:], ALU.mult, ALU.add))
            done(dve.scalar_tensor_tensor(packed_f[:], packed_f[:], float(E), of_group[:, 0, :], ALU.mult, ALU.add))
            done(dve.tensor_copy(packed[:], packed_f[:]))
            dve.sem_inc(sem("tables"), 1)
            dve.wait_ge(*ev("x2t_kept", NT - 1))

            def place_mul(k, u, group):
                n = 4 * k + u
                e = expert_of(group, u)
                dve.wait_ge(sem(f"ur_ld{u}"), 16 * (k + 1))
                dve.wait_ge(*ev("uplaces_done", n - 1))
                dve.scalar_tensor_tensor(uplace[:], ur[:, u, D:D + K], iota_e[:, bass.ds(e, 1)],
                                         ur[:, u, D + K:ROW], ALU.is_equal, ALU.mult).then_inc(sem("uplace_done"), 1)

            def place_sum(k, u):
                n = 4 * k + u
                dve.wait_ge(*ev("uplace_done", n))
                dve.wait_ge(*ev("udest_done", n - 4))
                dve.tensor_reduce(uplace_s[u][:], uplace[:], AX, ALU.add).then_inc(sem("uplaces_done"), 1)

            def place_int(k, u):
                n = 4 * k + u
                dve.wait_ge(*ev("uplaces_done", n))
                dve.wait_ge(sem(f"y_out{u}"), 16 * (k + 1))
                dve.tensor_scalar(udest[u][:], uplace_s[u][:], float(NOWHERE), None, ALU.add)\
                   .then_inc(sem("udest_done"), 1)

            def ux_evac(k, u):
                n = 4 * k + u
                dve.wait_ge(*ev("ux_ready", n))
                dve.wait_ge(*ev("h_ready", n - 2))
                dve.tensor_copy(uxt[:, 2 * (u % 2):2 * (u % 2) + 2, :],
                                ps_ux[u % 2][:, 0:D].rearrange("p (c n) -> p c n", c=2)).then_inc(sem("ux_evac"), 1)

            def ht_evac(k, u):
                n = 4 * k + u
                dve.wait_ge(*ev("ht_ready", n))
                dve.wait_ge(*ev("y_ready", n - 2))
                dve.tensor_copy(uht[:, 2 * (u % 2):2 * (u % 2) + 2, :],
                                ps_uht[u % 2][0:IC, 0:D].rearrange("p (c n) -> p c n", c=2)).then_inc(sem("ht_evac"), 1)

            blocks(dve, [(6, ht_evac), (4, place_mul), (3, ux_evac), (4, place_sum), (7, place_int)], (place_mul,))

            def add_slot(j):
                def stage(k, u):
                    t = 4 * k + u
                    r = ln["ln3", u][0]
                    if j == 0:
                        dve.wait_ge(*ld("y6_ld", k, u))
                        dve.wait_ge(*ev("ln3_done", t - 4))
                    else:
                        dve.wait_ge(sem(f"e_chain{u % 2}"), (K - 1) * (2 * k + u // 2) + j)
                    dve.scalar_tensor_tensor(r[:], y6[u][:, j, :], weights[:, bass.ds(t, 1), j:j + 1]
                                             .rearrange("p a k -> p (a k)"), r[:] if j else slot(xall, t),
                                             ALU.mult, ALU.add)\
                       .then_inc(sem(f"e_chain{u % 2}" if j < K - 1 else "ln3_sum"), 1)
                return stage

            def sums3(k, u):
                dve.wait_ge(*ev("ln3_sum", 4 * k + u))
                norm_sums("ln3", 4 * k + u, u, ln["ln3", u][0][:])

            def mean3(k, u):
                norm_mean("ln3", 4 * k + u, u, 4)

            tiles(dve, [(2, sums3), (0, add_slot(0)), (1, add_slot(3)), (2, mean3), (0, add_slot(1)), (1, add_slot(4)),
                        (0, add_slot(2)), (1, add_slot(5))], ways=4)


def _shape_constants():
    p = np.arange(P)
    q, k = p[:, None] % S, np.arange(S)[None, :]
    seen = k <= q
    gam = (np.float32(1) - np.float32(2) ** (-5 - np.arange(RH, dtype=np.float32))).astype(np.float32)
    expo = (k - np.arange(S)[:, None]).astype(np.float32)
    dec = np.where(expo[None] <= 0, gam[:, None, None] ** expo[None], 0).astype(np.float32)
    dec = dec / np.sqrt(dec.sum(-1))[:, None, :] / np.sqrt(np.float32(D // RH))
    dec_t = np.tile(dec.transpose(2, 0, 1), (2, 1, 1))
    tok = np.arange(NT)[None, :, None] * P + p[:, None, None]
    return {
        "ident": np.eye(P),
        "k_parity": np.stack([(p // HD) % 2 == 0, (p // HD) % 2 == 1], 1),
        "v_parity": (np.arange(D)[None, :] // HD) % 2 == (p // S)[:, None],
        "rel": np.where(seen, k - q, 0),
        "causal": np.where(seen, 0.0, -1e9),
        "decay_t": dec_t,
        "pair": p[:, None] % S == p[None, :] % S,
        "tri": p[:, None] < p[None, :],
        "iota_b": np.broadcast_to(np.arange(BW), (E, BW)),
        "iota_e": np.broadcast_to(np.arange(E + 4), (P, E + 4)),
        "places": tok * K + np.arange(K) - NOWHERE,
    }


def kernel(x, ctx_2048, L0_attn_qkv_w, L0_attn_qkv_b, L0_attn_out_w, L0_attn_out_b, L0_attn_alibi_slopes,
           L0_xattn_Wh, L0_xattn_wg_w, L0_xattn_wo_w, L0_xattn_gn_gamma, L0_xattn_gn_beta, L0_ffn_gate_w,
           L0_ffn_experts_w1, L0_ffn_experts_w2, L0_ffn_shared_gate_up, L0_ffn_shared_down):
    import concourse.bacc as bacc
    from concourse.bass_utils import run_bass_kernel_spmd

    rows = np.asarray(x).reshape(T, D)
    ctx = np.asarray(ctx_2048).reshape(T, D)
    qkv_b = np.asarray(L0_attn_qkv_b)
    dims = (np.array(ORDER)[:, None] * HD + np.arange(HD)).reshape(-1)
    qkv_rows = np.concatenate([np.arange(2 * D), 2 * D + dims])
    arrays = {
        "x": rows, "x_t": rows.T, "ctx": ctx, "ctx_t": ctx.T,
        "wqkv_t": np.asarray(L0_attn_qkv_w)[qkv_rows].T,
        "b_qk": qkv_b[:2 * D].reshape(4, P).T, "b_v": qkv_b[2 * D + dims].reshape(2, P).T,
        "slopes": np.broadcast_to(np.asarray(L0_attn_alibi_slopes)[np.array(ORDER)], (P, H)),
        "wout_t": np.asarray(L0_attn_out_w).T[dims],
        "b_out": np.broadcast_to(np.asarray(L0_attn_out_b), (P, D)),
        "wh": np.asarray(L0_xattn_Wh), "wh_t": np.asarray(L0_xattn_Wh).transpose(0, 2, 1),
        "wg": np.asarray(L0_xattn_wg_w), "wo": np.asarray(L0_xattn_wo_w),
        "gamma": np.asarray(L0_xattn_gn_gamma).reshape(2, P).T,
        "beta": np.asarray(L0_xattn_gn_beta).reshape(2, P).T,
        "gate_t": np.asarray(L0_ffn_gate_w).T,
        "w1_t": np.asarray(L0_ffn_experts_w1).transpose(0, 2, 1),
        "w2_t": np.asarray(L0_ffn_experts_w2).transpose(0, 2, 1),
        "sgu_t": np.asarray(L0_ffn_shared_gate_up).T,
        "sdn_t": np.asarray(L0_ffn_shared_down).T,
    }
    arrays = {n: np.ascontiguousarray(v) for n, v in arrays.items()}
    arrays.update({n: np.ascontiguousarray(v, dtype=np.float32) for n, v in _shape_constants().items()})
    nc = bacc.Bacc("TRN2", target_bir_lowering=False, num_devices=1)
    aps = {n: nc.dram_tensor("in_" + n, v.shape, F32, kind="ExternalInput").ap() for n, v in arrays.items()}
    out = nc.dram_tensor("out_rows", (T, D), F32, kind="ExternalOutput").ap()
    decoder_layer(nc, aps, out)
    r = run_bass_kernel_spmd(nc, [{"in_" + n: v for n, v in arrays.items()}], core_ids=[0])
    return r.results[0]["out_rows"].reshape(B, S, D)
```
